# Optimizing a Trainium2 kernel written in Bass

```python
import numpy as np
import jax
import jax.numpy as jnp

def _softmax(x, axis=-1):
    return jax.nn.softmax(x, axis=axis)

def _gelu(x):
    return jax.nn.gelu(x, approximate=True)

def _silu(x):
    return jax.nn.silu(x)

def _sigmoid(x):
    return jax.nn.sigmoid(x)

def _layernorm(x, axis=-1, eps=1e-05):
    m = jnp.mean(x, axis=axis, keepdims=True)
    v = jnp.var(x, axis=axis, keepdims=True)
    return (x - m) / jnp.sqrt(v + eps)

def _scatter_add(tgt, idx, src, axis=0):
    return tgt.at[idx].add(src)

def _segment_sum(src, seg, n):
    return jax.ops.segment_sum(src, seg, n)
kernel_name = 'mk_prb_d4_jaxref_r8_0ba322'

def setup_inputs(seed: int=0):
    np.random.seed(seed)
    _w = jnp.asarray

    def _L0_attn_setup():
        import jax, jax.numpy as jnp
        import numpy as np
        import math
        HIDDEN = 256
        HEADS = 16
        HEAD_DIM = HIDDEN // HEADS
        SEQ = 256
        BATCH = 1
        THRESH = 0.7
        key = jax.random.key(seed)
        ks = jax.random.split(key, 9)
        init = lambda k, shape: jax.random.normal(k, shape, dtype=jnp.float32) * 0.02
        return {'hidden_states': jax.random.normal(ks[0], (BATCH, SEQ, HIDDEN), dtype=jnp.float32), 'Wq': init(ks[1], (HIDDEN, HIDDEN)), 'bq': jnp.zeros((HIDDEN,), jnp.float32), 'Wk': init(ks[2], (HIDDEN, HIDDEN)), 'bk': jnp.zeros((HIDDEN,), jnp.float32), 'Wv': init(ks[3], (HIDDEN, HIDDEN)), 'bv': jnp.zeros((HIDDEN,), jnp.float32), 'Wo': init(ks[4], (HIDDEN, HIDDEN)), 'bo': jnp.zeros((HIDDEN,), jnp.float32), 'truth_gate': jnp.full((1,), THRESH, jnp.float32), 'balance_gate': jnp.full((1,), THRESH, jnp.float32), 'order_gate': jnp.full((1,), THRESH, jnp.float32), 'justice_gate': jnp.full((1,), THRESH, jnp.float32), 'harmony_gate': jnp.full((1,), THRESH, jnp.float32)}
    _L0_attn_in = _L0_attn_setup()

    def _L0_ffn_setup():
        import jax, jax.numpy as jnp
        import numpy as np
        DIM_IN = 256
        DIM_HIDDEN = 1024
        key = jax.random.key(seed)
        k_x, k_g, k_u, k_d = jax.random.split(key, 4)
        s_in = 1.0 / np.sqrt(DIM_IN)
        s_hid = 1.0 / np.sqrt(DIM_HIDDEN)
        x = jax.random.normal(k_x, (4, 256, DIM_IN), dtype=jnp.float32)
        w_gate = jax.random.uniform(k_g, (DIM_HIDDEN, DIM_IN), jnp.float32, -s_in, s_in)
        w_up = jax.random.uniform(k_u, (DIM_HIDDEN, DIM_IN), jnp.float32, -s_in, s_in)
        w_down = jax.random.uniform(k_d, (DIM_IN, DIM_HIDDEN), jnp.float32, -s_hid, s_hid)
        return {'x': x, 'w_gate': w_gate, 'w_up': w_up, 'w_down': w_down}
    _L0_ffn_in = _L0_ffn_setup()

    def _L1_attn_setup():
        import jax, jax.numpy as jnp
        import numpy as np
        EMBED = 256
        HEADS = 16
        HEAD_DIM = EMBED // HEADS
        CHUNK = 128
        BASE = 10000.0
        EPS = 1e-06

        def _alibi_log_decay(h):
            slopes = 2.0 ** (-8.0 * (jnp.arange(h, dtype=jnp.float32) + 1.0) / h)
            return -slopes

        def _lrpe_rotate(x):
            b, n, h, d = x.shape
            half = d // 2
            theta = BASE ** (-2.0 * jnp.arange(half, dtype=jnp.float32) / d)
            ang = jnp.arange(n, dtype=jnp.float32)[:, None] * theta[None, :]
            cos = jnp.cos(ang)[None, :, None, :]
            sin = jnp.sin(ang)[None, :, None, :]
            x1, x2 = (x[..., :half], x[..., half:])
            return jnp.concatenate([x1 * cos - x2 * sin, x1 * sin + x2 * cos], axis=-1)

        def _lightning_attn(q, k, v, log_lam):
            b, n, h, d = q.shape
            C = CHUNK
            nc = n // C
            qc = q.reshape(b, nc, C, h, d).transpose(1, 0, 2, 3, 4)
            kc = k.reshape(b, nc, C, h, d).transpose(1, 0, 2, 3, 4)
            vc = v.reshape(b, nc, C, h, d).transpose(1, 0, 2, 3, 4)
            i = jnp.arange(C, dtype=jnp.float32)
            diff = i[:, None] - i[None, :]
            D = jnp.where(diff[None] >= 0, jnp.exp(log_lam[:, None, None] * diff[None]), 0.0)
            decay_q = jnp.exp(log_lam[None, :] * (i[:, None] + 1.0))
            decay_k = jnp.exp(log_lam[None, :] * (C - 1.0 - i[:, None]))
            lam_C = jnp.exp(log_lam * C)

            def step(S, qkv):
                qi, ki, vi = qkv
                scores = jnp.einsum('bthd,bshd->bhts', qi, ki) * D[None]
                o_intra = jnp.einsum('bhts,bshd->bthd', scores, vi)
                o_inter = jnp.einsum('bthd,bhde->bthe', qi * decay_q[None, :, :, None], S)
                S_new = lam_C[None, :, None, None] * S + jnp.einsum('bshd,bshe->bhde', ki * decay_k[None, :, :, None], vi)
                return (S_new, o_intra + o_inter)
            S0 = jnp.zeros((b, h, d, d), q.dtype)
            _, o = jax.lax.scan(step, S0, (qc, kc, vc))
            return o.transpose(1, 0, 2, 3, 4).reshape(b, n, h, d)

        def _gated_group_rmsnorm(o, gate, weight):
            b, n, d = o.shape
            x = o * jax.nn.sigmoid(gate)
            xg = x.reshape(b, n, HEADS, HEAD_DIM)
            ms = jnp.mean(xg * xg, axis=-1, keepdims=True)
            xg = xg * jax.lax.rsqrt(ms + EPS)
            return xg.reshape(b, n, d) * weight
        key = jax.random.key(seed)
        ks = jax.random.split(key, 8)
        b, n, d = (2, 256, EMBED)
        std = 0.02
        return {'x': jax.random.normal(ks[0], (b, n, d), jnp.float32), 'Wq': jax.random.normal(ks[1], (d, d), jnp.float32) * std, 'Wk': jax.random.normal(ks[2], (d, d), jnp.float32) * std, 'Wv': jax.random.normal(ks[3], (d, d), jnp.float32) * std, 'Wo': jax.random.normal(ks[4], (d, d), jnp.float32) * std, 'Wg1': jax.random.normal(ks[5], (d, HEAD_DIM), jnp.float32) * std, 'Wg2': jax.random.normal(ks[6], (HEAD_DIM, d), jnp.float32) * std, 'norm_weight': jnp.ones((d,), jnp.float32)}
    _L1_attn_in = _L1_attn_setup()

    def _L1_ffn_setup():
        import jax, jax.numpy as jnp
        import numpy as np
        B, S, D = (4, 64, 256)
        E, K, H = (8, 2, 176)
        HS = 2 * 176
        ALPHA = 0.001
        W_SCALE = 0.02

        def _moe_forward(hidden_states, gate_w, w_gate, w_up, w_down, sw_gate, sw_up, sw_down):
            b, s, d = hidden_states.shape
            x = hidden_states.reshape(-1, d)
            T = x.shape[0]
            logits = x @ gate_w
            scores = jax.nn.softmax(logits, axis=-1)
            topk_w, topk_idx = jax.lax.top_k(scores, K)
            mask = jax.nn.one_hot(topk_idx, E, dtype=scores.dtype).sum(axis=1)
            ce = mask.mean(axis=0)
            Pi = scores.mean(axis=0)
            aux_loss = (Pi * ce * E).sum() * ALPHA
            comb = jnp.zeros((T, E), dtype=x.dtype)
            comb = comb.at[jnp.arange(T)[:, None], topk_idx].add(topk_w)
            g = jax.nn.silu(jnp.einsum('td,edh->teh', x, w_gate)) * jnp.einsum('td,edh->teh', x, w_up)
            routed = jnp.einsum('teh,ehd,te->td', g, w_down, comb)
            shared = jax.nn.silu(x @ sw_gate) * (x @ sw_up) @ sw_down
            out = (routed + shared).reshape(b, s, d)
            return (out, aux_loss)
        key = jax.random.key(seed)
        ks = jax.random.split(key, 8)
        rn = lambda k, sh: jax.random.normal(k, sh, dtype=jnp.float32)
        return {'hidden_states': rn(ks[0], (B, S, D)), 'gate_w': rn(ks[1], (D, E)) * W_SCALE, 'w_gate': rn(ks[2], (E, D, H)) * W_SCALE, 'w_up': rn(ks[3], (E, D, H)) * W_SCALE, 'w_down': rn(ks[4], (E, H, D)) * W_SCALE, 'sw_gate': rn(ks[5], (D, HS)) * W_SCALE, 'sw_up': rn(ks[6], (D, HS)) * W_SCALE, 'sw_down': rn(ks[7], (HS, D)) * W_SCALE}
    _L1_ffn_in = _L1_ffn_setup()

    def _L2_attn_setup():
        import jax, jax.numpy as jnp
        import numpy as np
        DIM = 256
        N_HEADS = 16
        N_KV_HEADS = 4
        HEAD_DIM = DIM // N_HEADS
        N_REP = N_HEADS // N_KV_HEADS
        ROPE_BASE = 10000.0

        def _rope_cos_sin(seq_len, dtype):
            inv_freq = 1.0 / ROPE_BASE ** (jnp.arange(0, HEAD_DIM, 2, dtype=jnp.float32) / HEAD_DIM)
            t = jnp.arange(seq_len, dtype=jnp.float32)
            freqs = jnp.einsum('s,d->sd', t, inv_freq)
            emb = jnp.concatenate([freqs, freqs], axis=-1)
            return (jnp.cos(emb).astype(dtype), jnp.sin(emb).astype(dtype))

        def _rotate_half(x):
            x1, x2 = jnp.split(x, 2, axis=-1)
            return jnp.concatenate([-x2, x1], axis=-1)

        def _apply_rope(x, cos, sin):
            return x * cos[None, None, :, :] + _rotate_half(x) * sin[None, None, :, :]
        key = jax.random.key(seed)
        ks = jax.random.split(key, 5)
        B, S = (2, 256)
        x = jax.random.normal(ks[0], (B, S, DIM), dtype=jnp.float32)
        sd = DIM ** (-0.5)
        wq = jax.random.normal(ks[1], (DIM, N_HEADS * HEAD_DIM), dtype=jnp.float32) * sd
        wk = jax.random.normal(ks[2], (DIM, N_KV_HEADS * HEAD_DIM), dtype=jnp.float32) * sd
        wv = jax.random.normal(ks[3], (DIM, N_KV_HEADS * HEAD_DIM), dtype=jnp.float32) * sd
        wo = jax.random.normal(ks[4], (DIM, DIM), dtype=jnp.float32) * sd
        return {'x': x, 'wq': wq, 'wk': wk, 'wv': wv, 'wo': wo}
    _L2_attn_in = _L2_attn_setup()

    def _L2_ffn_setup():
        import jax, jax.numpy as jnp
        import numpy as np
        ALPHA = 1.702
        LIMIT = 7.0
        TOP_K = 2
        E, H, I = (8, 256, 256)
        B, S = (2, 256)
        key = jax.random.key(seed)
        ks = jax.random.split(key, 7)
        return {'hidden_states': jax.random.normal(ks[0], (B, S, H), dtype=jnp.float32), 'router_weight': jax.random.normal(ks[1], (E, H), dtype=jnp.float32) * 0.02, 'router_bias': jax.random.normal(ks[2], (E,), dtype=jnp.float32) * 0.02, 'gate_up_proj': jax.random.normal(ks[3], (E, H, 2 * I), dtype=jnp.float32) * 0.02, 'gate_up_proj_bias': jax.random.normal(ks[4], (E, 2 * I), dtype=jnp.float32) * 0.02, 'down_proj': jax.random.normal(ks[5], (E, I, H), dtype=jnp.float32) * 0.02, 'down_proj_bias': jax.random.normal(ks[6], (E, H), dtype=jnp.float32) * 0.02}
    _L2_ffn_in = _L2_ffn_setup()

    def _L3_attn_setup():
        import jax, jax.numpy as jnp
        import numpy as np
        NUM_STEPS = 3
        NUM_HEADS = 8
        HEAD_DIM = 128
        EPS = 1e-05

        def layernorm(x, g, b):
            mu = jnp.mean(x, -1, keepdims=True)
            var = jnp.mean(jnp.square(x - mu), -1, keepdims=True)
            return (x - mu) * jax.lax.rsqrt(var + EPS) * g + b

        def entmax15(x):
            x = (x - jnp.max(x, -1, keepdims=True)) / 2.0
            xs = jnp.flip(jnp.sort(x, -1), -1)
            rho = jnp.arange(1, x.shape[-1] + 1, dtype=x.dtype)
            mean = jnp.cumsum(xs, -1) / rho
            meansq = jnp.cumsum(xs * xs, -1) / rho
            ss = rho * (meansq - jnp.square(mean))
            tau = mean - jnp.sqrt(jnp.clip((1.0 - ss) / rho, 0.0, None))
            support = jnp.sum(tau <= xs, -1, keepdims=True)
            tau_star = jnp.take_along_axis(tau, support - 1, -1)
            return jnp.square(jnp.clip(x - tau_star, 0.0, None))
        key = jax.random.key(seed)
        ks = jax.random.split(key, 6)
        B, S, Hd, Md, N = (2, 128, 256, 128, 256)
        THD = NUM_HEADS * HEAD_DIM
        return {'hidden': jax.random.normal(ks[0], (B, S, Hd), jnp.float32), 'memory': jax.random.normal(ks[1], (N, Md), jnp.float32), 'Wq': jax.random.normal(ks[2], (THD, Hd), jnp.float32) / np.float32(np.sqrt(Hd)), 'Wk': jax.random.normal(ks[3], (THD, Md), jnp.float32) / np.float32(np.sqrt(Md)), 'Wv': jax.random.normal(ks[4], (THD, Md), jnp.float32) / np.float32(np.sqrt(Md)), 'Wo': jax.random.normal(ks[5], (Hd, THD), jnp.float32) / np.float32(np.sqrt(THD)), 'log_beta': jnp.full((NUM_HEADS,), float(np.log(1.0 / np.sqrt(HEAD_DIM))), jnp.float32), 'g_state': jnp.ones((Hd,), jnp.float32), 'b_state': jnp.zeros((Hd,), jnp.float32), 'g_mem': jnp.ones((Md,), jnp.float32), 'b_mem': jnp.zeros((Md,), jnp.float32)}
    _L3_attn_in = _L3_attn_setup()

    def _L3_ffn_setup():
        import jax, jax.numpy as jnp
        import numpy as np
        B, S, H = (4, 128, 256)
        E, K, I, SI = (16, 4, 176, 704)

        def _silu_mul(gu, inter):
            return jax.nn.silu(gu[:, :inter]) * gu[:, inter:]
        key = jax.random.key(seed)
        ks = jax.random.split(key, 7)
        s = 0.02
        return {'hidden_states': jax.random.normal(ks[0], (B, S, H), jnp.float32), 'gate_w': jax.random.normal(ks[1], (E, H), jnp.float32) * s, 'expert_gate_up': jax.random.normal(ks[2], (E, 2 * I, H), jnp.float32) * s, 'expert_down': jax.random.normal(ks[3], (E, H, I), jnp.float32) * s, 'shared_gate_up': jax.random.normal(ks[4], (2 * SI, H), jnp.float32) * s, 'shared_down': jax.random.normal(ks[5], (H, SI), jnp.float32) * s, 'shared_gate_vec': jax.random.normal(ks[6], (1, H), jnp.float32) * s}
    _L3_ffn_in = _L3_ffn_setup()
    _d = {'L0_attn_hidden_states': _L0_attn_in['hidden_states'], 'L0_attn_Wq': _L0_attn_in['Wq'], 'L0_attn_bq': _L0_attn_in['bq'], 'L0_attn_Wk': _L0_attn_in['Wk'], 'L0_attn_bk': _L0_attn_in['bk'], 'L0_attn_Wv': _L0_attn_in['Wv'], 'L0_attn_bv': _L0_attn_in['bv'], 'L0_attn_Wo': _L0_attn_in['Wo'], 'L0_attn_bo': _L0_attn_in['bo'], 'L0_attn_truth_gate': _L0_attn_in['truth_gate'], 'L0_attn_balance_gate': _L0_attn_in['balance_gate'], 'L0_attn_order_gate': _L0_attn_in['order_gate'], 'L0_attn_justice_gate': _L0_attn_in['justice_gate'], 'L0_attn_harmony_gate': _L0_attn_in['harmony_gate'], 'L0_ffn_w_gate': _L0_ffn_in['w_gate'], 'L0_ffn_w_up': _L0_ffn_in['w_up'], 'L0_ffn_w_down': _L0_ffn_in['w_down'], 'L1_attn_Wq': _L1_attn_in['Wq'], 'L1_attn_Wk': _L1_attn_in['Wk'], 'L1_attn_Wv': _L1_attn_in['Wv'], 'L1_attn_Wo': _L1_attn_in['Wo'], 'L1_attn_Wg1': _L1_attn_in['Wg1'], 'L1_attn_Wg2': _L1_attn_in['Wg2'], 'L1_attn_norm_weight': _L1_attn_in['norm_weight'], 'L1_ffn_gate_w': _L1_ffn_in['gate_w'], 'L1_ffn_w_gate': _L1_ffn_in['w_gate'], 'L1_ffn_w_up': _L1_ffn_in['w_up'], 'L1_ffn_w_down': _L1_ffn_in['w_down'], 'L1_ffn_sw_gate': _L1_ffn_in['sw_gate'], 'L1_ffn_sw_up': _L1_ffn_in['sw_up'], 'L1_ffn_sw_down': _L1_ffn_in['sw_down'], 'L2_attn_wq': _L2_attn_in['wq'], 'L2_attn_wk': _L2_attn_in['wk'], 'L2_attn_wv': _L2_attn_in['wv'], 'L2_attn_wo': _L2_attn_in['wo'], 'L2_ffn_router_weight': _L2_ffn_in['router_weight'], 'L2_ffn_router_bias': _L2_ffn_in['router_bias'], 'L2_ffn_gate_up_proj': _L2_ffn_in['gate_up_proj'], 'L2_ffn_gate_up_proj_bias': _L2_ffn_in['gate_up_proj_bias'], 'L2_ffn_down_proj': _L2_ffn_in['down_proj'], 'L2_ffn_down_proj_bias': _L2_ffn_in['down_proj_bias'], 'L3_attn_memory': _L3_attn_in['memory'], 'L3_attn_Wq': _L3_attn_in['Wq'], 'L3_attn_Wk': _L3_attn_in['Wk'], 'L3_attn_Wv': _L3_attn_in['Wv'], 'L3_attn_Wo': _L3_attn_in['Wo'], 'L3_attn_log_beta': _L3_attn_in['log_beta'], 'L3_attn_g_state': _L3_attn_in['g_state'], 'L3_attn_b_state': _L3_attn_in['b_state'], 'L3_attn_g_mem': _L3_attn_in['g_mem'], 'L3_attn_b_mem': _L3_attn_in['b_mem'], 'L3_ffn_gate_w': _L3_ffn_in['gate_w'], 'L3_ffn_expert_gate_up': _L3_ffn_in['expert_gate_up'], 'L3_ffn_expert_down': _L3_ffn_in['expert_down'], 'L3_ffn_shared_gate_up': _L3_ffn_in['shared_gate_up'], 'L3_ffn_shared_down': _L3_ffn_in['shared_down'], 'L3_ffn_shared_gate_vec': _L3_ffn_in['shared_gate_vec']}
    _x0 = _d['L0_attn_hidden_states']
    _d['L0_attn_hidden_states'] = jax.random.normal(jax.random.fold_in(jax.random.key(seed), 1), (2, 512, 256), dtype=_x0.dtype)
    del _x0
    return _d

def reference(L0_attn_hidden_states, L0_attn_Wq, L0_attn_bq, L0_attn_Wk, L0_attn_bk, L0_attn_Wv, L0_attn_bv, L0_attn_Wo, L0_attn_bo, L0_attn_truth_gate, L0_attn_balance_gate, L0_attn_order_gate, L0_attn_justice_gate, L0_attn_harmony_gate, L0_ffn_w_gate, L0_ffn_w_up, L0_ffn_w_down, L1_attn_Wq, L1_attn_Wk, L1_attn_Wv, L1_attn_Wo, L1_attn_Wg1, L1_attn_Wg2, L1_attn_norm_weight, L1_ffn_gate_w, L1_ffn_w_gate, L1_ffn_w_up, L1_ffn_w_down, L1_ffn_sw_gate, L1_ffn_sw_up, L1_ffn_sw_down, L2_attn_wq, L2_attn_wk, L2_attn_wv, L2_attn_wo, L2_ffn_router_weight, L2_ffn_router_bias, L2_ffn_gate_up_proj, L2_ffn_gate_up_proj_bias, L2_ffn_down_proj, L2_ffn_down_proj_bias, L3_attn_memory, L3_attn_Wq, L3_attn_Wk, L3_attn_Wv, L3_attn_Wo, L3_attn_log_beta, L3_attn_g_state, L3_attn_b_state, L3_attn_g_mem, L3_attn_b_mem, L3_ffn_gate_w, L3_ffn_expert_gate_up, L3_ffn_expert_down, L3_ffn_shared_gate_up, L3_ffn_shared_down, L3_ffn_shared_gate_vec):

    def _L0_attn_ref(hidden_states, Wq, bq, Wk, bk, Wv, bv, Wo, bo, truth_gate, balance_gate, order_gate, justice_gate, harmony_gate):
        import jax, jax.numpy as jnp
        import numpy as np
        import math
        HIDDEN = 256
        HEADS = 16
        HEAD_DIM = HIDDEN // HEADS
        SEQ = 256
        BATCH = 1
        THRESH = 0.7
        B, S, D = hidden_states.shape
        H, hd = (HEADS, HEAD_DIM)

        def proj(W, b):
            return (hidden_states @ W.T + b).reshape(B, S, H, hd).transpose(0, 2, 1, 3)
        q, k, v = (proj(Wq, bq), proj(Wk, bk), proj(Wv, bv))
        scores = jnp.einsum('bhqd,bhkd->bhqk', q, k) / math.sqrt(hd)
        truth_penalty = jax.nn.sigmoid(truth_gate) * (jnp.linalg.norm(k, axis=-1, keepdims=True) * 0.01)
        logp = jax.nn.log_softmax(scores, axis=-1)
        entropy = -jnp.sum(jnp.exp(logp) * logp, axis=-1, keepdims=True)
        balance_adjustment = jax.nn.sigmoid(balance_gate) * (entropy / math.log(S) * 0.1)
        position_bias = jnp.arange(S, dtype=jnp.float32) / S
        order_bonus = jax.nn.sigmoid(order_gate) * (position_bias * 0.05)
        mean_score = scores.mean(axis=-1, keepdims=True)
        justice_adjustment = jax.nn.sigmoid(justice_gate) * ((mean_score - scores) * 0.1)
        smoothness = -jnp.abs(scores[..., 1:] - scores[..., :-1]).mean(axis=-1, keepdims=True)
        harmony_smooth = jax.nn.sigmoid(harmony_gate) * (smoothness * 0.1)
        scores = scores - truth_penalty + balance_adjustment + order_bonus + justice_adjustment + harmony_smooth
        attn = jax.nn.softmax(scores, axis=-1)
        out = jnp.einsum('bhqk,bhkd->bhqd', attn, v)
        out = out.transpose(0, 2, 1, 3).reshape(B, S, D)
        return out @ Wo.T + bo

    def _L0_ffn_ref(x, w_gate, w_up, w_down):
        import jax, jax.numpy as jnp
        import numpy as np
        DIM_IN = 256
        DIM_HIDDEN = 1024
        gate = jnp.einsum('bsd,hd->bsh', x, w_gate)
        up = jnp.einsum('bsd,hd->bsh', x, w_up)
        gated = jax.nn.silu(gate) * up
        return jnp.einsum('bsh,dh->bsd', gated, w_down)

    def _L1_attn_ref(x, Wq, Wk, Wv, Wo, Wg1, Wg2, norm_weight):
        import jax, jax.numpy as jnp
        import numpy as np
        EMBED = 256
        HEADS = 16
        HEAD_DIM = EMBED // HEADS
        CHUNK = 128
        BASE = 10000.0
        EPS = 1e-06

        def _alibi_log_decay(h):
            slopes = 2.0 ** (-8.0 * (jnp.arange(h, dtype=jnp.float32) + 1.0) / h)
            return -slopes

        def _lrpe_rotate(x):
            b, n, h, d = x.shape
            half = d // 2
            theta = BASE ** (-2.0 * jnp.arange(half, dtype=jnp.float32) / d)
            ang = jnp.arange(n, dtype=jnp.float32)[:, None] * theta[None, :]
            cos = jnp.cos(ang)[None, :, None, :]
            sin = jnp.sin(ang)[None, :, None, :]
            x1, x2 = (x[..., :half], x[..., half:])
            return jnp.concatenate([x1 * cos - x2 * sin, x1 * sin + x2 * cos], axis=-1)

        def _lightning_attn(q, k, v, log_lam):
            b, n, h, d = q.shape
            C = CHUNK
            nc = n // C
            qc = q.reshape(b, nc, C, h, d).transpose(1, 0, 2, 3, 4)
            kc = k.reshape(b, nc, C, h, d).transpose(1, 0, 2, 3, 4)
            vc = v.reshape(b, nc, C, h, d).transpose(1, 0, 2, 3, 4)
            i = jnp.arange(C, dtype=jnp.float32)
            diff = i[:, None] - i[None, :]
            D = jnp.where(diff[None] >= 0, jnp.exp(log_lam[:, None, None] * diff[None]), 0.0)
            decay_q = jnp.exp(log_lam[None, :] * (i[:, None] + 1.0))
            decay_k = jnp.exp(log_lam[None, :] * (C - 1.0 - i[:, None]))
            lam_C = jnp.exp(log_lam * C)

            def step(S, qkv):
                qi, ki, vi = qkv
                scores = jnp.einsum('bthd,bshd->bhts', qi, ki) * D[None]
                o_intra = jnp.einsum('bhts,bshd->bthd', scores, vi)
                o_inter = jnp.einsum('bthd,bhde->bthe', qi * decay_q[None, :, :, None], S)
                S_new = lam_C[None, :, None, None] * S + jnp.einsum('bshd,bshe->bhde', ki * decay_k[None, :, :, None], vi)
                return (S_new, o_intra + o_inter)
            S0 = jnp.zeros((b, h, d, d), q.dtype)
            _, o = jax.lax.scan(step, S0, (qc, kc, vc))
            return o.transpose(1, 0, 2, 3, 4).reshape(b, n, h, d)

        def _gated_group_rmsnorm(o, gate, weight):
            b, n, d = o.shape
            x = o * jax.nn.sigmoid(gate)
            xg = x.reshape(b, n, HEADS, HEAD_DIM)
            ms = jnp.mean(xg * xg, axis=-1, keepdims=True)
            xg = xg * jax.lax.rsqrt(ms + EPS)
            return xg.reshape(b, n, d) * weight
        b, n, d = x.shape
        q = (x @ Wq).reshape(b, n, HEADS, HEAD_DIM)
        k = (x @ Wk).reshape(b, n, HEADS, HEAD_DIM)
        v = (x @ Wv).reshape(b, n, HEADS, HEAD_DIM)
        q = jax.nn.silu(q)
        k = jax.nn.silu(k)
        q = _lrpe_rotate(q)
        k = _lrpe_rotate(k)
        log_lam = _alibi_log_decay(HEADS)
        o = _lightning_attn(q, k, v, log_lam).reshape(b, n, d)
        gate = x @ Wg1 @ Wg2
        o = _gated_group_rmsnorm(o, gate, norm_weight)
        return o @ Wo

    def _L1_ffn_ref(hidden_states, gate_w, w_gate, w_up, w_down, sw_gate, sw_up, sw_down):
        import jax, jax.numpy as jnp
        import numpy as np
        B, S, D = (4, 64, 256)
        E, K, H = (8, 2, 176)
        HS = 2 * 176
        ALPHA = 0.001
        W_SCALE = 0.02

        def _moe_forward(hidden_states, gate_w, w_gate, w_up, w_down, sw_gate, sw_up, sw_down):
            b, s, d = hidden_states.shape
            x = hidden_states.reshape(-1, d)
            T = x.shape[0]
            logits = x @ gate_w
            scores = jax.nn.softmax(logits, axis=-1)
            topk_w, topk_idx = jax.lax.top_k(scores, K)
            mask = jax.nn.one_hot(topk_idx, E, dtype=scores.dtype).sum(axis=1)
            ce = mask.mean(axis=0)
            Pi = scores.mean(axis=0)
            aux_loss = (Pi * ce * E).sum() * ALPHA
            comb = jnp.zeros((T, E), dtype=x.dtype)
            comb = comb.at[jnp.arange(T)[:, None], topk_idx].add(topk_w)
            g = jax.nn.silu(jnp.einsum('td,edh->teh', x, w_gate)) * jnp.einsum('td,edh->teh', x, w_up)
            routed = jnp.einsum('teh,ehd,te->td', g, w_down, comb)
            shared = jax.nn.silu(x @ sw_gate) * (x @ sw_up) @ sw_down
            out = (routed + shared).reshape(b, s, d)
            return (out, aux_loss)
        out, _aux = _moe_forward(hidden_states, gate_w, w_gate, w_up, w_down, sw_gate, sw_up, sw_down)
        return out

    def _L2_attn_ref(x, wq, wk, wv, wo):
        import jax, jax.numpy as jnp
        import numpy as np
        DIM = 256
        N_HEADS = 16
        N_KV_HEADS = 4
        HEAD_DIM = DIM // N_HEADS
        N_REP = N_HEADS // N_KV_HEADS
        ROPE_BASE = 10000.0

        def _rope_cos_sin(seq_len, dtype):
            inv_freq = 1.0 / ROPE_BASE ** (jnp.arange(0, HEAD_DIM, 2, dtype=jnp.float32) / HEAD_DIM)
            t = jnp.arange(seq_len, dtype=jnp.float32)
            freqs = jnp.einsum('s,d->sd', t, inv_freq)
            emb = jnp.concatenate([freqs, freqs], axis=-1)
            return (jnp.cos(emb).astype(dtype), jnp.sin(emb).astype(dtype))

        def _rotate_half(x):
            x1, x2 = jnp.split(x, 2, axis=-1)
            return jnp.concatenate([-x2, x1], axis=-1)

        def _apply_rope(x, cos, sin):
            return x * cos[None, None, :, :] + _rotate_half(x) * sin[None, None, :, :]
        B, S, _ = x.shape
        scale = HEAD_DIM ** (-0.5)
        q = (x @ wq).reshape(B, S, N_HEADS, HEAD_DIM).transpose(0, 2, 1, 3)
        k = (x @ wk).reshape(B, S, N_KV_HEADS, HEAD_DIM).transpose(0, 2, 1, 3)
        v = (x @ wv).reshape(B, S, N_KV_HEADS, HEAD_DIM).transpose(0, 2, 1, 3)
        k = jnp.repeat(k, N_REP, axis=1)
        v = jnp.repeat(v, N_REP, axis=1)
        cos, sin = _rope_cos_sin(S, x.dtype)
        q = _apply_rope(q, cos, sin)
        k = _apply_rope(k, cos, sin)
        attn = jnp.einsum('bhqd,bhkd->bhqk', q, k) * scale
        causal = jnp.triu(jnp.ones((S, S), dtype=bool), k=1)
        attn = jnp.where(causal[None, None], -jnp.inf, attn)
        attn = jax.nn.softmax(attn.astype(jnp.float32), axis=-1).astype(q.dtype)
        out = jnp.einsum('bhqk,bhkd->bhqd', attn, v)
        out = out.transpose(0, 2, 1, 3).reshape(B, S, DIM)
        return out @ wo

    def _L2_ffn_ref(hidden_states, router_weight, router_bias, gate_up_proj, gate_up_proj_bias, down_proj, down_proj_bias):
        import jax, jax.numpy as jnp
        import numpy as np
        ALPHA = 1.702
        LIMIT = 7.0
        TOP_K = 2
        E, H, I = (8, 256, 256)
        B, S = (2, 256)
        bsz, seq_len, hidden = hidden_states.shape
        h = hidden_states.reshape(-1, hidden)
        T = h.shape[0]
        logits = h @ router_weight.T + router_bias
        top_vals, top_idx = jax.lax.top_k(logits, TOP_K)
        top_w = jax.nn.softmax(top_vals, axis=-1)
        scores = jnp.zeros_like(logits).at[jnp.arange(T)[:, None], top_idx].set(top_w)
        gate_up = jnp.einsum('th,ehj->etj', h, gate_up_proj) + gate_up_proj_bias[:, None, :]
        gate = gate_up[..., ::2]
        up = gate_up[..., 1::2]
        gate = jnp.minimum(gate, LIMIT)
        up = jnp.clip(up, -LIMIT, LIMIT)
        glu = gate * jax.nn.sigmoid(gate * ALPHA)
        act = (up + 1.0) * glu
        expert_out = jnp.einsum('eti,eih->eth', act, down_proj) + down_proj_bias[:, None, :]
        out = jnp.einsum('te,eth->th', scores, expert_out)
        return out.reshape(bsz, seq_len, hidden)

    def _L3_attn_ref(hidden, memory, Wq, Wk, Wv, Wo, log_beta, g_state, b_state, g_mem, b_mem):
        import jax, jax.numpy as jnp
        import numpy as np
        NUM_STEPS = 3
        NUM_HEADS = 8
        HEAD_DIM = 128
        EPS = 1e-05

        def layernorm(x, g, b):
            mu = jnp.mean(x, -1, keepdims=True)
            var = jnp.mean(jnp.square(x - mu), -1, keepdims=True)
            return (x - mu) * jax.lax.rsqrt(var + EPS) * g + b

        def entmax15(x):
            x = (x - jnp.max(x, -1, keepdims=True)) / 2.0
            xs = jnp.flip(jnp.sort(x, -1), -1)
            rho = jnp.arange(1, x.shape[-1] + 1, dtype=x.dtype)
            mean = jnp.cumsum(xs, -1) / rho
            meansq = jnp.cumsum(xs * xs, -1) / rho
            ss = rho * (meansq - jnp.square(mean))
            tau = mean - jnp.sqrt(jnp.clip((1.0 - ss) / rho, 0.0, None))
            support = jnp.sum(tau <= xs, -1, keepdims=True)
            tau_star = jnp.take_along_axis(tau, support - 1, -1)
            return jnp.square(jnp.clip(x - tau_star, 0.0, None))
        B, S, _ = hidden.shape
        N = memory.shape[0]
        H, hd = (NUM_HEADS, HEAD_DIM)
        Q = layernorm(hidden, g_state, b_state) @ Wq.T
        mn = layernorm(memory, g_mem, b_mem)
        K = (mn @ Wk.T).reshape(N, H, hd).transpose(1, 0, 2)
        V = (mn @ Wv.T).reshape(N, H, hd).transpose(1, 0, 2)
        xi = Q.reshape(B, S, H, hd).transpose(0, 2, 1, 3)
        beta = jnp.exp(log_beta)[None, :, None, None]
        for _ in range(NUM_STEPS):
            scores = jnp.einsum('bhsd,hnd->bhsn', xi, K) * beta
            w = entmax15(scores)
            xi = jnp.einsum('bhsn,hnd->bhsd', w, V)
        out = xi.transpose(0, 2, 1, 3).reshape(B, S, H * hd) @ Wo.T
        return out

    def _L3_ffn_ref(hidden_states, gate_w, expert_gate_up, expert_down, shared_gate_up, shared_down, shared_gate_vec):
        import jax, jax.numpy as jnp
        import numpy as np
        B, S, H = (4, 128, 256)
        E, K, I, SI = (16, 4, 176, 704)

        def _silu_mul(gu, inter):
            return jax.nn.silu(gu[:, :inter]) * gu[:, inter:]
        orig_shape = hidden_states.shape
        x = hidden_states.reshape(-1, H)
        router_logits = x @ gate_w.T
        routing_probs = jax.nn.softmax(router_logits.astype(jnp.float32), axis=-1)
        topk_w, topk_idx = jax.lax.top_k(routing_probs, K)
        topk_w = topk_w / topk_w.sum(axis=-1, keepdims=True)
        topk_w = topk_w.astype(x.dtype)
        combine = (jax.nn.one_hot(topk_idx, E, dtype=x.dtype) * topk_w[..., None]).sum(1)
        shared = _silu_mul(x @ shared_gate_up.T, SI) @ shared_down.T
        shared = shared * jax.nn.sigmoid(x @ shared_gate_vec.T)

        def step(acc, ew):
            w_gu, w_d, cw = ew
            h = _silu_mul(x @ w_gu.T, I)
            return (acc + h @ w_d.T * cw[:, None], None)
        acc0 = jnp.zeros_like(x)
        sparse, _ = jax.lax.scan(step, acc0, (expert_gate_up, expert_down, combine.T))
        return (shared + sparse).reshape(orig_shape)
    x = L0_attn_hidden_states
    xn = _layernorm(x, axis=-1)
    x = x + _L0_attn_ref(xn, L0_attn_Wq, L0_attn_bq, L0_attn_Wk, L0_attn_bk, L0_attn_Wv, L0_attn_bv, L0_attn_Wo, L0_attn_bo, L0_attn_truth_gate, L0_attn_balance_gate, L0_attn_order_gate, L0_attn_justice_gate, L0_attn_harmony_gate) + _L0_ffn_ref(xn, L0_ffn_w_gate, L0_ffn_w_up, L0_ffn_w_down)
    xn = _layernorm(x, axis=-1)
    x = x + _L1_attn_ref(xn, L1_attn_Wq, L1_attn_Wk, L1_attn_Wv, L1_attn_Wo, L1_attn_Wg1, L1_attn_Wg2, L1_attn_norm_weight) + _L1_ffn_ref(xn, L1_ffn_gate_w, L1_ffn_w_gate, L1_ffn_w_up, L1_ffn_w_down, L1_ffn_sw_gate, L1_ffn_sw_up, L1_ffn_sw_down)
    xn = _layernorm(x, axis=-1)
    x = x + _L2_attn_ref(xn, L2_attn_wq, L2_attn_wk, L2_attn_wv, L2_attn_wo) + _L2_ffn_ref(xn, L2_ffn_router_weight, L2_ffn_router_bias, L2_ffn_gate_up_proj, L2_ffn_gate_up_proj_bias, L2_ffn_down_proj, L2_ffn_down_proj_bias)
    xn = _layernorm(x, axis=-1)
    x = x + _L3_attn_ref(xn, L3_attn_memory, L3_attn_Wq, L3_attn_Wk, L3_attn_Wv, L3_attn_Wo, L3_attn_log_beta, L3_attn_g_state, L3_attn_b_state, L3_attn_g_mem, L3_attn_b_mem) + _L3_ffn_ref(xn, L3_ffn_gate_w, L3_ffn_expert_gate_up, L3_ffn_expert_down, L3_ffn_shared_gate_up, L3_ffn_shared_down, L3_ffn_shared_gate_vec)
    return x

_drawn_inputs = setup_inputs


def setup_inputs(seed=0):
    import zlib

    import numpy as np

    out = dict(_drawn_inputs(seed))
    spreads = {'L0_attn_bq': (0.0, 0.8),
     'L0_attn_bk': (0.0, 2.0),
     'L0_attn_bv': (0.0, 0.1),
     'L0_attn_bo': (0.0, 0.1),
     'L1_attn_norm_weight': (1.0, 0.2),
     'L3_attn_log_beta': (-2.4260151386260986, 0.2),
     'L3_attn_g_state': (1.0, 0.2),
     'L3_attn_b_state': (0.0, 0.29),
     'L3_attn_g_mem': (1.0, 0.2),
     'L3_attn_b_mem': (0.0, 0.28)}
    factors = {'L0_attn_Wq': 8.0,
     'L0_attn_Wk': 8.0,
     'L0_attn_Wv': 3.362,
     'L1_attn_Wg1': 5.2,
     'L1_attn_Wg2': 5.377,
     'L1_ffn_gate_w': 6.747,
     'L1_ffn_w_gate': 5.849,
     'L1_ffn_w_up': 5.938,
     'L1_ffn_w_down': 5.773,
     'L2_ffn_router_bias': 10.027,
     'L2_ffn_gate_up_proj_bias': 8.0,
     'L3_ffn_gate_w': 8.0,
     'L3_ffn_expert_gate_up': 8.0,
     'L3_ffn_expert_down': 8.0,
     'L3_ffn_shared_gate_up': 4.533,
     'L3_ffn_shared_down': 4.448,
     'L3_ffn_shared_gate_vec': 8.0,
     'L1_ffn_sw_gate': 3.029,
     'L1_ffn_sw_up': 2.739,
     'L1_ffn_sw_down': 2.89,
     'L2_ffn_down_proj_bias': 3.593}
    for name, (base, spread) in spreads.items():
        noise = np.random.default_rng([zlib.crc32(name.encode()), seed]).standard_normal(out[name].shape)
        drawn = base * np.exp(spread * noise) if base else spread * noise
        out[name] = jnp.asarray(drawn.astype(out[name].dtype))
    for name, factor in factors.items():
        out[name] = (out[name] * factor).astype(out[name].dtype)
    return out
```

```python
from contextlib import ExitStack

import concourse.bass as bass
from concourse import mybir

F32 = mybir.dt.float32
BF16 = mybir.dt.bfloat16
ALU = mybir.AluOpType
ACT = mybir.ActivationFunctionType
AX = mybir.AxisListType

P = 128
D = 256
KD = D // P
AREA = 17800
WAREA = 6144
B, S = 2, 512
TOK = B * S
NT = TOK // P
TPS = S // P
H, HD = 16, 16
GH = P // HD
NG = H // GH
VW = HD + 1
NE = 17
CR = 3 * NE
GUW = 2 * D
EXPERTS = (0, 8, 8, 16)
TOPK = (0, 2, 2, 4)
CHUNKS = (8, 14, 16, 28)
LN_EPS = 1e-5
MASKED = -1e30
H3, HD3 = 8, 128
MEM = 256
STEPS3 = 3
BARRIERS = 25
NEWTON = 5


def build(nc, a, out):
    with ExitStack() as ctx:
        def sb(name, shape, dt=F32):
            return ctx.enter_context(nc.sbuf_tensor(name, shape, dt))

        area = sb("area", [P, AREA])
        taken = {0: 0, 1: 0, 3: 0}
        warea = sb("warea", [P, WAREA])
        wtaken = {0: 0, 3: 0}

        def part(layer, shape, area=area, taken=taken, AREA=AREA):
            size = 1
            for k in shape[1:]:
                size *= k
            at = taken[layer]
            taken[layer] = at + size
            assert at + size <= AREA
            names = "abcd"[:len(shape) - 1]
            return area[:, at:at + size].rearrange(f"p ({' '.join(names)}) -> p {' '.join(names)}",
                                                   **dict(zip(names, shape[1:])))

        def wpart(layer, shape):
            return part(layer, shape, warea, wtaken, WAREA)

        def sem(name):
            return ctx.enter_context(nc.semaphore(name))

        bank = [ctx.enter_context(nc.psum_tensor(f"bank{i}", [P, 512], F32)) for i in range(8)]

        ident = sb("ident", [P, P])
        identb = sb("identb", [P, P], BF16)
        head_mask = sb("head_mask", [P, GH])
        causal = sb("causal", [P, P])
        rope = sb("rope", [P, 2, TPS, 2, HD // 2])
        half_neg = sb("half_neg", [P, NT * H])
        wqkv = [wpart(0, [P, KD, 768]), wpart(0, [P, KD, 768]), sb("wqkv2", [P, KD, 576])]
        wo = [sb(f"wo{n}", [P, KD, D]) for n in range(3)]
        bqkv = wpart(0, [P, 768])
        bo = sb("bo", [P, D])
        gates = sb("gates", [P, 5])
        router = [None, sb("router1", [P, KD, 8]), sb("router2", [P, KD, 8]), sb("router3", [P, KD, NE])]
        rbias = sb("rbias", [P, 8])
        dbias = sb("dbias", [8, D])
        gu_bias = sb("gu_bias", [P, CHUNKS[2], 2])
        lower = sb("lower", [P, 16, 16])
        decay = wpart(0, [P, H, P])
        decay_q = sb("decay_q", [P, H])
        decay_k = sb("decay_k", [P, H])
        lam_chunk = sb("lam_chunk", [P, NG, P])
        own_block = sb("own_block", [P, P])
        wg1 = sb("wg1", [P, KD, HD])
        wg2 = sb("wg2", [HD, D])
        norm_w = sb("norm_w", [P, D])

        x = sb("x", [P, NT, D])
        xnT = sb("xnT", [P, KD, TOK])
        xn = sb("xn", [P, 2, D])
        st6 = sb("st6", [P, NT, 6])
        mv = sb("mv", [P, NT, 2])
        rstd = sb("rstd", [P, NT])
        nmr = sb("nmr", [P, NT])
        tok = sb("tok", [P, 2, 512])
        tmp = sb("tmp", [P, 2, 512])
        qT = part(0, [P, NG, TOK])
        kT = part(0, [P, NG, TOK])
        v = part(0, [P, NT, H, VW])
        taken[1] = taken[0]
        kdT = part(0, [P, NG, TOK])
        raw = part(0, [P, NT, H, VW])
        ao = sb("ao", [P, NT, D])
        aoT = sb("aoT", [P, KD, TOK])
        logits = sb("logits", [P, NT, 16])
        probs = sb("probs", [P, NT, 16])
        comb = sb("comb", [P, NT, NE])
        combp = sb("combp", [P, NT, CR], BF16)
        combT = sb("combT", [CR, TOK], BF16)
        rank = sb("rank", [P, 16, 16])
        rank2 = sb("rank2", [P, 16, 16])
        rowm = sb("rowm", [P, NT])
        rowz = sb("rowz", [P, NT])
        rankn = sb("rankn", [P, NT, 16])
        shared = sb("shared", [P, NT])

        wgu = [sb(f"wgu{c}", [P, GUW]) for c in range(2)]
        wd = sb("wd", [P, 2, D])
        sel = [sb(f"sel{c}", [CR, P], BF16) for c in range(2)]
        th = sb("th", [P, 2, 512])
        gl = sb("gl", [P, 2, 512])
        up = sb("up", [P, 2, 512])
        hT = sb("hT", [P, 4, 512])

        phase_done = sem("phase_done")
        loaded = [sem(f"weights{n}_loaded") for n in range(4)]
        x_loaded = sem("x_loaded")
        phases = {}

        def barrier(eng):
            n = phases[eng.engine] = phases.get(eng.engine, 0) + 1
            eng.drain().then_inc(phase_done, 1)
            eng.wait_ge(phase_done, 4 * n)

        def mm(o, l, r, start=True, stop=True):
            return nc.tensor.matmul(o, l, r, start=start, stop=stop)

        def total(n):
            pairs = CHUNKS[n] // 2
            t = {"stats_ready": 1, "rstd_ready": 1, "xn_ready": NT, "xn_T": NT, "xnT_ready": NT}
            for k in ("qk_ready", "v_ready", "qk_tok", "qk_T", "qk_copied", "v_copied", "ao_T", "aoT_ready",
                      "o_ready", "o_added"):
                t[k] = NT if n < 3 else 0
            for k in ("logits_ready", "logits_copied"):
                t[k] = NT if n == 3 else 0
            t["route_exp"] = 2 if n else 0
            t["comb_T"] = (0, 2, 3, 2)[n]
            for k in ("guA_loaded", "guB_loaded"):
                t[k] = (32 if n else 16) * pairs
            t["down_loaded"] = 16 * pairs
            for k in ("guA_used", "guB_used", "down_used"):
                t[k] = pairs
            for k in ("gate_ready", "up_ready", "tanh_ready", "gate_used", "up_used", "h_ready", "part_ready",
                      "part_added"):
                t[k] = 4 * pairs
            for k in ("comb_ready", "comb_used"):
                t[k] = 4 * pairs if n else 0
            t["gate_clipped"] = 4 * pairs if n == 2 else 0
            return t

        LS = {k: sem(k) for k in total(0)}
        AT = [{k: sum(total(m)[k] for m in range(n)) for k in total(0)} for n in range(4)]

        def vector_norm(dve, n):
            s, at = LS, AT[n]
            if n == 0:
                dve.wait_ge(x_loaded, 16)
            for t in range(NT):
                dve.bn_stats(st6[:, t, :], x[:, t, :])
            dve.drain()
            for t in range(NT):
                last = dve.bn_aggr(mv[:, t, :], st6[:, t, :])
            last.then_inc(s["stats_ready"], 1)
            for t in range(NT):
                dve.wait_ge(s["xn_T"], at["xn_T"] + t + 1)
                dve.tensor_copy(xnT[:, :, t * P:(t + 1) * P],
                                bank[t % 2][:, 0:D].rearrange("p (k t) -> p k t", k=KD)).then_inc(s["xnT_ready"], 1)

        def pool_norm(pool, n):
            s, at = LS, AT[n]
            pool.wait_ge(s["stats_ready"], at["stats_ready"] + 1)
            pool.tensor_scalar(rstd[:], mv[:, :, 1], LN_EPS, None, ALU.add)
            pool.drain()
            pool.tensor_tensor(rstd[:], rstd[:], half_neg[:, 0:NT], ALU.pow)
            pool.drain()
            pool.tensor_tensor(nmr[:], mv[:, :, 0], rstd[:], ALU.mult)
            pool.drain()
            pool.tensor_scalar(nmr[:], nmr[:], -1.0, None, ALU.mult).then_inc(s["rstd_ready"], 1)

        def scalar_norm(act, n):
            s, at = LS, AT[n]
            act.wait_ge(s["rstd_ready"], at["rstd_ready"] + 1)
            for t in range(NT):
                if t >= 2:
                    act.wait_ge(s["xn_T"], at["xn_T"] + t - 1)
                act.activation(xn[:, t % 2, :], x[:, t, :], ACT.Identity, bias=nmr[:, t:t + 1],
                               scale=rstd[:, t:t + 1]).then_inc(s["xn_ready"], 1)

        def tensor_norm(pe, n):
            s, at = LS, AT[n]
            for t in range(NT):
                pe.wait_ge(s["xn_ready"], at["xn_ready"] + t + 1)
                if t >= 2:
                    pe.wait_ge(s["xnT_ready"], at["xnT_ready"] + t - 1)
                for k in range(KD):
                    last = nc.tensor.transpose(bank[t % 2][:, k * P:(k + 1) * P], xn[:, t % 2, k * P:(k + 1) * P],
                                               ident[:])
                last.then_inc(s["xn_T"], 1)

        def tensor_project(pe, n):
            s, at = LS, AT[n]
            vw = wqkv[n].shape[2] - 512

            def turn(t):
                pe.wait_ge(s["qk_tok"], at["qk_tok"] + t + 1)
                if t >= 2:
                    pe.wait_ge(s["qk_copied"], at["qk_copied"] + t - 1)
                for c in range(4):
                    last = nc.tensor.transpose(bank[4 + t % 2][:, c * P:(c + 1) * P],
                                               tok[:, t % 2, c * P:(c + 1) * P], ident[:])
                last.then_inc(s["qk_T"], 1)

            for t in range(NT):
                pe.wait_ge(s["xnT_ready"], at["xnT_ready"] + t + 1)
                if t >= 2:
                    pe.wait_ge(s["qk_tok"], at["qk_tok"] + t - 1)
                ts = slice(t * P, (t + 1) * P)
                for k in range(KD):
                    last = mm(bank[t % 2][:], xnT[:, k, ts], wqkv[n][:, k, 0:512], k == 0, k == KD - 1)
                last.then_inc(s["qk_ready"], 1)
                if t >= 2:
                    pe.wait_ge(s["v_copied"], at["v_copied"] + t - 1)
                for k in range(KD):
                    last = mm(bank[2 + t % 2][:, 0:vw], xnT[:, k, ts], wqkv[n][:, k, 512:], k == 0, k == KD - 1)
                if n:
                    for k in range(KD):
                        last = mm(bank[2 + t % 2][:, D:D + 8], xnT[:, k, ts], router[n][:, k, :], k == 0, k == KD - 1)
                last.then_inc(s["v_ready"], 1)
                if t:
                    turn(t - 1)
            turn(NT - 1)

        def vector_project(dve, n):
            s, at = LS, AT[n]
            for t in range(NT):
                dve.wait_ge(s["qk_ready"], at["qk_ready"] + t + 1)
                if t >= 2:
                    dve.wait_ge(s["qk_T"], at["qk_T"] + t - 1)
                o, qk = tok[:, t % 2, :], bank[t % 2]
                if n == 0:
                    dve.tensor_tensor(o, qk[:], bqkv[:, 0:512], ALU.add).then_inc(s["qk_tok"], 1)
                else:
                    src = qk[:]
                    if n == 1:
                        dve.wait_ge(silu_tanh, t + 1)
                        dve.scalar_tensor_tensor(tmp[:, 0, :], th[:, t % 2, :], 1.0, qk[:], ALU.add, ALU.mult)
                        dve.drain()
                        dve.tensor_scalar(tmp[:, 0, :], tmp[:, 0, :], 0.5, None, ALU.mult)
                        dve.drain()
                        src = tmp[:, 0, :]
                    sh = src.rearrange("p (h a e) -> p h a e", a=2, e=HD // 2)
                    oh = o.rearrange("p (h a e) -> p h a e", a=2, e=HD // 2)
                    mh = tmp[:, 1, :].rearrange("p (h a e) -> p h a e", a=2, e=HD // 2)
                    cs = [rope[:, n - 1, t % TPS, i, :].unsqueeze(1).to_broadcast([P, 2 * H, HD // 2]) for i in (0, 1)]
                    for a2 in (0, 1):
                        dve.tensor_tensor(oh[:, :, a2, :], sh[:, :, a2, :], cs[0], ALU.mult)
                        dve.tensor_tensor(mh[:, :, a2, :], sh[:, :, 1 - a2, :], cs[1], ALU.mult)
                    dve.drain()
                    dve.tensor_tensor(oh[:, :, 0, :], oh[:, :, 0, :], mh[:, :, 0, :], ALU.subtract)
                    dve.tensor_tensor(oh[:, :, 1, :], oh[:, :, 1, :], mh[:, :, 1, :], ALU.add)
                    dve.drain().then_inc(s["qk_tok"], 1)
                if n == 0:
                    dve.drain()
                    dve.tensor_tensor(tmp[:, 0, 0:D], tok[:, t % 2, D:], tok[:, t % 2, D:], ALU.mult)
                    dve.drain()
                    dve.tensor_reduce(knorm[:, t, :], tmp[:, 0, 0:D].rearrange("p (h e) -> p h e", e=HD), AX.X, ALU.add)
                if n == 1:
                    dve.drain()
                    dve.tensor_tensor(kd[:, t, :].rearrange("p (h e) -> p h e", e=HD),
                                      tok[:, t % 2, D:].rearrange("p (h e) -> p h e", e=HD),
                                      decay_k[:].unsqueeze(2).to_broadcast([P, H, HD]), ALU.mult)
                dve.wait_ge(s["v_ready"], at["v_ready"] + t + 1)
                vb = bank[2 + t % 2]
                if n == 0:
                    dve.tensor_tensor(tmp[:, 1, 0:D], vb[:, 0:D], bqkv[:, 512:], ALU.add)
                    dve.drain().then_inc(s["v_copied"], 1)
                    dve.tensor_scalar(v[:, t, :, 0:HD], tmp[:, 1, 0:D].rearrange("p (h e) -> p h e", e=HD),
                                      order_exp[:, t % TPS:t % TPS + 1], None, ALU.mult)
                    dve.tensor_copy(v[:, t, :, HD], order_exp[:, t % TPS:t % TPS + 1].to_broadcast([P, H]))
                elif n == 1:
                    dve.tensor_copy(v[:, t, :, 0:HD], vb[:, 0:D].rearrange("p (h e) -> p h e", e=HD))
                    dve.tensor_copy(logits[:, t, 0:8], vb[:, D:D + 8]).then_inc(s["v_copied"], 1)
                else:
                    dve.tensor_copy(v[:, t, 0:4, 0:HD], vb[:, 0:64].rearrange("p (h e) -> p h e", e=HD))
                    dve.tensor_tensor(logits[:, t, 0:8], vb[:, D:D + 8], rbias[:], ALU.add).then_inc(s["v_copied"], 1)
            if n == 2:
                dve.memset(v[:, :, 0:4, HD:VW], 1.0)

        def scalar_project(act, n):
            s, at = LS, AT[n]

            def out_T(t):
                act.wait_ge(s["qk_T"], at["qk_T"] + t + 1)
                src = bank[4 + t % 2][:].rearrange("p (q t) -> p q t", t=P)
                act.activation(qT[:, :, t * P:(t + 1) * P], src[:, 0:NG, :], ACT.Copy)
                act.activation(kT[:, :, t * P:(t + 1) * P], src[:, NG:, :], ACT.Copy)
                act.drain().then_inc(s["qk_copied"], 1)

            for t in range(NT):
                if n == 1:
                    act.wait_ge(s["qk_ready"], at["qk_ready"] + t + 1)
                    if t >= 2:
                        act.wait_ge(s["qk_tok"], at["qk_tok"] + t - 1)
                    act.activation(th[:, t % 2, :], bank[t % 2][:], ACT.Tanh, scale=0.5).then_inc(silu_tanh, 1)
                    if t:
                        out_T(t - 1)
                else:
                    out_T(t)
            if n == 1:
                out_T(NT - 1)

        silu_tanh = sem("silu_tanh")
        knorm = sb("knorm", [P, NT, H])
        kd = part(1, [P, NT, D])
        order_exp = sb("order_exp", [P, TPS])

        def tensor_out(pe, n):
            s, at = LS, AT[n]
            for t in range(NT):
                if t >= 2:
                    pe.wait_ge(s["aoT_ready"], at["aoT_ready"] + t - 1)
                for k in range(KD):
                    last = nc.tensor.transpose(bank[t % 2][:, k * P:(k + 1) * P], ao[:, t, k * P:(k + 1) * P], ident[:])
                last.then_inc(s["ao_T"], 1)
                if t:
                    tensor_out_product(pe, n, t - 1)
            tensor_out_product(pe, n, NT - 1)

        def tensor_out_product(pe, n, t):
            s, at = LS, AT[n]
            pe.wait_ge(s["aoT_ready"], at["aoT_ready"] + t + 1)
            if t >= 2:
                pe.wait_ge(s["o_added"], at["o_added"] + t - 1)
            for k in range(KD):
                last = mm(bank[2 + t % 2][:, 0:D], aoT[:, k, t * P:(t + 1) * P], wo[n][:, k, :], k == 0, k == KD - 1)
            last.then_inc(s["o_ready"], 1)

        def scalar_out(act, n):
            s, at = LS, AT[n]
            for t in range(NT):
                act.wait_ge(s["ao_T"], at["ao_T"] + t + 1)
                act.activation(aoT[:, :, t * P:(t + 1) * P], bank[t % 2][:, 0:D].rearrange("p (k t) -> p k t", k=KD),
                               ACT.Copy).then_inc(s["aoT_ready"], 1)

        def vector_out(dve, n):
            s, at = LS, AT[n]
            if n == 0:
                dve.tensor_tensor(x[:], x[:], bo[:].unsqueeze(1).to_broadcast([P, NT, D]), ALU.add)
                dve.drain()
            for t in range(NT):
                dve.wait_ge(s["o_ready"], at["o_ready"] + t + 1)
                dve.tensor_tensor(x[:, t, :], x[:, t, :], bank[2 + t % 2][:, 0:D], ALU.add).then_inc(s["o_added"], 1)

        qm = [part(0, [P, S]) for i in range(2)]
        eA = part(0, [P, 2, S])
        eP = [part(0, [P, S]) for i in range(2)]
        eT = [part(0, [P, S]) for i in range(2)]
        row8 = sb("row8", [P, 3, 8])
        nbias = sb("nbias", [P, 2, 2])
        cpair = sb("cpair", [P, 2, 2])
        neg_max = sb("neg_max", [P, NT, H])
        sum_exp = sb("sum_exp", [P, NT, H])
        sum_es = sb("sum_es", [P, NT, H])
        sum_diff = sb("sum_diff", [P, NT, H])
        sum_s = sb("sum_s", [P, NT, H])
        AS = {k: sem(k) for k in ("qm_ready", "score_ready", "diff_ready", "bias_ready",
                                               "expP_ready", "scores_summed", "diff_read",
                                               "mean_read", "turned", "eT_ready", "head_ready", "head_copied")}
        UNITS = H * B * TPS
        HEADS_AT = [dict.fromkeys(AS, 0), None,
                    {k: H * B if k in ("qm_ready", "head_ready", "head_copied") else UNITS for k in AS}]

        def head_loops(eng, body):
            with eng.Fori(0, B) as b:
                with eng.Fori(0, NG) as g:
                    with eng.Fori(0, GH // 2) as hp:
                        body(b, g, hp, b * (NG * GH // 2) + g * (GH // 2) + hp)

        def tensor_heads(pe, n):
            s, at = AS, HEADS_AT[n]

            def body(b, g, hp, i):
                def score(u):
                    hh, j = u // TPS, u % TPS
                    if j == 0:
                        pe.wait_ge(s["qm_ready"], at["qm_ready"] + i * 2 + hh + 1)
                    w = S if n == 0 else (j + 1) * P
                    q = qm[hh][:, j * P:(j + 1) * P]
                    pe.wait_ge(s["expP_ready"], at["expP_ready"] + i * 8 + u + 1)
                    if n == 0:
                        pe.wait_ge(s["scores_summed"], at["scores_summed"] + i * 8 + u + 1)
                    last = mm(bank[u % 2][:, 0:w], q, kT[:, bass.ds(g, 1), bass.ds(b * S, w)], True, n == 0)
                    if n == 2:
                        last = mm(bank[u % 2][:, j * P:w], ident[:], causal[:], False, True)
                    last.then_inc(s["score_ready"], 1)
                    if n == 0:
                        pe.wait_ge(s["diff_read"], at["diff_read"] + i * 8 + u + 1)
                        pe.wait_ge(s["mean_read"], at["mean_read"] + i * 8 + u + 1)
                        last = mm(bank[2 + u % 2][:], q, kdT[:, bass.ds(g, 1), bass.ds(b * S, S)])
                        last.then_inc(s["diff_ready"], 1)

                def turn(u):
                    j = u % TPS
                    pe.wait_ge(s["expP_ready"], at["expP_ready"] + i * 8 + u + 3)
                    pe.wait_ge(s["eT_ready"], at["eT_ready"] + i * 8 + u + 1)
                    for c in range(TPS if n == 0 else j + 1):
                        last = nc.tensor.transpose(bank[4 + u % 2][:, c * P:(c + 1) * P],
                                                   eP[u % 2][:, c * P:(c + 1) * P], ident[:])
                    last.then_inc(s["turned"], 1)

                def weigh(u):
                    hh, j = u // TPS, u % TPS
                    pe.wait_ge(s["eT_ready"], at["eT_ready"] + i * 8 + u + 3)
                    if j == 0:
                        pe.wait_ge(s["head_copied"], at["head_copied"] + i * 2 + hh + 1)
                    last_c = TPS - 1 if n == 0 else j
                    for c in range(last_c + 1):
                        head = g * GH + hp * 2 + hh if n == 0 else g * 2 + hp // 2
                        last = mm(bank[6 + hh][:, j * VW:(j + 1) * VW], eT[u % 2][:, c * P:(c + 1) * P],
                                  v[:, bass.ds(b * TPS + c, 1), bass.ds(head, 1), :], c == 0, c == last_c)
                    if j == TPS - 1:
                        last.then_inc(s["head_ready"], 1)

                U = 2 * TPS
                for u in range(U + 2):
                    if u < U:
                        score(u)
                    if 1 <= u <= U:
                        turn(u - 1)
                    if u >= 2:
                        weigh(u - 2)

            head_loops(pe, body)

        def scalar_heads(act, n):
            s, at = AS, HEADS_AT[n]
            if n == 0:
                act.drain().then_inc(s["expP_ready"], 2)
            if n == 0:
                act.drain().then_inc(s["diff_read"], 2)

            def body(b, g, hp, i):
                for u in range(2 * TPS):
                    hh, j = u // TPS, u % TPS
                    w = S if n == 0 else (j + 1) * P
                    row = b * TPS + j
                    head = g * GH + hp * 2 + hh
                    act.wait_ge(s["bias_ready"], at["bias_ready"] + i * 8 + u + 1)
                    if n == 0:
                        act.activation(eA[:, u % 2, :], bank[u % 2][:], ACT.Exp, bias=nbias[:, u % 2, 0:1],
                                       scale=HD ** -0.5,
                                       accum_out=sum_exp[:, bass.ds(row, 1), bass.ds(head, 1)])
                    act.wait_ge(s["turned"], at["turned"] + i * 8 + u + 1)
                    act.activation(eP[u % 2][:, 0:w], bank[u % 2][:, 0:w], ACT.Exp, bias=nbias[:, u % 2, 1:2],
                                   scale=cpair[:, n // 2, 1:2]).then_inc(s["expP_ready"], 1)
                    if n == 0:
                        act.wait_ge(s["mean_read"], at["mean_read"] + i * 8 + u + 3)
                        act.activation(bank[2 + u % 2][:, 0:S - 1], bank[2 + u % 2][:, 0:S - 1], ACT.Abs,
                                       accum_out=sum_diff[:, bass.ds(row, 1), bass.ds(head, 1)]).then_inc(s["diff_read"], 1)

            head_loops(act, body)

        def vector_heads(dve, n):
            s, at = AS, HEADS_AT[n]
            if n == 0:
                dve.drain().then_inc(s["scores_summed"], 2)
                dve.drain().then_inc(s["mean_read"], 2)
            if n == 0:
                dve.drain().then_inc(s["head_copied"], 2)
            if n == 0:
                dve.drain().then_inc(s["eT_ready"], 2)

            def body(b, g, hp, i):
                def mask(hh):
                    dve.tensor_scalar(qm[hh][:], qT[:, bass.ds(g, 1), bass.ds(b * S, S)],
                                      head_mask[:, bass.ds(hp * 2 + hh, 1)], None, ALU.mult).then_inc(s["qm_ready"], 1)

                def maximum(u):
                    hh, j = u // TPS, u % TPS
                    w = S if n == 0 else (j + 1) * P
                    dve.wait_ge(s["score_ready"], at["score_ready"] + i * 8 + u + 1)
                    dve.tensor_reduce(row8[:, 0, u:u + 1], bank[u % 2][:, 0:w], AX.X, ALU.max, negate=True)
                    dve.drain()
                    dve.tensor_tensor(nbias[:, u % 2, :], row8[:, 0, u:u + 1].to_broadcast([P, 2]),
                                      cpair[:, n // 2, :], ALU.mult).then_inc(s["bias_ready"], 1)
                    if n == 0:
                        dve.wait_ge(s["diff_ready"], at["diff_ready"] + i * 8 + u + 1)
                        dve.tensor_copy(row8[:, 2, u:u + 1], bank[2 + u % 2][:, S - 1:S]).then_inc(s["mean_read"], 1)

                def entropy(u):
                    hh, j = u // TPS, u % TPS
                    dve.wait_ge(s["expP_ready"], at["expP_ready"] + i * 8 + u + 3)
                    dve.tensor_tensor_reduce(eA[:, u % 2, :], eA[:, u % 2, :], bank[u % 2][:], 1.0, 0.0, ALU.mult, ALU.add,
                                             row8[:, 1, u:u + 1]
                                             ).then_inc(s["scores_summed"], 1)

                def copy_T(u):
                    j = u % TPS
                    w = S if n == 0 else (j + 1) * P
                    dve.wait_ge(s["turned"], at["turned"] + i * 8 + u + 3)
                    dve.tensor_copy(eT[u % 2][:, 0:w], bank[4 + u % 2][:, 0:w]).then_inc(s["eT_ready"], 1)

                def copy_head(hh):
                    dve.wait_ge(s["head_ready"], at["head_ready"] + i * 2 + hh + 1)
                    dve.tensor_copy(raw[:, bass.ds(b * TPS, TPS), bass.ds(g * GH + hp * 2 + hh, 1), :],
                                    bank[6 + hh][:, 0:TPS * VW].rearrange("p (j o e) -> p j o e", o=1, e=VW)
                                    ).then_inc(s["head_copied"], 1)

                for hh in range(2):
                    mask(hh)
                for u in range(2 * TPS + 2):
                    if u < 2 * TPS:
                        maximum(u)
                    if n == 0 and 1 <= u <= 2 * TPS:
                        entropy(u - 1)
                    if 2 <= u:
                        copy_T(u - 2)
                    if u == TPS + 3:
                        copy_head(0)
                copy_head(1)
                if n == 0:
                    dve.drain()
                    for q, stat in enumerate((neg_max, sum_es, sum_s)):
                        dve.tensor_copy(stat[:, bass.ds(b * TPS, TPS), bass.ds(g * GH + hp * 2, 2)],
                                        row8[:, q, :].rearrange("p (h j) -> p j h", j=TPS))

            if n == 0:
                dve.drain().then_inc(s["turned"], 2)
            head_loops(dve, body)

        rowc = sb("rowc", [P, NT, H])
        rowt = sb("rowt", [P, NT, H])
        rowu = sb("rowu", [P, NT, H])
        lnz = sb("lnz", [P, NT, H])
        rfac = sb("rfac", [P, NT, H])
        half_pos = sb("half_pos", [P, NT * H])
        zeros = sb("zeros", [P, 1])
        lnz_ready = sem("lnz_ready")
        kn_ready = sem("kn_ready")
        row_ready = sem("row_ready")
        fac_ready = sem("fac_ready")
        gate_exp = sem("gate_exp")
        gates_ready = sem("gates_ready")
        order_ready = sem("order_ready")
        order_pos = sb("order_pos", [P, TPS])
        gt = sb("gt", [P, 16])

        def scalar_gates(act):
            act.wait_ge(loaded[0], LOADS[0])
            act.activation(gt[:, 0:5], gates[:], ACT.Exp, scale=-1.0).then_inc(gate_exp, 1)
            act.wait_ge(gates_ready, 1)
            act.activation(order_exp[:], order_pos[:], ACT.Exp, scale=gt[:, 7:8]).then_inc(order_ready, 1)

        def vector_gates(dve):
            dve.wait_ge(gate_exp, 1)
            dve.tensor_scalar(gt[:, 0:5], gt[:, 0:5], 1.0, None, ALU.add)
            dve.drain()
            dve.reciprocal(gt[:, 5:10], gt[:, 0:5])
            dve.drain()
            dve.tensor_scalar(cpair[:, 0, 1:2], gt[:, 8:9], -0.1 * HD ** -0.5, HD ** -0.5, ALU.mult, ALU.add)
            dve.memset(cpair[:, 0, 0:1], HD ** -0.5)
            dve.memset(cpair[:, 1, :], HD ** -0.5)
            dve.memset(half_neg[:], -0.5)
            dve.memset(half_pos[:], 0.5)
            dve.memset(comb[:], 0.0)
            dve.tensor_copy(identb[:], ident[:])
            dve.drain().then_inc(gates_ready, 1)
            dve.wait_ge(order_ready, 1)

        def vector_diffs(dve):
            for g in range(NG):
                for b in range(B):
                    o = b * S
                    dve.tensor_tensor(kdT[:, g, o:o + S - 1], kT[:, g, o + 1:o + S], kT[:, g, o:o + S - 1], ALU.subtract)
                    dve.tensor_reduce(kdT[:, g, o + S - 1:o + S], kT[:, g, o:o + S], AX.X, ALU.add)

        def pool_rows(pool):
            pool.tensor_tensor(knorm[:].rearrange("p t h -> p (t h)"), knorm[:].rearrange("p t h -> p (t h)"),
                               half_pos[:], ALU.pow).then_inc(kn_ready, 1)

        def scalar_rows(act):
            act.activation(lnz[:], sum_exp[:], ACT.Ln).then_inc(lnz_ready, 1)
            act.wait_ge(row_ready, 1)
            act.activation(rfac[:], rowt[:], ACT.Exp).then_inc(fac_ready, 1)

        def vector_rows(dve):
            isq = HD ** -0.5
            dve.reciprocal(rowu[:], sum_exp[:])
            dve.drain()
            dve.tensor_tensor(rowu[:], rowu[:], sum_es[:], ALU.mult)
            dve.drain()
            dve.tensor_tensor(rowu[:], rowu[:], neg_max[:], ALU.add)
            dve.wait_ge(lnz_ready, 1)
            dve.drain()
            dve.tensor_scalar(rowu[:], rowu[:], isq, None, ALU.mult)
            dve.drain()
            dve.tensor_tensor(rowu[:], rowu[:], lnz[:], ALU.subtract)
            dve.drain()
            dve.tensor_scalar(rowu[:], rowu[:], gt[:, 6:7], -0.1 / LN_S, ALU.mult, ALU.mult)
            dve.wait_ge(kn_ready, 1)
            dve.tensor_scalar(rowt[:], knorm[:], gt[:, 5:6], -0.01, ALU.mult, ALU.mult)
            dve.drain()
            dve.tensor_tensor(rowc[:], rowu[:], rowt[:], ALU.add)
            dve.drain()
            dve.tensor_scalar(rowu[:], sum_s[:], gt[:, 8:9], 0.1 * isq / S, ALU.mult, ALU.mult)
            dve.drain()
            dve.tensor_tensor(rowc[:], rowc[:], rowu[:], ALU.add)
            dve.drain()
            dve.tensor_scalar(rowt[:], sum_diff[:], gt[:, 9:10], -0.1 * isq / (S - 1), ALU.mult, ALU.mult)
            dve.drain()
            dve.tensor_tensor(rowc[:], rowc[:], rowt[:], ALU.add)
            dve.drain()
            dve.tensor_scalar(rowu[:], neg_max[:], cpair[:, 0, 1:2], -1.0, ALU.mult, ALU.mult)
            dve.drain()
            dve.tensor_tensor(lnz[:], rowc[:], rowu[:], ALU.add)
            dve.drain()
            dve.tensor_tensor(rowt[:], rowc[:], lnz[:], ALU.subtract)
            dve.drain()
            dve.tensor_tensor(rowt[:], rowt[:], rowu[:], ALU.add).then_inc(row_ready, 1)
            dve.wait_ge(fac_ready, 1)
            for t in range(NT):
                dve.tensor_tensor(raw[:, t, :, :], raw[:, t, :, :], rfac[:, t, :].unsqueeze(2).to_broadcast([P, H, VW]),
                                  ALU.mult)
            dve.drain()
            vector_divide(dve)

        def vector_divide(dve):
            dve.reciprocal(rowu[:], raw[:, :, :, HD])
            dve.drain()
            for t in range(NT):
                dve.tensor_tensor(ao[:, t, :].rearrange("p (h e) -> p h e", e=HD), raw[:, t, :, 0:HD],
                                  rowu[:, t, :].unsqueeze(2).to_broadcast([P, H, HD]), ALU.mult)

        qx = part(1, [P, 2, GH, P])
        sD = [part(1, [P, 4 * P]) for i in range(4)]
        state = part(1, [P, NG, P])
        stmp = part(1, [P, NG, P])
        g1T = part(1, [P, TOK])[0:HD, :]
        gsig = part(1, [P, 2, D])
        ms = sb("ms", [P, NT, H])
        L1 = {k: sem(f"lin_{k}") for k in ("g1_ready", "g1_copied", "qx_ready", "qx_used", "sc_ready", "sc_masked",
                                            "own_ready", "own_read", "st_ready", "st_done", "gate_ready", "gate_th",
                                            "gate_read", "ms_ready", "ms_root")}

        def tensor_linear(pe):
            s = L1
            for c in range(2):
                for k in range(KD):
                    last = mm(bank[c][0:HD, :], wg1[:, k, :], xnT[:, k, c * 512:(c + 1) * 512], k == 0, k == KD - 1)
                last.then_inc(s["g1_ready"], 1)
            pe.wait_ge(s["g1_copied"], 2)
            for t in range(NT):
                first = t % TPS == 0
                ts = slice(t * P, (t + 1) * P)
                if t:
                    pe.wait_ge(s["gate_read"], t)
                mm(bank[7][:, 0:D], g1T[:, ts], wg2[:]).then_inc(s["gate_ready"], 1)
                for g in range(NG):
                    pe.wait_ge(s["qx_ready"], t * NG + g + 1)
                    if t:
                        pe.wait_ge(s["sc_masked"], 2 * ((t - 1) * NG + g + 1))
                    for c in range(2):
                        last = mm(bank[2 * g + c][:], kT[:, g, ts],
                                  qx[:, g, 4 * c:4 * c + 4, :].rearrange("p h t -> p (h t)"))
                    last.then_inc(s["sc_ready"], 1)
                if t:
                    pe.wait_ge(s["own_read"], t)
                if not first:
                    pe.wait_ge(s["st_done"], t)
                    for g in range(NG):
                        mm(bank[5][:, g * P:(g + 1) * P], qT[:, g, ts], state[:, g, :])
                for g in range(NG):
                    pe.wait_ge(s["sc_masked"], 2 * (t * NG + g + 1))
                    for hh in range(GH):
                        h = g * GH + hh
                        last = mm(bank[4][:, h * HD:(h + 1) * HD], sD[2 * g + hh // 4][:, (hh % 4) * P:(hh % 4 + 1) * P],
                                  v[:, t, h, 0:HD])
                last.then_inc(s["own_ready"], 1)
                if t:
                    pe.wait_ge(s["st_done"], t)
                for g in range(NG):
                    last = mm(bank[6][:, g * P:(g + 1) * P], kd[:, t, g * P:(g + 1) * P], v[:, t, g * GH:(g + 1) * GH, 0:HD])
                last.then_inc(s["st_ready"], 1)

        def scalar_linear(act):
            s = L1
            for c in range(2):
                act.wait_ge(s["g1_ready"], c + 1)
                act.activation(g1T[:, c * 512:(c + 1) * 512], bank[c][0:HD, :], ACT.Copy).then_inc(s["g1_copied"], 1)
            for t in range(NT):
                act.wait_ge(s["gate_ready"], t + 1)
                if t >= 2:
                    act.wait_ge(s["own_read"], t - 1)
                act.activation(gsig[:, t % 2, :], bank[7][:, 0:D], ACT.Tanh, scale=0.5).then_inc(s["gate_read"], 1)

        def vector_linear(dve):
            s = L1
            for t in range(NT):
                first = t % TPS == 0
                ts = slice(t * P, (t + 1) * P)
                for g in range(NG):
                    if t:
                        dve.wait_ge(s["sc_ready"], (t - 1) * NG + g + 1)
                    dve.tensor_tensor(qx[:, g, :, :], qT[:, g, ts].unsqueeze(1).to_broadcast([P, GH, P]),
                                      head_mask[:].unsqueeze(2).to_broadcast([P, GH, P]), ALU.mult
                                      ).then_inc(s["qx_ready"], 1)
                if t:
                    dve.wait_ge(s["own_ready"], t)
                for g in range(NG):
                    dve.wait_ge(s["sc_ready"], t * NG + g + 1)
                    for c in range(2):
                        h = g * GH + 4 * c
                        dve.tensor_tensor(sD[2 * g + c][:], bank[2 * g + c][:],
                                          decay[:, h:h + 4, :].rearrange("p h t -> p (h t)"), ALU.mult
                                          ).then_inc(s["sc_masked"], 1)
                dve.wait_ge(s["st_ready"], t + 1)
                new = bank[6][:, 0:D].rearrange("p (g e) -> p g e", g=NG)
                dve.tensor_tensor(stmp[:], new, own_block[:].unsqueeze(1).to_broadcast([P, NG, P]), ALU.mult)
                if first:
                    dve.drain()
                    dve.tensor_copy(state[:], stmp[:]).then_inc(s["st_done"], 1)
                else:
                    dve.tensor_tensor(state[:], state[:], lam_chunk[:], ALU.mult)
                    dve.drain()
                    dve.tensor_tensor(state[:], state[:], stmp[:], ALU.add).then_inc(s["st_done"], 1)
                dve.wait_ge(s["own_ready"], t + 1)
                o = ao[:, t, :].rearrange("p (h e) -> p h e", e=HD)
                if first:
                    dve.tensor_copy(ao[:, t, :], bank[4][:, 0:D])
                else:
                    dve.tensor_tensor(o, bank[5][:, 0:D].rearrange("p (h e) -> p h e", e=HD),
                                      decay_q[:].unsqueeze(2).to_broadcast([P, H, HD]), ALU.mult)
                    dve.drain()
                    dve.tensor_tensor(ao[:, t, :], ao[:, t, :], bank[4][:, 0:D], ALU.add)
                dve.drain()
                dve.wait_ge(s["gate_read"], t + 1)
                dve.scalar_tensor_tensor(ao[:, t, :], gsig[:, t % 2, :], 1.0, ao[:, t, :], ALU.add, ALU.mult
                                         ).then_inc(s["own_read"], 1)
                dve.drain()
                dve.tensor_tensor(tmp[:, 0, 0:D], ao[:, t, :], ao[:, t, :], ALU.mult)
                dve.drain()
                dve.tensor_reduce(ms[:, t, :], tmp[:, 0, 0:D].rearrange("p (h e) -> p h e", e=HD), AX.X, ALU.add)
            dve.drain()
            dve.tensor_scalar(ms[:], ms[:], 0.25 / HD, 1e-6, ALU.mult, ALU.add).then_inc(s["ms_ready"], 1)
            dve.wait_ge(s["ms_root"], 1)
            for t in range(NT):
                o = ao[:, t, :].rearrange("p (h e) -> p h e", e=HD)
                dve.tensor_tensor(o, o, ms[:, t, :].unsqueeze(2).to_broadcast([P, H, HD]), ALU.mult)
            dve.drain()
            for t in range(NT):
                dve.scalar_tensor_tensor(ao[:, t, :], ao[:, t, :], 0.5, norm_w[:], ALU.mult, ALU.mult)

        def pool_linear(pool):
            pool.wait_ge(L1["ms_ready"], 1)
            pool.tensor_tensor(ms[:].rearrange("p t h -> p (t h)"), ms[:].rearrange("p t h -> p (t h)"), half_neg[:],
                               ALU.pow).then_inc(L1["ms_root"], 1)

        def vector_route(dve, n):
            s, at = LS, AT[n]
            E = EXPERTS[n]
            if n == 3:
                for t in range(NT):
                    dve.wait_ge(s["logits_ready"], at["logits_ready"] + t + 1)
                    dve.tensor_copy(logits[:, t, 0:16], bank[t % 2][:, 0:16])
                    dve.tensor_copy(shared[:, t:t + 1], bank[t % 2][:, 16:17])
                    dve.drain().then_inc(s["logits_copied"], 1)
            lg, pr, cm = logits[:, :, 0:E], probs[:, :, 0:E], comb[:, :, 0:E]

            def wide(r):
                return r[:].unsqueeze(2).to_broadcast([P, NT, E])

            dve.drain()
            dve.tensor_reduce(rowm[:], lg, AX.X, ALU.max)
            dve.drain()
            dve.tensor_tensor(pr, lg, wide(rowm), ALU.subtract)
            dve.drain().then_inc(s["route_exp"], 1)
            dve.wait_ge(s["route_exp"], at["route_exp"] + 2)
            if n != 2:
                dve.tensor_reduce(rowz[:], pr, AX.X, ALU.add)
                dve.drain()
                dve.reciprocal(rowz[:], rowz[:])
                dve.drain()
                dve.tensor_tensor(pr, pr, wide(rowz), ALU.mult)
                dve.drain()
            key = lg if n == 2 else pr
            for t in range(NT):
                ahead = key[:, t, :].unsqueeze(1).to_broadcast([P, E, E])
                own = key[:, t, :].unsqueeze(2).to_broadcast([P, E, E])
                dve.tensor_tensor(rank[:, 0:E, 0:E], ahead, own, ALU.is_gt)
                dve.tensor_tensor(rank2[:, 0:E, 0:E], ahead, own, ALU.is_equal)
                dve.drain()
                dve.tensor_tensor(rank2[:, 0:E, 0:E], rank2[:, 0:E, 0:E], lower[:, 0:E, 0:E], ALU.mult)
                dve.drain()
                dve.tensor_tensor(rank[:, 0:E, 0:E], rank[:, 0:E, 0:E], rank2[:, 0:E, 0:E], ALU.add)
                dve.drain()
                dve.tensor_reduce(rankn[:, t, 0:E], rank[:, 0:E, 0:E], AX.X, ALU.add)
                dve.drain()
            dve.tensor_scalar(rankn[:, :, 0:E], rankn[:, :, 0:E], float(TOPK[n]), None, ALU.is_lt)
            dve.drain()
            dve.tensor_tensor(cm, rankn[:, :, 0:E], pr, ALU.mult)
            dve.drain()
            if n != 1:
                dve.tensor_reduce(rowz[:], cm, AX.X, ALU.add)
                dve.drain()
                dve.reciprocal(rowz[:], rowz[:])
                dve.drain()
                dve.tensor_tensor(cm, cm, wide(rowz), ALU.mult)
                dve.drain()
            dve.tensor_scalar(cm, cm, 0.5, None, ALU.mult)
            if n == 1:
                dve.memset(comb[:, :, E:E + 1], 0.5)
            if n == 2:
                dve.memset(comb[:, :, E:E + 1], 0.0)
            if n == 3:
                dve.tensor_scalar(comb[:, :, E], shared[:], 1.0, 0.25, ALU.add, ALU.mult)
            dve.drain()
            hi, mid, lo = (combp[:, :, i * NE:(i + 1) * NE] for i in range(3))
            rest = rank[:].rearrange("p a b -> p (a b)")[:, 0:NT * NE].rearrange("p (t e) -> p t e", e=NE)
            dve.tensor_copy(hi, comb[:])
            dve.drain()
            dve.tensor_tensor(rest, comb[:], hi, ALU.subtract)
            dve.drain()
            dve.tensor_copy(mid, rest)
            dve.drain()
            dve.tensor_tensor(lo, rest, mid, ALU.subtract)
            dve.drain().then_inc(s["comb_T"], 1)
            dve.wait_ge(s["comb_T"], at["comb_T"] + 2)
            dve.tensor_copy(combT[:], bankb)
            if n == 2:
                dve.wait_ge(s["comb_T"], at["comb_T"] + 3)
                dve.tensor_copy(combF[0:8, :], bank[6][0:8, :])
                dve.tensor_copy(combF2[0:8, :], bank[7][0:8, :])
                dve.drain()

        bankb = bank[5][0:CR, :].bitcast(BF16)
        combF = sb("combF", [8, 512])
        combF2 = sb("combF2", [8, 512])

        def scalar_route(act, n):
            s, at = LS, AT[n]
            E = EXPERTS[n]
            act.wait_ge(s["route_exp"], at["route_exp"] + 1)
            act.activation(probs[:, :, 0:E], probs[:, :, 0:E], ACT.Exp)
            if n == 3:
                act.activation(shared[:], shared[:], ACT.Tanh, scale=0.5)
            act.drain().then_inc(s["route_exp"], 1)

        def tensor_route(pe, n):
            s, at = LS, AT[n]
            if n == 3:
                for t in range(NT):
                    if t >= 2:
                        pe.wait_ge(s["logits_copied"], at["logits_copied"] + t - 1)
                    for k in range(KD):
                        last = mm(bank[t % 2][:, 0:NE], xnT[:, k, t * P:(t + 1) * P], router[3][:, k, :],
                                  k == 0, k == KD - 1)
                    last.then_inc(s["logits_ready"], 1)
            pe.wait_ge(s["comb_T"], at["comb_T"] + 1)
            for t in range(NT):
                last = nc.tensor.transpose(bankb[:, t * P:(t + 1) * P], combp[:, t, :], identb[:])
            last.then_inc(s["comb_T"], 1)
            if n == 2:
                for t in range(NT):
                    last = nc.tensor.transpose(bank[6 + t // 4][0:8, (t % 4) * P:(t % 4 + 1) * P], comb[:, t, 0:8], ident[:])
                last.then_inc(s["comb_T"], 1)

        GB, UB, CB, DB = 4, 5, 6, 7

        def sync_ffn(sp, n, first, count):
            s, at = LS, AT[n]
            base = sum(CHUNKS[:n])
            with sp.Fori(first, first + count) as p:
                sp.wait_ge(s["guA_used"], at["guA_used"] + p + 1)
                sp.dma_start(wgu[0][:], a["gu"][bass.ds(p * 2 + base, 1), :, :].rearrange("a p n -> (a p) n")).then_inc(s["guA_loaded"], 16)
                if n:
                    sp.dma_start(sel[0][:], a[f"sel{n}"][bass.ds(p * 2, 1), :, :].rearrange("a p n -> (a p) n")).then_inc(s["guA_loaded"], 16)
                sp.wait_ge(s["guB_used"], at["guB_used"] + p + 1)
                sp.dma_start(wgu[1][:], a["gu"][bass.ds(p * 2 + base + 1, 1), :, :].rearrange("a p n -> (a p) n")).then_inc(s["guB_loaded"], 16)
                if n:
                    sp.dma_start(sel[1][:], a[f"sel{n}"][bass.ds(p * 2 + 1, 1), :, :].rearrange("a p n -> (a p) n")).then_inc(s["guB_loaded"], 16)
                sp.wait_ge(s["down_used"], at["down_used"] + p + 1)
                sp.dma_start(wd[:], a["down"][bass.ds(p * 2 + base, 2), :, :].rearrange("a p n -> p a n")).then_inc(s["down_loaded"], 16)

        def tensor_ffn_start(pe, n):
            s, at = LS, AT[n]
            if n == 0:
                for k in ("guA_used", "guB_used", "down_used"):
                    pe.drain().then_inc(s[k], 1)

        def tensor_ffn_pair(pe, n, p):
            s, at = LS, AT[n]
            inc = 32 if n else 16

            def gate_up(u):
                half, c = u // 2, u % 2
                if half == 0:
                    pe.wait_ge(s["guB_loaded" if c else "guA_loaded"], at["guA_loaded"] + p * inc + inc)
                ts = slice(half * 512, half * 512 + 512)
                pe.wait_ge(s["gate_used"], at["gate_used"] + p * 4 + u + 1)
                for k in range(KD):
                    last = mm(bank[GB][:], wgu[c][:, k * P:(k + 1) * P], xnT[:, k, ts], k == 0, k == KD - 1)
                last.then_inc(s["gate_ready"], 1)
                pe.wait_ge(s["up_used"], at["up_used"] + p * 4 + u + 1)
                for k in range(KD):
                    last = mm(bank[UB][:], wgu[c][:, (2 + k) * P:(3 + k) * P], xnT[:, k, ts], k == 0, k == KD - 1)
                last.then_inc(s["up_ready"], 1)
                if n:
                    pe.wait_ge(s["comb_used"], at["comb_used"] + p * 4 + u + 1)
                    last = mm(bank[CB][:], sel[c][:], combT[:, ts])
                    last.then_inc(s["comb_ready"], 1)
                if half == 1:
                    pe.drain().then_inc(s["guB_used" if c else "guA_used"], 1)

            def down(half):
                if half == 0:
                    pe.wait_ge(s["down_loaded"], at["down_loaded"] + p * 16 + 16)
                pe.wait_ge(s["h_ready"], at["h_ready"] + p * 4 + 2 * half + 2)
                for q in range(2):
                    pe.wait_ge(s["part_added"], at["part_added"] + p * 4 + 2 * half + q + 1)
                    for r in range(2):
                        t = 2 * q + r
                        for c in range(2):
                            last = mm(bank[DB][:, r * D:(r + 1) * D], hT[:, 2 * half + c, t * P:(t + 1) * P], wd[:, c, :],
                                      c == 0, c == 1)
                    last.then_inc(s["part_ready"], 1)

            gate_up(0)
            gate_up(1)
            gate_up(2)
            down(0)
            gate_up(3)
            down(1)
            pe.drain().then_inc(s["down_used"], 1)

        def scalar_ffn_pair(act, n, p):
            s, at = LS, AT[n]
            for u in range(4):
                if n == 2:
                    act.wait_ge(s["gate_clipped"], at["gate_clipped"] + p * 4 + u + 1)
                    act.activation(th[:, u % 2, :], gl[:, u % 2, :], ACT.Tanh, scale=0.5 * 1.702).then_inc(s["tanh_ready"], 1)
                else:
                    act.wait_ge(s["gate_ready"], at["gate_ready"] + p * 4 + u + 1)
                    act.wait_ge(s["gate_used"], at["gate_used"] + p * 4 + u + 1)
                    act.activation(th[:, u % 2, :], bank[GB][:], ACT.Tanh, scale=0.5).then_inc(s["tanh_ready"], 1)

        def vector_ffn_start(dve, n):
            s, at = LS, AT[n]
            if n == 0:
                for k in ("gate_used", "up_used", "part_added", "comb_used"):
                    dve.drain().then_inc(s[k], 1)

        def vector_ffn_pair(dve, n, p):
            s, at = LS, AT[n]

            def unit(u):
                i = u % 2
                h = hT[:, u, :]
                if n == 2:
                    bias = [gu_bias[:, bass.ds(p * 2 + u % 2, 1), c:c + 1] for c in (0, 1)]
                    dve.wait_ge(s["gate_ready"], at["gate_ready"] + p * 4 + u + 1)
                    dve.tensor_scalar(gl[:, i, :], bank[GB][:], bias[0], 7.0, ALU.add, ALU.min)
                    dve.drain().then_inc(s["gate_clipped"], 1)
                    dve.wait_ge(s["up_ready"], at["up_ready"] + p * 4 + u + 1)
                    dve.tensor_scalar(up[:, i, :], bank[UB][:], bias[1], 7.0, ALU.add, ALU.min)
                    dve.drain().then_inc(s["up_used"], 1)
                    dve.tensor_scalar(up[:, i, :], up[:, i, :], -7.0, 1.0, ALU.max, ALU.add)
                    dve.wait_ge(s["tanh_ready"], at["tanh_ready"] + p * 4 + u + 1)
                    dve.scalar_tensor_tensor(gl[:, i, :], th[:, i, :], 1.0, gl[:, i, :], ALU.add, ALU.mult)
                    dve.drain().then_inc(s["gate_used"], 1)
                    dve.tensor_tensor(gl[:, i, :], gl[:, i, :], up[:, i, :], ALU.mult)
                    dve.drain()
                else:
                    dve.wait_ge(s["tanh_ready"], at["tanh_ready"] + p * 4 + u + 1)
                    dve.scalar_tensor_tensor(gl[:, i, :], th[:, i, :], 1.0, bank[GB][:], ALU.add, ALU.mult
                                             ).then_inc(s["gate_used"], 1)
                    dve.drain()
                    dve.wait_ge(s["up_ready"], at["up_ready"] + p * 4 + u + 1)
                    if n == 0:
                        dve.scalar_tensor_tensor(h, gl[:, i, :], 0.5, bank[UB][:], ALU.mult, ALU.mult)
                        dve.drain().then_inc(s["up_used"], 1)
                    else:
                        dve.tensor_tensor(gl[:, i, :], gl[:, i, :], bank[UB][:], ALU.mult).then_inc(s["up_used"], 1)
                        dve.drain()
                if n:
                    dve.wait_ge(s["comb_ready"], at["comb_ready"] + p * 4 + u + 1)
                    dve.tensor_tensor(h, gl[:, i, :], bank[CB][:], ALU.mult)
                    dve.drain().then_inc(s["comb_used"], 1)
                dve.drain().then_inc(s["h_ready"], 1)

            def add(half):
                for q in range(2):
                    dve.wait_ge(s["part_ready"], at["part_ready"] + p * 4 + 2 * half + q + 1)
                    t = half * TPS + 2 * q
                    dve.tensor_tensor(x[:, t:t + 2, :], x[:, t:t + 2, :],
                                      bank[DB][:].rearrange("p (t n) -> p t n", n=D), ALU.add).then_inc(s["part_added"], 1)

            unit(0)
            unit(1)
            unit(2)
            add(0)
            unit(3)
            add(1)

        bias2_ready = sem("bias2_ready")
        bias2_added = sem("bias2_added")

        def tensor_bias2(pe):
            for t in range(NT):
                if t >= 2:
                    pe.wait_ge(bias2_added, t - 1)
                cf = (combF, combF2)[t // 4]
                mm(bank[t % 2][:, 0:D], cf[:, (t % 4) * P:(t % 4 + 1) * P], dbias[:]).then_inc(bias2_ready, 1)

        def vector_bias2(dve):
            for t in range(NT):
                dve.wait_ge(bias2_ready, t + 1)
                dve.scalar_tensor_tensor(x[:, t, :], bank[t % 2][:, 0:D], 2.0, x[:, t, :], ALU.mult, ALU.add
                                         ).then_inc(bias2_added, 1)

        wq3 = wpart(3, [P, KD, H3 * HD3])
        wk3 = wpart(3, [P, H3 * HD3])
        wv3 = wpart(3, [P, H3 * HD3])
        wo3 = wpart(3, [P, H3, D])
        mem = sb("mem", [P, 2, P])
        memT = sb("memT", [P, MEM])
        aff = sb("aff", [P, 6])
        lbeta = sb("lbeta", [P, H3])
        st3 = sb("st3", [P, NT + 2, 6])
        mv3 = sb("mv3", [P, NT + 2, 2])
        rs3 = sb("rs3", [P, NT + 2])
        nm3 = sb("nm3", [P, NT + 2])
        xn3 = part(3, [P, NT, D])
        K3 = part(3, [P, H3, MEM])
        V3 = part(3, [P, 2, H3 * HD3])
        xi = [part(3, [P, 512]) for i in range(2)]
        sc3 = [part(3, [P, TPS, MEM]) for i in range(2)]
        re3 = part(3, [P, 2, TPS, MEM])
        w3 = [part(3, [P, TPS, MEM]) for i in range(2)]
        wT3 = [part(3, [P, 2, 512]) for i in range(2)]
        mx3 = sb("mx3", [P, 2, TPS])
        tau = sb("tau", [P, 2, TPS])
        s1 = sb("s1", [P, 2, TPS])
        s2 = sb("s2", [P, 2, TPS])
        na = sb("na", [P, 2, TPS])
        nb = sb("nb", [P, 2, TPS])
        N3 = {k: sem(f"mem_{k}") for k in ("stats", "rstd", "normed", "turned", "copied", "kv_ready", "kv_copied",
                                            "beta", "q_ready", "xi_ready", "xi_used", "sc_ready", "sc_max", "shifted",
                                            "sums_ready", "tau_ready", "w_rel", "w_ready", "w_T", "wT_ready",
                                            "o_ready", "o_added", "norm1")}

        def scalar_norm3(act):
            for t in range(NT):
                act.activation(xn3[:, t, :], x[:, t, :], ACT.Identity, bias=nmr[:, t:t + 1], scale=rstd[:, t:t + 1])
            act.drain().then_inc(N3["norm1"], 1)
            act.activation(lbeta[:], lbeta[:], ACT.Exp)
            act.drain().then_inc(N3["beta"], 1)
            act.wait_ge(N3["rstd"], 1)
            for t in range(NT):
                act.activation(xn3[:, t, :], xn3[:, t, :], ACT.Identity, bias=nm3[:, t:t + 1], scale=rs3[:, t:t + 1]
                               ).then_inc(N3["normed"], 1)
            for m in range(2):
                act.activation(mem[:, m, :], mem[:, m, :], ACT.Identity, bias=nm3[:, NT + m:NT + m + 1],
                               scale=rs3[:, NT + m:NT + m + 1]).then_inc(N3["normed"], 1)

        def vector_norm3(dve):
            dve.wait_ge(N3["norm1"], 1)
            for t in range(NT):
                dve.bn_stats(st3[:, t, :], xn3[:, t, :])
            for m in range(2):
                dve.bn_stats(st3[:, NT + m, :], mem[:, m, :])
            dve.drain()
            for t in range(NT + 2):
                dve.bn_aggr(mv3[:, t, :], st3[:, t, :])
            dve.drain().then_inc(N3["stats"], 1)
            dve.wait_ge(N3["beta"], 1)
            dve.tensor_scalar(lbeta[:], lbeta[:], 0.5, None, ALU.mult)
            dve.drain()
            for t in range(NT):
                dve.wait_ge(N3["turned"], t + 1)
                for k in range(KD):
                    dve.tensor_scalar(aoT[:, k, t * P:(t + 1) * P], bank[t % 2][:, k * P:(k + 1) * P],
                                      aff[:, k:k + 1], aff[:, 2 + k:3 + k], ALU.mult, ALU.add)
                dve.drain().then_inc(N3["copied"], 1)
            dve.wait_ge(N3["turned"], NT + 1)
            dve.tensor_scalar(memT[:], bank[2][:, 0:MEM], aff[:, 4:5], aff[:, 5:6], ALU.mult, ALU.add)
            dve.drain().then_inc(N3["copied"], 1)
            for h in range(H3):
                dve.wait_ge(N3["kv_ready"], h + 1)
                dve.tensor_scalar(K3[:, h, :], bank[4 + h % 2][:, 0:MEM], lbeta[:, h:h + 1], None, ALU.mult
                                  ).then_inc(N3["kv_copied"], 1)
            for c in range(4):
                dve.wait_ge(N3["kv_ready"], H3 + c + 1)
                dve.tensor_copy(V3[:, c // 2, (c % 2) * 512:(c % 2 + 1) * 512], bank[4 + c % 2][:]
                                ).then_inc(N3["kv_copied"], 1)

        def pool_norm3(pool):
            pool.wait_ge(N3["stats"], 1)
            pool.tensor_scalar(rs3[:], mv3[:, :, 1], LN_EPS, None, ALU.add)
            pool.drain()
            pool.tensor_tensor(rs3[:], rs3[:], half_neg[:, 0:NT + 2], ALU.pow)
            pool.drain()
            pool.tensor_tensor(nm3[:], mv3[:, :, 0], rs3[:], ALU.mult)
            pool.drain()
            pool.tensor_scalar(nm3[:], nm3[:], -1.0, None, ALU.mult)
            pool.drain().then_inc(N3["rstd"], 1)

        def tensor_norm3(pe):
            for t in range(NT):
                pe.wait_ge(N3["normed"], t + 1)
                if t >= 2:
                    pe.wait_ge(N3["copied"], t - 1)
                for k in range(KD):
                    last = nc.tensor.transpose(bank[t % 2][:, k * P:(k + 1) * P], xn3[:, t, k * P:(k + 1) * P], ident[:])
                last.then_inc(N3["turned"], 1)
            pe.wait_ge(N3["normed"], NT + 2)
            for m in range(2):
                last = nc.tensor.transpose(bank[2][:, m * P:(m + 1) * P], mem[:, m, :], ident[:])
            last.then_inc(N3["turned"], 1)
            pe.wait_ge(N3["copied"], NT + 1)
            for h in range(H3):
                if h >= 2:
                    pe.wait_ge(N3["kv_copied"], h - 1)
                mm(bank[4 + h % 2][:, 0:MEM], wk3[:, h * HD3:(h + 1) * HD3], memT[:]).then_inc(N3["kv_ready"], 1)
            for c in range(4):
                pe.wait_ge(N3["kv_copied"], H3 + c - 1)
                mm(bank[4 + c % 2][:], memT[:, (c // 2) * P:(c // 2 + 1) * P], wv3[:, (c % 2) * 512:(c % 2 + 1) * 512]
                   ).then_inc(N3["kv_ready"], 1)

        wq_s = part(3, [P, KD, HD3])
        v3_s = part(3, [P, 2, HD3])
        wo3_s = part(3, [P, D])
        head3_ready = sem("mem_head_ready")
        head3_used = sem("mem_head_used")

        def tensor_attention3(pe, h):
            n = N3
            pe.wait_ge(head3_ready, h + 1)
            for i in range(2):
                pe.wait_ge(n["o_added"], h * 8 + 4 * i + 4)
                for k in range(KD):
                    last = mm(bank[2 * i][:], wq_s[:, k, :], aoT[:, k, i * 512:(i + 1) * 512], k == 0, k == KD - 1)
                last.then_inc(n["q_ready"], 1)
            for st in range(STEPS3):
                for i in range(2):
                    j = st * 2 + i
                    pe.wait_ge(n["xi_ready"], h * 8 + j + 1)
                    for t in range(TPS):
                        last = mm(bank[2 * i + t // 2][:, (t % 2) * MEM:(t % 2 + 1) * MEM], xi[i][:, t * P:(t + 1) * P],
                                  K3[:, bass.ds(h, 1), :])
                    last.then_inc(n["sc_ready"], 1)
                for i in range(2):
                    j = st * 2 + i
                    pe.wait_ge(n["w_ready"], h * 6 + j + 1)
                    for m in range(2):
                        for t in range(TPS):
                            last = nc.tensor.transpose(bank[2 * i + m][:, t * P:(t + 1) * P],
                                                       w3[i][:, t, m * P:(m + 1) * P], ident[:])
                    last.then_inc(n["w_T"], 1)
                    pe.wait_ge(n["wT_ready"], h * 6 + j + 1)
                    for m in range(2):
                        last = mm(bank[2 * i][:], v3_s[:, m, :], wT3[i][:, m, :], m == 0, m == 1)
                    last.then_inc(n["q_ready"], 1)
            for i in range(2):
                pe.wait_ge(n["xi_ready"], h * 8 + 6 + i + 1)
                for t in range(TPS):
                    if t >= 2:
                        pe.wait_ge(n["o_added"], h * 8 + 4 * i + t + 7)
                    last = mm(bank[2 * i + t % 2][:, 0:D], xi[i][:, t * P:(t + 1) * P], wo3_s[:])
                    last.then_inc(n["o_ready"], 1)
            pe.drain().then_inc(head3_used, 1)

        def scalar_attention3(act, h):
            n = N3

            def take_xi(i, j):
                act.wait_ge(n["q_ready"], h * 8 + j + 1)
                act.activation(xi[i][:], bank[2 * i][:], ACT.Copy).then_inc(n["xi_ready"], 1)

            for i in range(2):
                take_xi(i, i)
            for st in range(STEPS3):
                for it in range(NEWTON + 1):
                    for i in range(2):
                        j = st * 2 + i
                        act.wait_ge(n["tau_ready"], h * 6 * (NEWTON + 1) + st * 2 * (NEWTON + 1) + it * 2 + i + 1)
                        for t in range(TPS):
                            if it < NEWTON:
                                act.activation(re3[:, i, t, :], sc3[i][:, t, :], ACT.Relu, bias=tau[:, i, t:t + 1],
                                               accum_out=s1[:, i, t:t + 1])
                            else:
                                act.activation(re3[:, i, t, :], sc3[i][:, t, :], ACT.Relu, bias=tau[:, i, t:t + 1])
                        act.drain().then_inc(n["w_rel"], 1)
                for i in range(2):
                    j = st * 2 + i
                    act.wait_ge(n["w_T"], h * 6 + j + 1)
                    for m in range(2):
                        act.activation(wT3[i][:, m, :], bank[2 * i + m][:], ACT.Copy)
                    act.drain().then_inc(n["wT_ready"], 1)
                    take_xi(i, 2 + j)

        def vector_attention3(dve, h):
            n = N3
            with_tau = h * 6 * (NEWTON + 1)
            for st in range(STEPS3):
                for i in range(2):
                    j = st * 2 + i
                    dve.wait_ge(n["sc_ready"], h * 6 + j + 1)
                    for c in range(2):
                        sc = bank[2 * i + c][:].rearrange("p (t m) -> p t m", m=MEM)
                        dve.tensor_reduce(mx3[:, i, 2 * c:2 * c + 2], sc, AX.X, ALU.max)
                    dve.memset(tau[:, i, :], 1.0)
                    dve.drain()
                    for c in range(2):
                        sc = bank[2 * i + c][:].rearrange("p (t m) -> p t m", m=MEM)
                        dve.tensor_tensor(sc3[i][:, 2 * c:2 * c + 2, :], sc,
                                          mx3[:, i, 2 * c:2 * c + 2].unsqueeze(2).to_broadcast([P, 2, MEM]), ALU.subtract)
                    dve.drain().then_inc(n["tau_ready"], 1)
                for it in range(NEWTON):
                    for i in range(2):
                        r = with_tau + st * 2 * (NEWTON + 1) + it * 2 + i + 1
                        dve.wait_ge(n["w_rel"], r)
                        for t in range(TPS):
                            dve.tensor_tensor_reduce(w3[i][:, t, :], re3[:, i, t, :], re3[:, i, t, :], 1.0, 0.0, ALU.mult, ALU.add,
                                                     s2[:, i, t:t + 1])
                        dve.drain()
                        dve.scalar_tensor_tensor(nb[:, i, :], s2[:, i, :], 3.0, s1[:, i, :], ALU.add, ALU.mult)
                        dve.tensor_tensor(na[:, i, :], s2[:, i, :], s2[:, i, :], ALU.mult)
                        dve.drain()
                        dve.reciprocal(nb[:, i, :], nb[:, i, :])
                        dve.drain()
                        dve.scalar_tensor_tensor(na[:, i, :], na[:, i, :], -1.0, nb[:, i, :], ALU.add, ALU.mult)
                        dve.drain()
                        dve.tensor_tensor(tau[:, i, :], tau[:, i, :], na[:, i, :], ALU.subtract)
                        dve.drain()
                        dve.tensor_scalar(tau[:, i, :], tau[:, i, :], MEM ** -0.5, 1.0, ALU.max, ALU.min)
                        dve.drain().then_inc(n["tau_ready"], 1)
                for i in range(2):
                    r = with_tau + st * 2 * (NEWTON + 1) + NEWTON * 2 + i + 1
                    dve.wait_ge(n["w_rel"], r)
                    dve.tensor_tensor(w3[i][:], re3[:, i, :, :], re3[:, i, :, :], ALU.mult)
                    dve.drain().then_inc(n["w_ready"], 1)
            for i in range(2):
                for t in range(TPS):
                    dve.wait_ge(n["o_ready"], h * 8 + 4 * i + t + 1)
                    dve.tensor_tensor(x[:, i * TPS + t, :], x[:, i * TPS + t, :], bank[2 * i + t % 2][:, 0:D], ALU.add)
                    dve.drain().then_inc(n["o_added"], 1)

        def pool_attention3(pool):
            with pool.Fori(0, H3) as h:
                pool.wait_ge(head3_used, h + 1)
                pool.tensor_copy(wq_s[:], wq3[:, :, bass.ds(h * HD3, HD3)])
                pool.tensor_copy(v3_s[:], V3[:, :, bass.ds(h * HD3, HD3)])
                pool.tensor_copy(wo3_s[:], wo3[:, bass.ds(h, 1), :])
                pool.drain().then_inc(head3_ready, 1)

        LOADS = [0, 0, 0, 0]
        loads = [
            [(ident, "ident"), (head_mask, "head_mask"), (gates, "gates"), (order_pos, "order_pos"), (wqkv[0], "wqkv0"),
             (bqkv, "bqkv"), (wo[0], "wo0"), (bo, "bo")],
            [(rope, "rope"), (wqkv[1], "wqkv1"), (wo[1], "wo1"), (router[1], "router1"), (lower, "lower"),
             (decay, "decay"), (decay_q, "decay_q"), (decay_k, "decay_k"), (lam_chunk, "lam_chunk"),
             (own_block, "own_block"), (wg1, "wg1"), (wg2, "wg2"), (norm_w, "norm_w")],
            [(causal, "causal"), (wqkv[2], "wqkv2"), (wo[2], "wo2"), (router[2], "router2"), (rbias, "rbias"),
             (dbias, "dbias"), (gu_bias, "gu_bias")],
            [(wq3, "wq3"), (wk3, "wk3"), (wv3, "wv3"), (wo3, "wo3"), (mem, "mem"), (aff, "aff"), (lbeta, "lbeta"),
             (router[3], "router3")],
        ]
        for n in range(4):
            LOADS[n] = 16 * len(loads[n])
        LN_S = 6.238324625039508
        out_stored = sem("out_stored")
        PAIRS_IN = 8

        def load_broadcast(name):
            return a[name].shape[0] == 1

        block = ctx.enter_context(nc.Block())

        @block.sync
        def _(sp):
            sp.dma_start(x[:], a["x"]).then_inc(x_loaded, 16)
            for n in range(4):
                if n == 3:
                    sp.wait_ge(phase_done, 4 * 13)
                for dst, name in loads[n]:
                    src = a[name]
                    if load_broadcast(name):
                        src = src.to_broadcast([P] + list(src.shape[1:]))
                    sp.dma_start(dst[:], src).then_inc(loaded[n], 16)
                if n == 2:
                    sync_ffn(sp, 0, 0, CHUNKS[0] // 2)
                    sync_ffn(sp, 1, 0, CHUNKS[1] // 2)
            for n in range(2, 4):
                sync_ffn(sp, n, 0, CHUNKS[n] // 2)
            sp.wait_ge(phase_done, 4 * BARRIERS)
            sp.dma_start(out, x[:]).then_inc(out_stored, 16)
            sp.wait_ge(out_stored, 16)

        def ffn_loop(eng, pair, n, first=0, count=None):
            with eng.Fori(first, first + (count or CHUNKS[n] // 2 - first)) as p:
                pair(eng, n, p)

        @block.tensor
        def _(pe):
            pe.wait_ge(loaded[0], LOADS[0])
            for n in range(3):
                tensor_norm(pe, n)
                barrier(pe)
                pe.wait_ge(loaded[n], LOADS[n])
                if n == 2:
                    pe.wait_ge(loaded[1], LOADS[1])
                tensor_project(pe, n)
                barrier(pe)
                if n == 0:
                    barrier(pe)
                if n == 1:
                    tensor_linear(pe)
                else:
                    tensor_heads(pe, n)
                barrier(pe)
                if n != 1:
                    barrier(pe)
                tensor_out(pe, n)
                barrier(pe)
                if n:
                    tensor_route(pe, n)
                    barrier(pe)
                if n == 2:
                    tensor_bias2(pe)
                    barrier(pe)
                tensor_ffn_start(pe, n)
                ffn_loop(pe, tensor_ffn_pair, n)
                barrier(pe)
            tensor_norm(pe, 3)
            barrier(pe)
            pe.wait_ge(loaded[3], LOADS[3])
            tensor_norm3(pe)
            barrier(pe)
            tensor_route(pe, 3)
            barrier(pe)
            tensor_ffn_start(pe, 3)
            pe.drain().then_inc(head3_used, 1)
            with pe.Fori(0, H3) as h:
                tensor_attention3(pe, h)
                tensor_ffn_pair(pe, 3, h)
            ffn_loop(pe, tensor_ffn_pair, 3, PAIRS_IN)
            barrier(pe)

        @block.scalar
        def _(act):
            scalar_gates(act)
            for n in range(3):
                scalar_norm(act, n)
                barrier(act)
                scalar_project(act, n)
                barrier(act)
                if n == 0:
                    barrier(act)
                if n == 1:
                    scalar_linear(act)
                else:
                    scalar_heads(act, n)
                barrier(act)
                if n == 0:
                    scalar_rows(act)
                if n != 1:
                    barrier(act)
                scalar_out(act, n)
                barrier(act)
                if n:
                    scalar_route(act, n)
                    barrier(act)
                if n == 2:
                    barrier(act)
                ffn_loop(act, scalar_ffn_pair, n)
                barrier(act)
            scalar_norm(act, 3)
            barrier(act)
            act.wait_ge(loaded[3], LOADS[3])
            scalar_norm3(act)
            barrier(act)
            scalar_route(act, 3)
            barrier(act)
            with act.Fori(0, H3) as h:
                scalar_attention3(act, h)
                scalar_ffn_pair(act, 3, h)
            ffn_loop(act, scalar_ffn_pair, 3, PAIRS_IN)
            barrier(act)

        @block.vector
        def _(dve):
            dve.wait_ge(loaded[0], LOADS[0])
            vector_gates(dve)
            for n in range(3):
                vector_norm(dve, n)
                barrier(dve)
                if n:
                    dve.wait_ge(loaded[n], LOADS[n])
                vector_project(dve, n)
                barrier(dve)
                if n == 0:
                    vector_diffs(dve)
                    barrier(dve)
                if n == 1:
                    vector_linear(dve)
                else:
                    vector_heads(dve, n)
                barrier(dve)
                if n == 0:
                    vector_rows(dve)
                if n == 2:
                    vector_divide(dve)
                if n != 1:
                    barrier(dve)
                vector_out(dve, n)
                barrier(dve)
                if n:
                    vector_route(dve, n)
                    barrier(dve)
                if n == 2:
                    vector_bias2(dve)
                    barrier(dve)
                vector_ffn_start(dve, n)
                ffn_loop(dve, vector_ffn_pair, n)
                barrier(dve)
            vector_norm(dve, 3)
            barrier(dve)
            dve.wait_ge(loaded[3], LOADS[3])
            vector_norm3(dve)
            barrier(dve)
            vector_route(dve, 3)
            barrier(dve)
            vector_ffn_start(dve, 3)
            dve.drain().then_inc(N3["o_added"], 8)
            with dve.Fori(0, H3) as h:
                vector_attention3(dve, h)
                vector_ffn_pair(dve, 3, h)
            ffn_loop(dve, vector_ffn_pair, 3, PAIRS_IN)
            barrier(dve)

        @block.gpsimd
        def _(pool):
            pool.wait_ge(gates_ready, 1)
            for n in range(3):
                pool_norm(pool, n)
                barrier(pool)
                barrier(pool)
                if n == 0:
                    barrier(pool)
                if n == 1:
                    pool_linear(pool)
                barrier(pool)
                if n == 0:
                    pool_rows(pool)
                if n != 1:
                    barrier(pool)
                barrier(pool)
                if n:
                    barrier(pool)
                if n == 2:
                    barrier(pool)
                barrier(pool)
            pool_norm(pool, 3)
            barrier(pool)
            pool_norm3(pool)
            barrier(pool)
            barrier(pool)
            pool_attention3(pool)
            barrier(pool)




def _constants(np):
    p = np.arange(P)
    c = {"ident": np.eye(P, dtype=np.float32)}
    c["head_mask"] = (p[:, None] // HD == np.arange(GH)[None, :]).astype(np.float32)
    c["causal"] = np.where(p[None, :] > p[:, None], np.float32(MASKED), np.float32(0))
    c["own_block"] = (p[:, None] // HD == p[None, :] // HD).astype(np.float32)
    pos = (np.arange(TPS)[None, :] * P + p[:, None]).astype(np.float32)
    c["order_pos"] = (pos / np.float32(S) * np.float32(0.05)).astype(np.float32)
    half = HD // 2
    th1 = np.float32(10000.0) ** (np.float32(-2.0) * np.arange(half, dtype=np.float32) / np.float32(HD))
    th2 = np.float32(1.0) / np.float32(10000.0) ** (np.arange(0, HD, 2, dtype=np.float32) / np.float32(HD))
    rope = np.zeros((P, 2, TPS, 2, half), np.float32)
    for i, th in enumerate((th1, th2)):
        ang = (pos[:, :, None] * th.astype(np.float32)).astype(np.float32)
        rope[:, i, :, 0, :] = np.cos(ang)
        rope[:, i, :, 1, :] = np.sin(ang)
    c["rope"] = rope
    lam = -(2.0 ** (-8.0 * (np.arange(H) + 1.0) / H))
    d = p[None, None, :] - p[:, None, None]
    c["decay"] = np.where(d >= 0, np.exp(lam[None, :, None] * np.maximum(d, 0)), 0.0).astype(np.float32)
    c["decay_q"] = np.exp(lam[None, :] * (p[:, None] + 1.0)).astype(np.float32)
    c["decay_k"] = np.exp(lam[None, :] * (P - 1.0 - p[:, None])).astype(np.float32)
    lc = np.exp(lam * P).reshape(NG, GH)
    c["lam_chunk"] = np.ascontiguousarray(np.broadcast_to(lc[:, p // HD].T[:, :, None], (P, NG, P))).astype(np.float32)
    e = np.arange(16)
    c["lower"] = np.broadcast_to((e[None, :] < e[:, None]).astype(np.float32)[None], (1, 16, 16)).copy()
    for n, w in ((1, 176), (2, 256), (3, 176)):
        unit = np.arange(CHUNKS[n] * P)
        owner = np.minimum(unit // w, EXPERTS[n])
        sel = np.zeros((CHUNKS[n], CR, P), np.float32)
        for part in range(3):
            sel[unit // P, part * NE + owner, unit % P] = 1
        c[f"sel{n}"] = sel
    return c


def _rows(np, w):
    return np.ascontiguousarray(w.reshape(-1, P, w.shape[1]).transpose(1, 0, 2))


def kernel(**inputs):
    import ml_dtypes
    import numpy as np
    import concourse.bacc as bacc
    from concourse.bass_utils import run_bass_kernel_spmd as run

    i = {k: np.asarray(v) for k, v in inputs.items()}
    a = _constants(np)
    for n in (1, 2, 3):
        a[f"sel{n}"] = a[f"sel{n}"].astype(ml_dtypes.bfloat16)

    def row(*names):
        return np.concatenate([i[k].reshape(-1) for k in names])[None, :]

    a["x"] = np.ascontiguousarray(i["L0_attn_hidden_states"].reshape(NT, P, D).transpose(1, 0, 2))
    a["wqkv0"] = _rows(np, np.concatenate([i[f"L0_attn_W{c}"].T for c in "qkv"], 1))
    a["bqkv"] = row("L0_attn_bq", "L0_attn_bk", "L0_attn_bv")
    a["wo0"], a["bo"] = _rows(np, i["L0_attn_Wo"].T), row("L0_attn_bo")
    a["gates"] = row(*[f"L0_attn_{c}_gate" for c in ("truth", "balance", "order", "justice", "harmony")])
    a["wqkv1"] = _rows(np, np.concatenate([i[f"L1_attn_W{c}"] for c in "qkv"], 1))
    a["wo1"], a["router1"] = _rows(np, i["L1_attn_Wo"]), _rows(np, i["L1_ffn_gate_w"])
    a["wg1"], a["wg2"] = _rows(np, i["L1_attn_Wg1"]), i["L1_attn_Wg2"]
    a["norm_w"] = row("L1_attn_norm_weight")
    wk = np.repeat(i["L2_attn_wk"].reshape(D, 4, HD), 4, axis=1).reshape(D, D)
    a["wqkv2"] = _rows(np, np.concatenate([i["L2_attn_wq"], wk, i["L2_attn_wv"]], 1))
    a["wo2"], a["router2"] = _rows(np, i["L2_attn_wo"]), _rows(np, i["L2_ffn_router_weight"].T)
    a["rbias"], a["dbias"] = row("L2_ffn_router_bias"), i["L2_ffn_down_proj_bias"]
    a["wq3"] = _rows(np, i["L3_attn_Wq"].T)
    a["wk3"], a["wv3"] = i["L3_attn_Wk"].T, i["L3_attn_Wv"].T
    a["wo3"] = _rows(np, i["L3_attn_Wo"].T)
    a["mem"] = _rows(np, i["L3_attn_memory"])
    a["aff"] = np.concatenate([i["L3_attn_g_state"].reshape(2, P).T, i["L3_attn_b_state"].reshape(2, P).T,
                               i["L3_attn_g_mem"][:, None], i["L3_attn_b_mem"][:, None]], 1)
    a["lbeta"] = row("L3_attn_log_beta")
    a["router3"] = _rows(np, np.concatenate([i["L3_ffn_gate_w"], i["L3_ffn_shared_gate_vec"]], 0).T)

    def wide(w):
        return w.transpose(1, 0, 2).reshape(D, -1)

    ffn = [(i["L0_ffn_w_gate"].T, i["L0_ffn_w_up"].T, i["L0_ffn_w_down"].T, None)]
    ffn.append((np.concatenate([wide(i["L1_ffn_w_gate"]), i["L1_ffn_sw_gate"]], 1),
                np.concatenate([wide(i["L1_ffn_w_up"]), i["L1_ffn_sw_up"]], 1),
                np.concatenate([i["L1_ffn_w_down"].reshape(-1, D), i["L1_ffn_sw_down"]], 0), None))
    gu, bias = i["L2_ffn_gate_up_proj"], i["L2_ffn_gate_up_proj_bias"]
    ffn.append((wide(gu[:, :, 0::2]), wide(gu[:, :, 1::2]), i["L2_ffn_down_proj"].reshape(-1, D),
                (bias[:, 0::2].reshape(-1), bias[:, 1::2].reshape(-1))))
    eg, sg = i["L3_ffn_expert_gate_up"].transpose(0, 2, 1), i["L3_ffn_shared_gate_up"]
    ffn.append((np.concatenate([wide(eg[:, :, :176]), sg[:704].T], 1),
                np.concatenate([wide(eg[:, :, 176:]), sg[704:].T], 1),
                np.concatenate([i["L3_ffn_expert_down"].transpose(0, 2, 1).reshape(-1, D), i["L3_ffn_shared_down"].T], 0),
                None))
    a["gu"] = np.zeros((sum(CHUNKS), P, GUW), np.float32)
    a["down"] = np.zeros((sum(CHUNKS), P, D), np.float32)
    first = 0
    for n, (g, u, d, b) in enumerate(ffn):
        hidden, width = g.shape[1], CHUNKS[n] * P
        for at, w in ((0, g), (2 * P, u)):
            full = np.zeros((D, width), np.float32)
            full[:, :hidden] = w
            parts = full.reshape(KD, P, CHUNKS[n], P).transpose(2, 1, 0, 3).reshape(CHUNKS[n], P, D)
            a["gu"][first:first + CHUNKS[n], :, at:at + D] = parts
        if b is not None:
            a["gu_bias"] = np.stack([c.reshape(CHUNKS[n], P).T for c in b], 2)
        full = np.zeros((width, D), np.float32)
        full[:hidden] = d
        a["down"][first:first + CHUNKS[n]] = full.reshape(CHUNKS[n], P, D)
        first += CHUNKS[n]

    nc = bacc.Bacc("TRN2", target_bir_lowering=False, num_devices=1)
    arrays = {k: np.ascontiguousarray(v) for k, v in a.items()}
    aps = {k: nc.dram_tensor(f"in_{k}", v.shape, mybir.dt.from_np(v.dtype), kind="ExternalInput").ap()
           for k, v in arrays.items()}
    out = nc.dram_tensor("out", (P, NT, D), F32, kind="ExternalOutput").ap()
    build(nc, aps, out)
    r = run(nc, [{f"in_{k}": v for k, v in arrays.items()}], core_ids=[0])
    return r.results[0]["out"].transpose(1, 0, 2).reshape(B, S, D)
```

```python
from contextlib import ExitStack

import concourse.bass as bass
from concourse import mybir

F32 = mybir.dt.float32
BF16 = mybir.dt.bfloat16
ALU = mybir.AluOpType
ACT = mybir.ActivationFunctionType
AX = mybir.AxisListType

P = 128
D = 256
KD = D // P
AREA = 17800
WAREA = 6144
B, S = 2, 512
TOK = B * S
NT = TOK // P
TPS = S // P
H, HD = 16, 16
GH = P // HD
NG = H // GH
VW = HD + 1
NE = 17
CR = 3 * NE
GUW = 2 * D
EXPERTS = (0, 8, 8, 16)
TOPK = (0, 2, 2, 4)
CHUNKS = (8, 14, 16, 28)
LN_EPS = 1e-5
MASKED = -1e30
H3, HD3 = 8, 128
MEM = 256
STEPS3 = 3
BARRIERS = 25
NEWTON = 5


def build(nc, a, out):
    with ExitStack() as ctx:
        def sb(name, shape, dt=F32):
            return ctx.enter_context(nc.sbuf_tensor(name, shape, dt))

        area = sb("area", [P, AREA])
        taken = {0: 0, 1: 0, 3: 0}
        warea = sb("warea", [P, WAREA])
        wtaken = {0: 0, 3: 0}

        def part(layer, shape, area=area, taken=taken, AREA=AREA):
            size = 1
            for k in shape[1:]:
                size *= k
            at = taken[layer]
            taken[layer] = at + size
            assert at + size <= AREA
            names = "abcd"[:len(shape) - 1]
            return area[:, at:at + size].rearrange(f"p ({' '.join(names)}) -> p {' '.join(names)}",
                                                   **dict(zip(names, shape[1:])))

        def wpart(layer, shape):
            return part(layer, shape, warea, wtaken, WAREA)

        def sem(name):
            return ctx.enter_context(nc.semaphore(name))

        bank = [ctx.enter_context(nc.psum_tensor(f"bank{i}", [P, 512], F32)) for i in range(8)]

        ident = sb("ident", [P, P])
        identb = sb("identb", [P, P], BF16)
        head_mask = sb("head_mask", [P, GH])
        causal = sb("causal", [P, P])
        rope = sb("rope", [P, 2, TPS, 2, HD // 2])
        half_neg = sb("half_neg", [P, NT * H])
        wqkv = [wpart(0, [P, KD, 768]), wpart(0, [P, KD, 768]), sb("wqkv2", [P, KD, 576])]
        wo = [sb(f"wo{n}", [P, KD, D]) for n in range(3)]
        bqkv = wpart(0, [P, 768])
        bo = sb("bo", [P, D])
        gates = sb("gates", [P, 5])
        router = [None, sb("router1", [P, KD, 8]), sb("router2", [P, KD, 8]), sb("router3", [P, KD, NE])]
        rbias = sb("rbias", [P, 8])
        dbias = sb("dbias", [8, D])
        gu_bias = sb("gu_bias", [P, CHUNKS[2], 2])
        lower = sb("lower", [P, 16, 16])
        decay = wpart(0, [P, H, P])
        decay_q = sb("decay_q", [P, H])
        decay_k = sb("decay_k", [P, H])
        lam_chunk = sb("lam_chunk", [P, NG, P])
        own_block = sb("own_block", [P, P])
        wg1 = sb("wg1", [P, KD, HD])
        wg2 = sb("wg2", [HD, D])
        norm_w = sb("norm_w", [P, D])

        x = sb("x", [P, NT, D])
        xnT = sb("xnT", [P, KD, TOK])
        xn = sb("xn", [P, 2, D])
        st6 = sb("st6", [P, NT, 6])
        mv = sb("mv", [P, NT, 2])
        rstd = sb("rstd", [P, NT])
        nmr = sb("nmr", [P, NT])
        tok = sb("tok", [P, 2, 512])
        tmp = sb("tmp", [P, 2, 512])
        qT = part(0, [P, B * NG, S])
        kT = part(0, [P, B * NG, S])
        v = part(0, [P, B * H + 2, TPS, VW])
        taken[1] = taken[0]
        kdT = part(0, [P, B * NG, S])
        raw = part(0, [P, B * H + 2, TPS, VW])
        ao = sb("ao", [P, NT, D])
        aoT = sb("aoT", [P, KD, TOK])
        logits = sb("logits", [P, NT, 16])
        probs = sb("probs", [P, NT, 16])
        comb = sb("comb", [P, NT, NE])
        combp = sb("combp", [P, NT, CR], BF16)
        combT = sb("combT", [CR, TOK], BF16)
        rank = sb("rank", [P, 16, 16])
        rank2 = sb("rank2", [P, 16, 16])
        rowm = sb("rowm", [P, NT])
        rowz = sb("rowz", [P, NT])
        rankn = sb("rankn", [P, NT, 16])
        shared = sb("shared", [P, NT])

        wgu = [sb(f"wgu{c}", [P, GUW]) for c in range(2)]
        wd = sb("wd", [P, 2, D])
        sel = [sb(f"sel{c}", [CR, P], BF16) for c in range(2)]
        th = sb("th", [P, 2, 512])
        gl = sb("gl", [P, 2, 512])
        up = sb("up", [P, 2, 512])
        hT = sb("hT", [P, 4, 512])

        phase_done = sem("phase_done")
        loaded = [sem(f"weights{n}_loaded") for n in range(4)]
        x_loaded = sem("x_loaded")
        phases = {}

        def barrier(eng):
            n = phases[eng.engine] = phases.get(eng.engine, 0) + 1
            eng.drain().then_inc(phase_done, 1)
            eng.wait_ge(phase_done, 4 * n)

        def mm(o, l, r, start=True, stop=True):
            return nc.tensor.matmul(o, l, r, start=start, stop=stop)

        def total(n):
            pairs = CHUNKS[n] // 2
            t = {"stats_ready": 1, "rstd_ready": 1, "xn_ready": NT, "xn_T": NT, "xnT_ready": NT}
            for k in ("qk_ready", "v_ready", "qk_tok", "qk_T", "qk_copied", "v_copied", "ao_T", "aoT_ready",
                      "o_ready", "o_added"):
                t[k] = NT if n < 3 else 0
            for k in ("logits_ready", "logits_copied"):
                t[k] = NT if n == 3 else 0
            t["route_exp"] = 2 if n else 0
            t["comb_T"] = (0, 2, 3, 2)[n]
            for k in ("guA_loaded", "guB_loaded"):
                t[k] = (32 if n else 16) * pairs
            t["down_loaded"] = 16 * pairs
            for k in ("guA_used", "guB_used", "down_used"):
                t[k] = pairs
            for k in ("gate_ready", "up_ready", "tanh_ready", "gate_used", "up_used", "h_ready", "part_ready",
                      "part_added"):
                t[k] = 4 * pairs
            for k in ("comb_ready", "comb_used"):
                t[k] = 4 * pairs if n else 0
            t["gate_clipped"] = 4 * pairs if n == 2 else 0
            return t

        LS = {k: sem(k) for k in total(0)}
        AT = [{k: sum(total(m)[k] for m in range(n)) for k in total(0)} for n in range(4)]

        def vector_norm(dve, n):
            s, at = LS, AT[n]
            if n == 0:
                dve.wait_ge(x_loaded, 16)
            for t in range(NT):
                dve.bn_stats(st6[:, t, :], x[:, t, :])
            dve.drain()
            for t in range(NT):
                last = dve.bn_aggr(mv[:, t, :], st6[:, t, :])
            last.then_inc(s["stats_ready"], 1)
            for t in range(NT):
                dve.wait_ge(s["xn_T"], at["xn_T"] + t + 1)
                dve.tensor_copy(xnT[:, :, t * P:(t + 1) * P],
                                bank[t % 2][:, 0:D].rearrange("p (k t) -> p k t", k=KD)).then_inc(s["xnT_ready"], 1)

        def pool_norm(pool, n):
            s, at = LS, AT[n]
            pool.wait_ge(s["stats_ready"], at["stats_ready"] + 1)
            pool.tensor_scalar(rstd[:], mv[:, :, 1], LN_EPS, None, ALU.add)
            pool.drain()
            pool.tensor_tensor(rstd[:], rstd[:], half_neg[:, 0:NT], ALU.pow)
            pool.drain()
            pool.tensor_tensor(nmr[:], mv[:, :, 0], rstd[:], ALU.mult)
            pool.drain()
            pool.tensor_scalar(nmr[:], nmr[:], -1.0, None, ALU.mult).then_inc(s["rstd_ready"], 1)

        def scalar_norm(act, n):
            s, at = LS, AT[n]
            act.wait_ge(s["rstd_ready"], at["rstd_ready"] + 1)
            for t in range(NT):
                if t >= 2:
                    act.wait_ge(s["xn_T"], at["xn_T"] + t - 1)
                act.activation(xn[:, t % 2, :], x[:, t, :], ACT.Identity, bias=nmr[:, t:t + 1],
                               scale=rstd[:, t:t + 1]).then_inc(s["xn_ready"], 1)

        def tensor_norm(pe, n):
            s, at = LS, AT[n]
            for t in range(NT):
                pe.wait_ge(s["xn_ready"], at["xn_ready"] + t + 1)
                if t >= 2:
                    pe.wait_ge(s["xnT_ready"], at["xnT_ready"] + t - 1)
                for k in range(KD):
                    last = nc.tensor.transpose(bank[t % 2][:, k * P:(k + 1) * P], xn[:, t % 2, k * P:(k + 1) * P],
                                               ident[:])
                last.then_inc(s["xn_T"], 1)

        def heads_of(t):
            b = t // TPS
            return slice(b * H, (b + 1) * H)

        def v_of(t, first=0, count=H):
            at = 2 + t // TPS * H + first
            return v[:, at:at + count, t % TPS, :]

        def group_of(t):
            b, c = t // TPS, t % TPS
            return (slice(None), slice(b * NG, (b + 1) * NG), slice(c * P, (c + 1) * P))

        def tensor_project(pe, n):
            s, at = LS, AT[n]
            vw = wqkv[n].shape[2] - 512

            def turn(t):
                pe.wait_ge(s["qk_tok"], at["qk_tok"] + t + 1)
                if t >= 2:
                    pe.wait_ge(s["qk_copied"], at["qk_copied"] + t - 1)
                for c in range(4):
                    last = nc.tensor.transpose(bank[4 + t % 2][:, c * P:(c + 1) * P],
                                               tok[:, t % 2, c * P:(c + 1) * P], ident[:])
                last.then_inc(s["qk_T"], 1)

            for t in range(NT):
                pe.wait_ge(s["xnT_ready"], at["xnT_ready"] + t + 1)
                if t >= 2:
                    pe.wait_ge(s["qk_tok"], at["qk_tok"] + t - 1)
                ts = slice(t * P, (t + 1) * P)
                for k in range(KD):
                    last = mm(bank[t % 2][:], xnT[:, k, ts], wqkv[n][:, k, 0:512], k == 0, k == KD - 1)
                last.then_inc(s["qk_ready"], 1)
                if t >= 2:
                    pe.wait_ge(s["v_copied"], at["v_copied"] + t - 1)
                for k in range(KD):
                    last = mm(bank[2 + t % 2][:, 0:vw], xnT[:, k, ts], wqkv[n][:, k, 512:], k == 0, k == KD - 1)
                if n:
                    for k in range(KD):
                        last = mm(bank[2 + t % 2][:, D:D + 8], xnT[:, k, ts], router[n][:, k, :], k == 0, k == KD - 1)
                last.then_inc(s["v_ready"], 1)
                if t:
                    turn(t - 1)
            turn(NT - 1)

        def vector_project(dve, n):
            s, at = LS, AT[n]
            for t in range(NT):
                dve.wait_ge(s["qk_ready"], at["qk_ready"] + t + 1)
                if t >= 2:
                    dve.wait_ge(s["qk_T"], at["qk_T"] + t - 1)
                o, qk = tok[:, t % 2, :], bank[t % 2]
                if n == 0:
                    dve.tensor_tensor(o, qk[:], bqkv[:, 0:512], ALU.add).then_inc(s["qk_tok"], 1)
                else:
                    src = qk[:]
                    if n == 1:
                        dve.wait_ge(silu_tanh, t + 1)
                        dve.scalar_tensor_tensor(tmp[:, 0, :], th[:, t % 2, :], 1.0, qk[:], ALU.add, ALU.mult)
                        dve.drain()
                        dve.tensor_scalar(tmp[:, 0, :], tmp[:, 0, :], 0.5, None, ALU.mult)
                        dve.drain()
                        src = tmp[:, 0, :]
                    sh = src.rearrange("p (h a e) -> p h a e", a=2, e=HD // 2)
                    oh = o.rearrange("p (h a e) -> p h a e", a=2, e=HD // 2)
                    mh = tmp[:, 1, :].rearrange("p (h a e) -> p h a e", a=2, e=HD // 2)
                    cs = [rope[:, n - 1, t % TPS, i, :].unsqueeze(1).to_broadcast([P, 2 * H, HD // 2]) for i in (0, 1)]
                    for a2 in (0, 1):
                        dve.tensor_tensor(oh[:, :, a2, :], sh[:, :, a2, :], cs[0], ALU.mult)
                        dve.tensor_tensor(mh[:, :, a2, :], sh[:, :, 1 - a2, :], cs[1], ALU.mult)
                    dve.drain()
                    dve.tensor_tensor(oh[:, :, 0, :], oh[:, :, 0, :], mh[:, :, 0, :], ALU.subtract)
                    dve.tensor_tensor(oh[:, :, 1, :], oh[:, :, 1, :], mh[:, :, 1, :], ALU.add)
                    dve.drain().then_inc(s["qk_tok"], 1)
                if n == 0:
                    dve.drain()
                    dve.tensor_tensor(tmp[:, 0, 0:D], tok[:, t % 2, D:], tok[:, t % 2, D:], ALU.mult)
                    dve.drain()
                    dve.tensor_reduce(knorm[:, heads_of(t), t % TPS], tmp[:, 0, 0:D].rearrange("p (h e) -> p h e", e=HD), AX.X, ALU.add)
                if n == 1:
                    dve.drain()
                    dve.tensor_tensor(kd[:, t, :].rearrange("p (h e) -> p h e", e=HD),
                                      tok[:, t % 2, D:].rearrange("p (h e) -> p h e", e=HD),
                                      decay_k[:].unsqueeze(2).to_broadcast([P, H, HD]), ALU.mult)
                dve.wait_ge(s["v_ready"], at["v_ready"] + t + 1)
                vb = bank[2 + t % 2]
                if n == 0:
                    dve.tensor_tensor(tmp[:, 1, 0:D], vb[:, 0:D], bqkv[:, 512:], ALU.add)
                    dve.drain().then_inc(s["v_copied"], 1)
                    dve.tensor_scalar(v_of(t)[:, :, 0:HD], tmp[:, 1, 0:D].rearrange("p (h e) -> p h e", e=HD),
                                      order_exp[:, t % TPS:t % TPS + 1], None, ALU.mult)
                    dve.tensor_copy(v_of(t)[:, :, HD], order_exp[:, t % TPS:t % TPS + 1].to_broadcast([P, H]))
                elif n == 1:
                    dve.tensor_copy(v_of(t)[:, :, 0:HD], vb[:, 0:D].rearrange("p (h e) -> p h e", e=HD))
                    dve.tensor_copy(logits[:, t, 0:8], vb[:, D:D + 8]).then_inc(s["v_copied"], 1)
                else:
                    for r in range(4):
                        dve.tensor_copy(v_of(t).rearrange("p (h r) e -> p h r e", r=4)[:, :, r, 0:HD],
                                        vb[:, 0:64].rearrange("p (h e) -> p h e", e=HD))
                    dve.tensor_tensor(logits[:, t, 0:8], vb[:, D:D + 8], rbias[:], ALU.add).then_inc(s["v_copied"], 1)
            if n == 2:
                dve.memset(v[:, 2:, :, HD:VW], 1.0)

        def scalar_project(act, n):
            s, at = LS, AT[n]

            def out_T(t):
                act.wait_ge(s["qk_T"], at["qk_T"] + t + 1)
                src = bank[4 + t % 2][:].rearrange("p (q t) -> p q t", t=P)
                act.activation(qT[group_of(t)], src[:, 0:NG, :], ACT.Copy)
                act.activation(kT[group_of(t)], src[:, NG:, :], ACT.Copy)
                act.drain().then_inc(s["qk_copied"], 1)

            for t in range(NT):
                if n == 1:
                    act.wait_ge(s["qk_ready"], at["qk_ready"] + t + 1)
                    if t >= 2:
                        act.wait_ge(s["qk_tok"], at["qk_tok"] + t - 1)
                    act.activation(th[:, t % 2, :], bank[t % 2][:], ACT.Tanh, scale=0.5).then_inc(silu_tanh, 1)
                    if t:
                        out_T(t - 1)
                else:
                    out_T(t)
            if n == 1:
                out_T(NT - 1)

        silu_tanh = sem("silu_tanh")
        knorm = sb("knorm", [P, B * H, TPS])
        kd = part(1, [P, NT, D])
        order_exp = sb("order_exp", [P, TPS])

        def tensor_out(pe, n):
            s, at = LS, AT[n]
            for t in range(NT):
                if t >= 2:
                    pe.wait_ge(s["aoT_ready"], at["aoT_ready"] + t - 1)
                for k in range(KD):
                    last = nc.tensor.transpose(bank[t % 2][:, k * P:(k + 1) * P], ao[:, t, k * P:(k + 1) * P], ident[:])
                last.then_inc(s["ao_T"], 1)
                if t:
                    tensor_out_product(pe, n, t - 1)
            tensor_out_product(pe, n, NT - 1)

        def tensor_out_product(pe, n, t):
            s, at = LS, AT[n]
            pe.wait_ge(s["aoT_ready"], at["aoT_ready"] + t + 1)
            if t >= 2:
                pe.wait_ge(s["o_added"], at["o_added"] + t - 1)
            for k in range(KD):
                last = mm(bank[2 + t % 2][:, 0:D], aoT[:, k, t * P:(t + 1) * P], wo[n][:, k, :], k == 0, k == KD - 1)
            last.then_inc(s["o_ready"], 1)

        def scalar_out(act, n):
            s, at = LS, AT[n]
            for t in range(NT):
                act.wait_ge(s["ao_T"], at["ao_T"] + t + 1)
                act.activation(aoT[:, :, t * P:(t + 1) * P], bank[t % 2][:, 0:D].rearrange("p (k t) -> p k t", k=KD),
                               ACT.Copy).then_inc(s["aoT_ready"], 1)

        def vector_out(dve, n):
            s, at = LS, AT[n]
            if n == 0:
                dve.tensor_tensor(x[:], x[:], bo[:].unsqueeze(1).to_broadcast([P, NT, D]), ALU.add)
                dve.drain()
            for t in range(NT):
                dve.wait_ge(s["o_ready"], at["o_ready"] + t + 1)
                dve.tensor_tensor(x[:, t, :], x[:, t, :], bank[2 + t % 2][:, 0:D], ALU.add).then_inc(s["o_added"], 1)

        SB, FB, TB, OB = 0, 4, 6, 7
        U = 2 * TPS
        qm = [part(0, [P, S]) for i in range(2)]
        eA = part(0, [P, 2, S])
        eP = [part(0, [P, S]) for i in range(2)]
        eT = [part(0, [P, S]) for i in range(2)]
        row8 = sb("row8", [P, 3, U])
        nbias = sb("nbias", [P, 4, 2])
        cpair = sb("cpair", [P, 2, 2])
        neg_max_all = sb("neg_max", [P, B * H + 2, TPS])
        neg_max = neg_max_all[:, 2:, :]
        sum_exp_all = sb("sum_exp", [P, B * H + 2, TPS])
        sum_exp = sum_exp_all[:, 2:, :]
        sum_es_all = sb("sum_es", [P, B * H + 2, TPS])
        sum_es = sum_es_all[:, 2:, :]
        sum_diff_all = sb("sum_diff", [P, B * H + 2, TPS])
        sum_diff = sum_diff_all[:, 2:, :]
        sum_s_all = sb("sum_s", [P, B * H + 2, TPS])
        sum_s = sum_s_all[:, 2:, :]
        AS = {k: sem(k) for k in ("qm_ready", "score_ready", "diff_ready", "bias_ready", "expP_ready",
                                  "scores_summed", "diff_read", "mean_read", "turned", "eT_ready", "head_ready",
                                  "head_copied")}
        CREDIT = {"score_ready": 8, "diff_ready": 8, "expP_ready": 4, "scores_summed": 3, "diff_read": 2,
                  "mean_read": 2, "turned": 1, "eT_ready": 1, "head_copied": 1}
        TILES = H * B * TPS
        HEADS_AT = [dict.fromkeys(AS, 0), None,
                    dict.fromkeys(AS, TILES) | {"qm_ready": H * B, "head_ready": H * B + 1, "head_copied": H * B + 2,
                                                "turned": TILES + 1, "eT_ready": TILES + 1}]

        def head_loops(eng, body):
            with eng.Fori(0, B * NG) as bg:
                with eng.Fori(0, GH // 2) as hp:
                    body(bg, hp, bg * (GH // 2) + hp)

        def head_credits(eng, n, names):
            if n == 0:
                for k in names:
                    eng.drain().then_inc(AS[k], CREDIT[k])

        def tensor_heads(pe, n):
            s, at = AS, HEADS_AT[n]
            head_credits(pe, n, ("score_ready", "diff_ready", "turned"))

            def score(bg, i, u):
                hh, j = u // TPS, u % TPS
                if j == 0:
                    pe.wait_ge(s["qm_ready"], at["qm_ready"] + i * 2 + hh + 1)
                w = S if n == 0 else (j + 1) * P
                q = qm[hh][:, j * P:(j + 1) * P]
                pe.wait_ge(s["expP_ready"], at["expP_ready"] + i * U + u + 1)
                if n == 0:
                    pe.wait_ge(s["scores_summed"], at["scores_summed"] + i * U + u + 1)
                last = mm(bank[SB + u % 4][:, 0:w], q, kT[:, bass.ds(bg, 1), 0:w], True, n == 0)
                if n == 2:
                    last = mm(bank[SB + u % 4][:, j * P:w], ident[:], causal[:], False, True)
                last.then_inc(s["score_ready"], 1)
                if n == 0:
                    pe.wait_ge(s["diff_read"], at["diff_read"] + i * U + u + 1)
                    pe.wait_ge(s["mean_read"], at["mean_read"] + i * U + u + 1)
                    mm(bank[FB + u % 2][:], q, kdT[:, bass.ds(bg, 1), :]).then_inc(s["diff_ready"], 1)

            def turn(i, u):
                j = u % TPS
                pe.wait_ge(s["expP_ready"], at["expP_ready"] + i * U + u + 5)
                pe.wait_ge(s["eT_ready"], at["eT_ready"] + i * U + u + 2)
                for c in range(TPS if n == 0 else j + 1):
                    last = nc.tensor.transpose(bank[TB][:, c * P:(c + 1) * P], eP[u % 2][:, c * P:(c + 1) * P], ident[:])
                last.then_inc(s["turned"], 1)

            def weigh(i, u):
                hh, j = u // TPS, u % TPS
                pe.wait_ge(s["eT_ready"], at["eT_ready"] + i * U + u + 3)
                if j == 0:
                    pe.wait_ge(s["head_copied"], at["head_copied"] + i * 2 + hh + 2)
                last_c = TPS - 1 if n == 0 else j
                for c in range(last_c + 1):
                    last = mm(bank[OB][:, j * VW:(j + 1) * VW], eT[u % 2][:, c * P:(c + 1) * P],
                              v[:, bass.ds(i * 2 + hh + 2, 1), c, :], c == 0, c == last_c)
                if j == TPS - 1:
                    last.then_inc(s["head_ready"], 1)

            def body(bg, hp, i):
                for u in range(U):
                    score(bg, i, u)
                    turn(i, u - 1)
                    weigh(i, u - 2)

            pe.wait_ge(s["mean_read" if n == 0 else "head_copied"], at["mean_read" if n == 0 else "head_copied"] + 1)
            head_loops(pe, body)
            end = B * H // 2
            turn(end, -1)
            weigh(end, -2)
            weigh(end, -1)

        def pool_heads(pool, n):
            s, at = AS, HEADS_AT[n]

            def body(bg, hp, i):
                for hh in range(2):
                    k = "diff_ready" if n == 0 else "score_ready"
                    pool.wait_ge(s[k], at[k] + (i * 2 + hh) * TPS + TPS)
                    pool.tensor_tensor(qm[hh], qT[:, bass.ds(bg, 1), :].rearrange("p a s -> p (a s)"),
                                       head_mask[:, bass.ds(hp * 2 + hh, 1)].to_broadcast([P, S]), ALU.mult
                                       ).then_inc(s["qm_ready"], 1)

            head_loops(pool, body)

        def scalar_heads(act, n):
            s, at = AS, HEADS_AT[n]
            head_credits(act, n, ("expP_ready", "diff_read"))

            def body(bg, hp, i):
                for u in range(U):
                    hh, j = u // TPS, u % TPS
                    w = S if n == 0 else (j + 1) * P
                    row = (slice(None), bass.ds(i * 2 + hh + 2, 1), slice(j, j + 1))
                    act.wait_ge(s["bias_ready"], at["bias_ready"] + i * U + u + 1)
                    if n == 0:
                        act.wait_ge(s["scores_summed"], at["scores_summed"] + i * U + u + 3)
                        act.activation(eA[:, u % 2, :], bank[SB + u % 4][:], ACT.Exp, bias=nbias[:, u % 4, 0:1],
                                       scale=HD ** -0.5, accum_out=sum_exp_all[row])
                    act.wait_ge(s["turned"], at["turned"] + i * U + u + 1)
                    act.activation(eP[u % 2][:, 0:w], bank[SB + u % 4][:, 0:w], ACT.Exp, bias=nbias[:, u % 4, 1:2],
                                   scale=cpair[:, n // 2, 1:2]).then_inc(s["expP_ready"], 1)
                    if n == 0:
                        act.wait_ge(s["mean_read"], at["mean_read"] + i * U + u + 3)
                        act.activation(bank[FB + u % 2][:, 0:S - 1], bank[FB + u % 2][:, 0:S - 1], ACT.Abs,
                                       accum_out=sum_diff_all[row]).then_inc(s["diff_read"], 1)

            head_loops(act, body)

        def vector_heads(dve, n):
            s, at = AS, HEADS_AT[n]
            for z in (eP[1], eT[0], eT[1], v[:, 0:2, :, :], bank[OB][:, 0:TPS * VW], bank[SB + 3][:], eA[:, 1, :],
                      row8[:]):
                dve.memset(z, 0.0)
            head_credits(dve, n, ("head_copied", "eT_ready", "scores_summed", "mean_read"))
            if n == 2:
                dve.drain().then_inc(s["head_copied"], 1)

            def maximum(i, u):
                j = u % TPS
                w = S if n == 0 else (j + 1) * P
                dve.wait_ge(s["score_ready"], at["score_ready"] + i * U + u + 9)
                dve.tensor_reduce(row8[:, 0, u:u + 1], bank[SB + u % 4][:, 0:w], AX.X, ALU.max, negate=True)
                dve.drain()
                dve.tensor_tensor(nbias[:, u % 4, :], row8[:, 0, u:u + 1].to_broadcast([P, 2]), cpair[:, n // 2, :],
                                  ALU.mult).then_inc(s["bias_ready"], 1)
                if n == 0:
                    dve.wait_ge(s["diff_ready"], at["diff_ready"] + i * U + u + 9)
                    dve.tensor_copy(row8[:, 2, u:u + 1], bank[FB + u % 2][:, S - 1:S]).then_inc(s["mean_read"], 1)

            def entropy(i, u):
                dve.wait_ge(s["expP_ready"], at["expP_ready"] + i * U + u + 5)
                dve.tensor_tensor_reduce(eA[:, u % 2, :], eA[:, u % 2, :], bank[SB + u % 4][:], 1.0, 0.0, ALU.mult,
                                         ALU.add, row8[:, 1, u % U:u % U + 1]).then_inc(s["scores_summed"], 1)

            def copy_T(i, u):
                j = u % TPS
                w = S if n == 0 else (j + 1) * P
                dve.wait_ge(s["turned"], at["turned"] + i * U + u + 3)
                dve.tensor_copy(eT[u % 2][:, 0:w], bank[TB][:, 0:w]).then_inc(s["eT_ready"], 1)

            def copy_head(i, hh):
                dve.wait_ge(s["head_ready"], at["head_ready"] + i * 2 + hh + 2)
                dve.tensor_copy(raw[:, bass.ds(i * 2 + hh + 2, 1), :, :],
                                bank[OB][:, 0:TPS * VW].rearrange("p (o j e) -> p o j e", o=1, e=VW)
                                ).then_inc(s["head_copied"], 1)

            def keep(q, stat, i):
                dve.tensor_copy(stat[:, bass.ds(i * 2 + 2, 2), :], row8[:, q, :].rearrange("p (h j) -> p h j", j=TPS))

            def body(bg, hp, i):
                for u in range(U):
                    if u == 2:
                        copy_head(i, -1)
                    if u == TPS + 2:
                        copy_head(i, 0)
                    maximum(i, u)
                    if n == 0:
                        entropy(i, u - 1)
                    copy_T(i, u - 1)
                    if n == 0 and u == 0:
                        dve.drain()
                        keep(1, sum_es_all, i - 1)
                if n == 0:
                    dve.drain()
                    keep(0, neg_max_all, i)
                    keep(2, sum_s_all, i)
                    dve.drain()

            head_loops(dve, body)
            end = B * H // 2
            if n == 0:
                entropy(end, -1)
            copy_T(end, -1)
            if n == 0:
                dve.drain()
                keep(1, sum_es_all, end - 1)
            copy_head(end, -1)

        rowc = sb("rowc", [P, B * H, TPS])
        rowt = sb("rowt", [P, B * H, TPS])
        rowu = sb("rowu", [P, B * H, TPS])
        lnz = sb("lnz", [P, B * H, TPS])
        rfac = sb("rfac", [P, B * H, TPS])
        half_pos = sb("half_pos", [P, NT * H])
        zeros = sb("zeros", [P, 1])
        lnz_ready = sem("lnz_ready")
        kn_ready = sem("kn_ready")
        row_ready = sem("row_ready")
        fac_ready = sem("fac_ready")
        gate_exp = sem("gate_exp")
        gates_ready = sem("gates_ready")
        order_ready = sem("order_ready")
        order_pos = sb("order_pos", [P, TPS])
        gt = sb("gt", [P, 16])

        def scalar_gates(act):
            act.wait_ge(loaded[0], LOADS[0])
            act.activation(gt[:, 0:5], gates[:], ACT.Exp, scale=-1.0).then_inc(gate_exp, 1)
            act.wait_ge(gates_ready, 1)
            act.activation(order_exp[:], order_pos[:], ACT.Exp, scale=gt[:, 7:8]).then_inc(order_ready, 1)

        def vector_gates(dve):
            dve.wait_ge(gate_exp, 1)
            dve.tensor_scalar(gt[:, 0:5], gt[:, 0:5], 1.0, None, ALU.add)
            dve.drain()
            dve.reciprocal(gt[:, 5:10], gt[:, 0:5])
            dve.drain()
            dve.tensor_scalar(cpair[:, 0, 1:2], gt[:, 8:9], -0.1 * HD ** -0.5, HD ** -0.5, ALU.mult, ALU.add)
            dve.memset(cpair[:, 0, 0:1], HD ** -0.5)
            dve.memset(cpair[:, 1, :], HD ** -0.5)
            dve.memset(half_neg[:], -0.5)
            dve.memset(half_pos[:], 0.5)
            dve.memset(comb[:], 0.0)
            dve.tensor_copy(identb[:], ident[:])
            dve.drain().then_inc(gates_ready, 1)
            dve.wait_ge(order_ready, 1)

        def vector_diffs(dve):
            for bg in range(B * NG):
                dve.tensor_tensor(kdT[:, bg, 0:S - 1], kT[:, bg, 1:S], kT[:, bg, 0:S - 1], ALU.subtract)
                dve.tensor_reduce(kdT[:, bg, S - 1:S], kT[:, bg, :], AX.X, ALU.add)

        def pool_rows(pool):
            pool.tensor_tensor(knorm[:].rearrange("p h t -> p (h t)"), knorm[:].rearrange("p h t -> p (h t)"),
                               half_pos[:], ALU.pow).then_inc(kn_ready, 1)

        def scalar_rows(act):
            act.activation(lnz[:], sum_exp, ACT.Ln).then_inc(lnz_ready, 1)
            act.wait_ge(row_ready, 1)
            act.activation(rfac[:], rowt[:], ACT.Exp).then_inc(fac_ready, 1)

        def vector_rows(dve):
            isq = HD ** -0.5
            dve.reciprocal(rowu[:], sum_exp)
            dve.drain()
            dve.tensor_tensor(rowu[:], rowu[:], sum_es, ALU.mult)
            dve.drain()
            dve.tensor_tensor(rowu[:], rowu[:], neg_max, ALU.add)
            dve.wait_ge(lnz_ready, 1)
            dve.drain()
            dve.tensor_scalar(rowu[:], rowu[:], isq, None, ALU.mult)
            dve.drain()
            dve.tensor_tensor(rowu[:], rowu[:], lnz[:], ALU.subtract)
            dve.drain()
            dve.tensor_scalar(rowu[:], rowu[:], gt[:, 6:7], -0.1 / LN_S, ALU.mult, ALU.mult)
            dve.wait_ge(kn_ready, 1)
            dve.tensor_scalar(rowt[:], knorm[:], gt[:, 5:6], -0.01, ALU.mult, ALU.mult)
            dve.drain()
            dve.tensor_tensor(rowc[:], rowu[:], rowt[:], ALU.add)
            dve.drain()
            dve.tensor_scalar(rowu[:], sum_s, gt[:, 8:9], 0.1 * isq / S, ALU.mult, ALU.mult)
            dve.drain()
            dve.tensor_tensor(rowc[:], rowc[:], rowu[:], ALU.add)
            dve.drain()
            dve.tensor_scalar(rowt[:], sum_diff, gt[:, 9:10], -0.1 * isq / (S - 1), ALU.mult, ALU.mult)
            dve.drain()
            dve.tensor_tensor(rowc[:], rowc[:], rowt[:], ALU.add)
            dve.drain()
            dve.tensor_scalar(rowu[:], neg_max, cpair[:, 0, 1:2], -1.0, ALU.mult, ALU.mult)
            dve.drain()
            dve.tensor_tensor(lnz[:], rowc[:], rowu[:], ALU.add)
            dve.drain()
            dve.tensor_tensor(rowt[:], rowc[:], lnz[:], ALU.subtract)
            dve.drain()
            dve.tensor_tensor(rowt[:], rowt[:], rowu[:], ALU.add).then_inc(row_ready, 1)
            dve.wait_ge(fac_ready, 1)
            for t in range(NT):
                r = raw[:, 2:, :, :][:, heads_of(t), t % TPS, :]
                dve.tensor_tensor(r, r, rfac[:, heads_of(t), t % TPS].unsqueeze(2).to_broadcast([P, H, VW]), ALU.mult)
            dve.drain()
            vector_divide(dve)

        def vector_divide(dve):
            dve.reciprocal(rowu[:], raw[:, 2:, :, HD])
            dve.drain()
            for t in range(NT):
                dve.tensor_tensor(ao[:, t, :].rearrange("p (h e) -> p h e", e=HD), 
                                  raw[:, 2:, :, :][:, heads_of(t), t % TPS, 0:HD],
                                  rowu[:, heads_of(t), t % TPS].unsqueeze(2).to_broadcast([P, H, HD]), ALU.mult)

        qx = part(1, [P, 2, GH, P])
        sD = [part(1, [P, 4 * P]) for i in range(4)]
        state = part(1, [P, NG, P])
        stmp = part(1, [P, NG, P])
        g1T = part(1, [P, TOK])[0:HD, :]
        gsig = part(1, [P, 2, D])
        ms = sb("ms", [P, NT, H])
        L1 = {k: sem(f"lin_{k}") for k in ("g1_ready", "g1_copied", "qx_ready", "qx_used", "sc_ready", "sc_masked",
                                            "own_ready", "own_read", "st_ready", "st_done", "gate_ready", "gate_th",
                                            "gate_read", "ms_ready", "ms_root")}

        def tensor_linear(pe):
            s = L1
            for c in range(2):
                for k in range(KD):
                    last = mm(bank[c][0:HD, :], wg1[:, k, :], xnT[:, k, c * 512:(c + 1) * 512], k == 0, k == KD - 1)
                last.then_inc(s["g1_ready"], 1)
            pe.wait_ge(s["g1_copied"], 2)
            for t in range(NT):
                first = t % TPS == 0
                ts = slice(t * P, (t + 1) * P)
                if t:
                    pe.wait_ge(s["gate_read"], t)
                mm(bank[7][:, 0:D], g1T[:, ts], wg2[:]).then_inc(s["gate_ready"], 1)
                for g in range(NG):
                    pe.wait_ge(s["qx_ready"], t * NG + g + 1)
                    if t:
                        pe.wait_ge(s["sc_masked"], 2 * ((t - 1) * NG + g + 1))
                    for c in range(2):
                        last = mm(bank[2 * g + c][:], kT[group_of(t)][:, g, :],
                                  qx[:, g, 4 * c:4 * c + 4, :].rearrange("p h t -> p (h t)"))
                    last.then_inc(s["sc_ready"], 1)
                if t:
                    pe.wait_ge(s["own_read"], t)
                if not first:
                    pe.wait_ge(s["st_done"], t)
                    for g in range(NG):
                        mm(bank[5][:, g * P:(g + 1) * P], qT[group_of(t)][:, g, :], state[:, g, :])
                for g in range(NG):
                    pe.wait_ge(s["sc_masked"], 2 * (t * NG + g + 1))
                    for hh in range(GH):
                        h = g * GH + hh
                        last = mm(bank[4][:, h * HD:(h + 1) * HD], sD[2 * g + hh // 4][:, (hh % 4) * P:(hh % 4 + 1) * P],
                                  v_of(t, h, 1)[:, 0, 0:HD])
                last.then_inc(s["own_ready"], 1)
                if t:
                    pe.wait_ge(s["st_done"], t)
                for g in range(NG):
                    last = mm(bank[6][:, g * P:(g + 1) * P], kd[:, t, g * P:(g + 1) * P], v_of(t, g * GH, GH)[:, :, 0:HD])
                last.then_inc(s["st_ready"], 1)

        def scalar_linear(act):
            s = L1
            for c in range(2):
                act.wait_ge(s["g1_ready"], c + 1)
                act.activation(g1T[:, c * 512:(c + 1) * 512], bank[c][0:HD, :], ACT.Copy).then_inc(s["g1_copied"], 1)
            for t in range(NT):
                act.wait_ge(s["gate_ready"], t + 1)
                if t >= 2:
                    act.wait_ge(s["own_read"], t - 1)
                act.activation(gsig[:, t % 2, :], bank[7][:, 0:D], ACT.Tanh, scale=0.5).then_inc(s["gate_read"], 1)

        def vector_linear(dve):
            s = L1
            for t in range(NT):
                first = t % TPS == 0
                ts = slice(t * P, (t + 1) * P)
                for g in range(NG):
                    if t:
                        dve.wait_ge(s["sc_ready"], (t - 1) * NG + g + 1)
                    dve.tensor_tensor(qx[:, g, :, :], qT[group_of(t)][:, g, :].unsqueeze(1).to_broadcast([P, GH, P]),
                                      head_mask[:].unsqueeze(2).to_broadcast([P, GH, P]), ALU.mult
                                      ).then_inc(s["qx_ready"], 1)
                if t:
                    dve.wait_ge(s["own_ready"], t)
                for g in range(NG):
                    dve.wait_ge(s["sc_ready"], t * NG + g + 1)
                    for c in range(2):
                        h = g * GH + 4 * c
                        dve.tensor_tensor(sD[2 * g + c][:], bank[2 * g + c][:],
                                          decay[:, h:h + 4, :].rearrange("p h t -> p (h t)"), ALU.mult
                                          ).then_inc(s["sc_masked"], 1)
                dve.wait_ge(s["st_ready"], t + 1)
                new = bank[6][:, 0:D].rearrange("p (g e) -> p g e", g=NG)
                dve.tensor_tensor(stmp[:], new, own_block[:].unsqueeze(1).to_broadcast([P, NG, P]), ALU.mult)
                if first:
                    dve.drain()
                    dve.tensor_copy(state[:], stmp[:]).then_inc(s["st_done"], 1)
                else:
                    dve.tensor_tensor(state[:], state[:], lam_chunk[:], ALU.mult)
                    dve.drain()
                    dve.tensor_tensor(state[:], state[:], stmp[:], ALU.add).then_inc(s["st_done"], 1)
                dve.wait_ge(s["own_ready"], t + 1)
                o = ao[:, t, :].rearrange("p (h e) -> p h e", e=HD)
                if first:
                    dve.tensor_copy(ao[:, t, :], bank[4][:, 0:D])
                else:
                    dve.tensor_tensor(o, bank[5][:, 0:D].rearrange("p (h e) -> p h e", e=HD),
                                      decay_q[:].unsqueeze(2).to_broadcast([P, H, HD]), ALU.mult)
                    dve.drain()
                    dve.tensor_tensor(ao[:, t, :], ao[:, t, :], bank[4][:, 0:D], ALU.add)
                dve.drain()
                dve.wait_ge(s["gate_read"], t + 1)
                dve.scalar_tensor_tensor(ao[:, t, :], gsig[:, t % 2, :], 1.0, ao[:, t, :], ALU.add, ALU.mult
                                         ).then_inc(s["own_read"], 1)
                dve.drain()
                dve.tensor_tensor(tmp[:, 0, 0:D], ao[:, t, :], ao[:, t, :], ALU.mult)
                dve.drain()
                dve.tensor_reduce(ms[:, t, :], tmp[:, 0, 0:D].rearrange("p (h e) -> p h e", e=HD), AX.X, ALU.add)
            dve.drain()
            dve.tensor_scalar(ms[:], ms[:], 0.25 / HD, 1e-6, ALU.mult, ALU.add).then_inc(s["ms_ready"], 1)
            dve.wait_ge(s["ms_root"], 1)
            for t in range(NT):
                o = ao[:, t, :].rearrange("p (h e) -> p h e", e=HD)
                dve.tensor_tensor(o, o, ms[:, t, :].unsqueeze(2).to_broadcast([P, H, HD]), ALU.mult)
            dve.drain()
            for t in range(NT):
                dve.scalar_tensor_tensor(ao[:, t, :], ao[:, t, :], 0.5, norm_w[:], ALU.mult, ALU.mult)

        def pool_linear(pool):
            pool.wait_ge(L1["ms_ready"], 1)
            pool.tensor_tensor(ms[:].rearrange("p t h -> p (t h)"), ms[:].rearrange("p t h -> p (t h)"), half_neg[:],
                               ALU.pow).then_inc(L1["ms_root"], 1)

        def vector_route(dve, n):
            s, at = LS, AT[n]
            E = EXPERTS[n]
            if n == 3:
                for t in range(NT):
                    dve.wait_ge(s["logits_ready"], at["logits_ready"] + t + 1)
                    dve.tensor_copy(logits[:, t, 0:16], bank[t % 2][:, 0:16])
                    dve.tensor_copy(shared[:, t:t + 1], bank[t % 2][:, 16:17])
                    dve.drain().then_inc(s["logits_copied"], 1)
            lg, pr, cm = logits[:, :, 0:E], probs[:, :, 0:E], comb[:, :, 0:E]

            def wide(r):
                return r[:].unsqueeze(2).to_broadcast([P, NT, E])

            dve.drain()
            dve.tensor_reduce(rowm[:], lg, AX.X, ALU.max)
            dve.drain()
            dve.tensor_tensor(pr, lg, wide(rowm), ALU.subtract)
            dve.drain().then_inc(s["route_exp"], 1)
            dve.wait_ge(s["route_exp"], at["route_exp"] + 2)
            if n != 2:
                dve.tensor_reduce(rowz[:], pr, AX.X, ALU.add)
                dve.drain()
                dve.reciprocal(rowz[:], rowz[:])
                dve.drain()
                dve.tensor_tensor(pr, pr, wide(rowz), ALU.mult)
                dve.drain()
            key = lg if n == 2 else pr
            for t in range(NT):
                ahead = key[:, t, :].unsqueeze(1).to_broadcast([P, E, E])
                own = key[:, t, :].unsqueeze(2).to_broadcast([P, E, E])
                dve.tensor_tensor(rank[:, 0:E, 0:E], ahead, own, ALU.is_gt)
                dve.tensor_tensor(rank2[:, 0:E, 0:E], ahead, own, ALU.is_equal)
                dve.drain()
                dve.tensor_tensor(rank2[:, 0:E, 0:E], rank2[:, 0:E, 0:E], lower[:, 0:E, 0:E], ALU.mult)
                dve.drain()
                dve.tensor_tensor(rank[:, 0:E, 0:E], rank[:, 0:E, 0:E], rank2[:, 0:E, 0:E], ALU.add)
                dve.drain()
                dve.tensor_reduce(rankn[:, t, 0:E], rank[:, 0:E, 0:E], AX.X, ALU.add)
                dve.drain()
            dve.tensor_scalar(rankn[:, :, 0:E], rankn[:, :, 0:E], float(TOPK[n]), None, ALU.is_lt)
            dve.drain()
            dve.tensor_tensor(cm, rankn[:, :, 0:E], pr, ALU.mult)
            dve.drain()
            if n != 1:
                dve.tensor_reduce(rowz[:], cm, AX.X, ALU.add)
                dve.drain()
                dve.reciprocal(rowz[:], rowz[:])
                dve.drain()
                dve.tensor_tensor(cm, cm, wide(rowz), ALU.mult)
                dve.drain()
            dve.tensor_scalar(cm, cm, 0.5, None, ALU.mult)
            if n == 1:
                dve.memset(comb[:, :, E:E + 1], 0.5)
            if n == 2:
                dve.memset(comb[:, :, E:E + 1], 0.0)
            if n == 3:
                dve.tensor_scalar(comb[:, :, E], shared[:], 1.0, 0.25, ALU.add, ALU.mult)
            dve.drain()
            hi, mid, lo = (combp[:, :, i * NE:(i + 1) * NE] for i in range(3))
            rest = rank[:].rearrange("p a b -> p (a b)")[:, 0:NT * NE].rearrange("p (t e) -> p t e", e=NE)
            dve.tensor_copy(hi, comb[:])
            dve.drain()
            dve.tensor_tensor(rest, comb[:], hi, ALU.subtract)
            dve.drain()
            dve.tensor_copy(mid, rest)
            dve.drain()
            dve.tensor_tensor(lo, rest, mid, ALU.subtract)
            dve.drain().then_inc(s["comb_T"], 1)
            dve.wait_ge(s["comb_T"], at["comb_T"] + 2)
            dve.tensor_copy(combT[:], bankb)
            if n == 2:
                dve.wait_ge(s["comb_T"], at["comb_T"] + 3)
                dve.tensor_copy(combF[0:8, :], bank[6][0:8, :])
                dve.tensor_copy(combF2[0:8, :], bank[7][0:8, :])
                dve.drain()

        bankb = bank[5][0:CR, :].bitcast(BF16)
        combF = sb("combF", [8, 512])
        combF2 = sb("combF2", [8, 512])

        def scalar_route(act, n):
            s, at = LS, AT[n]
            E = EXPERTS[n]
            act.wait_ge(s["route_exp"], at["route_exp"] + 1)
            act.activation(probs[:, :, 0:E], probs[:, :, 0:E], ACT.Exp)
            if n == 3:
                act.activation(shared[:], shared[:], ACT.Tanh, scale=0.5)
            act.drain().then_inc(s["route_exp"], 1)

        def tensor_route(pe, n):
            s, at = LS, AT[n]
            if n == 3:
                for t in range(NT):
                    if t >= 2:
                        pe.wait_ge(s["logits_copied"], at["logits_copied"] + t - 1)
                    for k in range(KD):
                        last = mm(bank[t % 2][:, 0:NE], xnT[:, k, t * P:(t + 1) * P], router[3][:, k, :],
                                  k == 0, k == KD - 1)
                    last.then_inc(s["logits_ready"], 1)
            pe.wait_ge(s["comb_T"], at["comb_T"] + 1)
            for t in range(NT):
                last = nc.tensor.transpose(bankb[:, t * P:(t + 1) * P], combp[:, t, :], identb[:])
            last.then_inc(s["comb_T"], 1)
            if n == 2:
                for t in range(NT):
                    last = nc.tensor.transpose(bank[6 + t // 4][0:8, (t % 4) * P:(t % 4 + 1) * P], comb[:, t, 0:8], ident[:])
                last.then_inc(s["comb_T"], 1)

        GB, UB, CB, DB = 4, 5, 6, 7

        def sync_ffn(sp, n, first, count):
            s, at = LS, AT[n]
            base = sum(CHUNKS[:n])
            with sp.Fori(first, first + count) as p:
                sp.wait_ge(s["guA_used"], at["guA_used"] + p + 1)
                sp.dma_start(wgu[0][:], a["gu"][bass.ds(p * 2 + base, 1), :, :].rearrange("a p n -> (a p) n")).then_inc(s["guA_loaded"], 16)
                if n:
                    sp.dma_start(sel[0][:], a[f"sel{n}"][bass.ds(p * 2, 1), :, :].rearrange("a p n -> (a p) n")).then_inc(s["guA_loaded"], 16)
                sp.wait_ge(s["guB_used"], at["guB_used"] + p + 1)
                sp.dma_start(wgu[1][:], a["gu"][bass.ds(p * 2 + base + 1, 1), :, :].rearrange("a p n -> (a p) n")).then_inc(s["guB_loaded"], 16)
                if n:
                    sp.dma_start(sel[1][:], a[f"sel{n}"][bass.ds(p * 2 + 1, 1), :, :].rearrange("a p n -> (a p) n")).then_inc(s["guB_loaded"], 16)
                sp.wait_ge(s["down_used"], at["down_used"] + p + 1)
                sp.dma_start(wd[:], a["down"][bass.ds(p * 2 + base, 2), :, :].rearrange("a p n -> p a n")).then_inc(s["down_loaded"], 16)

        def tensor_ffn_start(pe, n):
            s, at = LS, AT[n]
            if n == 0:
                for k in ("guA_used", "guB_used", "down_used"):
                    pe.drain().then_inc(s[k], 1)

        def tensor_ffn_pair(pe, n, p):
            s, at = LS, AT[n]
            inc = 32 if n else 16

            def gate_up(u):
                half, c = u // 2, u % 2
                if half == 0:
                    pe.wait_ge(s["guB_loaded" if c else "guA_loaded"], at["guA_loaded"] + p * inc + inc)
                ts = slice(half * 512, half * 512 + 512)
                pe.wait_ge(s["gate_used"], at["gate_used"] + p * 4 + u + 1)
                for k in range(KD):
                    last = mm(bank[GB][:], wgu[c][:, k * P:(k + 1) * P], xnT[:, k, ts], k == 0, k == KD - 1)
                last.then_inc(s["gate_ready"], 1)
                pe.wait_ge(s["up_used"], at["up_used"] + p * 4 + u + 1)
                for k in range(KD):
                    last = mm(bank[UB][:], wgu[c][:, (2 + k) * P:(3 + k) * P], xnT[:, k, ts], k == 0, k == KD - 1)
                last.then_inc(s["up_ready"], 1)
                if n:
                    pe.wait_ge(s["comb_used"], at["comb_used"] + p * 4 + u + 1)
                    last = mm(bank[CB][:], sel[c][:], combT[:, ts])
                    last.then_inc(s["comb_ready"], 1)
                if half == 1:
                    pe.drain().then_inc(s["guB_used" if c else "guA_used"], 1)

            def down(half):
                if half == 0:
                    pe.wait_ge(s["down_loaded"], at["down_loaded"] + p * 16 + 16)
                pe.wait_ge(s["h_ready"], at["h_ready"] + p * 4 + 2 * half + 2)
                for q in range(2):
                    pe.wait_ge(s["part_added"], at["part_added"] + p * 4 + 2 * half + q + 1)
                    for r in range(2):
                        t = 2 * q + r
                        for c in range(2):
                            last = mm(bank[DB][:, r * D:(r + 1) * D], hT[:, 2 * half + c, t * P:(t + 1) * P], wd[:, c, :],
                                      c == 0, c == 1)
                    last.then_inc(s["part_ready"], 1)

            gate_up(0)
            gate_up(1)
            gate_up(2)
            down(0)
            gate_up(3)
            down(1)
            pe.drain().then_inc(s["down_used"], 1)

        def scalar_ffn_pair(act, n, p):
            s, at = LS, AT[n]
            for u in range(4):
                if n == 2:
                    act.wait_ge(s["gate_clipped"], at["gate_clipped"] + p * 4 + u + 1)
                    act.activation(th[:, u % 2, :], gl[:, u % 2, :], ACT.Tanh, scale=0.5 * 1.702).then_inc(s["tanh_ready"], 1)
                else:
                    act.wait_ge(s["gate_ready"], at["gate_ready"] + p * 4 + u + 1)
                    act.wait_ge(s["gate_used"], at["gate_used"] + p * 4 + u + 1)
                    act.activation(th[:, u % 2, :], bank[GB][:], ACT.Tanh, scale=0.5).then_inc(s["tanh_ready"], 1)

        def vector_ffn_start(dve, n):
            s, at = LS, AT[n]
            if n == 0:
                for k in ("gate_used", "up_used", "part_added", "comb_used"):
                    dve.drain().then_inc(s[k], 1)

        def vector_ffn_pair(dve, n, p):
            s, at = LS, AT[n]

            def unit(u):
                i = u % 2
                h = hT[:, u, :]
                if n == 2:
                    bias = [gu_bias[:, bass.ds(p * 2 + u % 2, 1), c:c + 1] for c in (0, 1)]
                    dve.wait_ge(s["gate_ready"], at["gate_ready"] + p * 4 + u + 1)
                    dve.tensor_scalar(gl[:, i, :], bank[GB][:], bias[0], 7.0, ALU.add, ALU.min)
                    dve.drain().then_inc(s["gate_clipped"], 1)
                    dve.wait_ge(s["up_ready"], at["up_ready"] + p * 4 + u + 1)
                    dve.tensor_scalar(up[:, i, :], bank[UB][:], bias[1], 7.0, ALU.add, ALU.min)
                    dve.drain().then_inc(s["up_used"], 1)
                    dve.tensor_scalar(up[:, i, :], up[:, i, :], -7.0, 1.0, ALU.max, ALU.add)
                    dve.wait_ge(s["tanh_ready"], at["tanh_ready"] + p * 4 + u + 1)
                    dve.scalar_tensor_tensor(gl[:, i, :], th[:, i, :], 1.0, gl[:, i, :], ALU.add, ALU.mult)
                    dve.drain().then_inc(s["gate_used"], 1)
                    dve.tensor_tensor(gl[:, i, :], gl[:, i, :], up[:, i, :], ALU.mult)
                    dve.drain()
                else:
                    dve.wait_ge(s["tanh_ready"], at["tanh_ready"] + p * 4 + u + 1)
                    dve.scalar_tensor_tensor(gl[:, i, :], th[:, i, :], 1.0, bank[GB][:], ALU.add, ALU.mult
                                             ).then_inc(s["gate_used"], 1)
                    dve.drain()
                    dve.wait_ge(s["up_ready"], at["up_ready"] + p * 4 + u + 1)
                    if n == 0:
                        dve.scalar_tensor_tensor(h, gl[:, i, :], 0.5, bank[UB][:], ALU.mult, ALU.mult)
                        dve.drain().then_inc(s["up_used"], 1)
                    else:
                        dve.tensor_tensor(gl[:, i, :], gl[:, i, :], bank[UB][:], ALU.mult).then_inc(s["up_used"], 1)
                        dve.drain()
                if n:
                    dve.wait_ge(s["comb_ready"], at["comb_ready"] + p * 4 + u + 1)
                    dve.tensor_tensor(h, gl[:, i, :], bank[CB][:], ALU.mult)
                    dve.drain().then_inc(s["comb_used"], 1)
                dve.drain().then_inc(s["h_ready"], 1)

            def add(half):
                for q in range(2):
                    dve.wait_ge(s["part_ready"], at["part_ready"] + p * 4 + 2 * half + q + 1)
                    t = half * TPS + 2 * q
                    dve.tensor_tensor(x[:, t:t + 2, :], x[:, t:t + 2, :],
                                      bank[DB][:].rearrange("p (t n) -> p t n", n=D), ALU.add).then_inc(s["part_added"], 1)

            unit(0)
            unit(1)
            unit(2)
            add(0)
            unit(3)
            add(1)

        bias2_ready = sem("bias2_ready")
        bias2_added = sem("bias2_added")

        def tensor_bias2(pe):
            for t in range(NT):
                if t >= 2:
                    pe.wait_ge(bias2_added, t - 1)
                cf = (combF, combF2)[t // 4]
                mm(bank[t % 2][:, 0:D], cf[:, (t % 4) * P:(t % 4 + 1) * P], dbias[:]).then_inc(bias2_ready, 1)

        def vector_bias2(dve):
            for t in range(NT):
                dve.wait_ge(bias2_ready, t + 1)
                dve.scalar_tensor_tensor(x[:, t, :], bank[t % 2][:, 0:D], 2.0, x[:, t, :], ALU.mult, ALU.add
                                         ).then_inc(bias2_added, 1)

        wq3 = wpart(3, [P, KD, H3 * HD3])
        wk3 = wpart(3, [P, H3 * HD3])
        wv3 = wpart(3, [P, H3 * HD3])
        wo3 = wpart(3, [P, H3, D])
        mem = sb("mem", [P, 2, P])
        memT = sb("memT", [P, MEM])
        aff = sb("aff", [P, 6])
        lbeta = sb("lbeta", [P, H3])
        st3 = sb("st3", [P, NT + 2, 6])
        mv3 = sb("mv3", [P, NT + 2, 2])
        rs3 = sb("rs3", [P, NT + 2])
        nm3 = sb("nm3", [P, NT + 2])
        xn3 = part(3, [P, NT, D])
        K3 = part(3, [P, H3, MEM])
        V3 = part(3, [P, 2, H3 * HD3])
        xi = [part(3, [P, 512]) for i in range(2)]
        sc3 = [part(3, [P, TPS, MEM]) for i in range(2)]
        re3 = part(3, [P, 2, TPS, MEM])
        w3 = [part(3, [P, TPS, MEM]) for i in range(2)]
        wT3 = [part(3, [P, 2, 512]) for i in range(2)]
        mx3 = sb("mx3", [P, 2, TPS])
        tau = sb("tau", [P, 2, TPS])
        s1 = sb("s1", [P, 2, TPS])
        s2 = sb("s2", [P, 2, TPS])
        na = sb("na", [P, 2, TPS])
        nb = sb("nb", [P, 2, TPS])
        N3 = {k: sem(f"mem_{k}") for k in ("stats", "rstd", "normed", "turned", "copied", "kv_ready", "kv_copied",
                                            "beta", "q_ready", "xi_ready", "xi_used", "sc_ready", "sc_max", "shifted",
                                            "sums_ready", "tau_ready", "w_rel", "w_ready", "w_T", "wT_ready",
                                            "o_ready", "o_added", "norm1")}

        def scalar_norm3(act):
            for t in range(NT):
                act.activation(xn3[:, t, :], x[:, t, :], ACT.Identity, bias=nmr[:, t:t + 1], scale=rstd[:, t:t + 1])
            act.drain().then_inc(N3["norm1"], 1)
            act.activation(lbeta[:], lbeta[:], ACT.Exp)
            act.drain().then_inc(N3["beta"], 1)
            act.wait_ge(N3["rstd"], 1)
            for t in range(NT):
                act.activation(xn3[:, t, :], xn3[:, t, :], ACT.Identity, bias=nm3[:, t:t + 1], scale=rs3[:, t:t + 1]
                               ).then_inc(N3["normed"], 1)
            for m in range(2):
                act.activation(mem[:, m, :], mem[:, m, :], ACT.Identity, bias=nm3[:, NT + m:NT + m + 1],
                               scale=rs3[:, NT + m:NT + m + 1]).then_inc(N3["normed"], 1)

        def vector_norm3(dve):
            dve.wait_ge(N3["norm1"], 1)
            for t in range(NT):
                dve.bn_stats(st3[:, t, :], xn3[:, t, :])
            for m in range(2):
                dve.bn_stats(st3[:, NT + m, :], mem[:, m, :])
            dve.drain()
            for t in range(NT + 2):
                dve.bn_aggr(mv3[:, t, :], st3[:, t, :])
            dve.drain().then_inc(N3["stats"], 1)
            dve.wait_ge(N3["beta"], 1)
            dve.tensor_scalar(lbeta[:], lbeta[:], 0.5, None, ALU.mult)
            dve.drain()
            for t in range(NT):
                dve.wait_ge(N3["turned"], t + 1)
                for k in range(KD):
                    dve.tensor_scalar(aoT[:, k, t * P:(t + 1) * P], bank[t % 2][:, k * P:(k + 1) * P],
                                      aff[:, k:k + 1], aff[:, 2 + k:3 + k], ALU.mult, ALU.add)
                dve.drain().then_inc(N3["copied"], 1)
            dve.wait_ge(N3["turned"], NT + 1)
            dve.tensor_scalar(memT[:], bank[2][:, 0:MEM], aff[:, 4:5], aff[:, 5:6], ALU.mult, ALU.add)
            dve.drain().then_inc(N3["copied"], 1)
            for h in range(H3):
                dve.wait_ge(N3["kv_ready"], h + 1)
                dve.tensor_scalar(K3[:, h, :], bank[4 + h % 2][:, 0:MEM], lbeta[:, h:h + 1], None, ALU.mult
                                  ).then_inc(N3["kv_copied"], 1)
            for c in range(4):
                dve.wait_ge(N3["kv_ready"], H3 + c + 1)
                dve.tensor_copy(V3[:, c // 2, (c % 2) * 512:(c % 2 + 1) * 512], bank[4 + c % 2][:]
                                ).then_inc(N3["kv_copied"], 1)

        def pool_norm3(pool):
            pool.wait_ge(N3["stats"], 1)
            pool.tensor_scalar(rs3[:], mv3[:, :, 1], LN_EPS, None, ALU.add)
            pool.drain()
            pool.tensor_tensor(rs3[:], rs3[:], half_neg[:, 0:NT + 2], ALU.pow)
            pool.drain()
            pool.tensor_tensor(nm3[:], mv3[:, :, 0], rs3[:], ALU.mult)
            pool.drain()
            pool.tensor_scalar(nm3[:], nm3[:], -1.0, None, ALU.mult)
            pool.drain().then_inc(N3["rstd"], 1)

        def tensor_norm3(pe):
            for t in range(NT):
                pe.wait_ge(N3["normed"], t + 1)
                if t >= 2:
                    pe.wait_ge(N3["copied"], t - 1)
                for k in range(KD):
                    last = nc.tensor.transpose(bank[t % 2][:, k * P:(k + 1) * P], xn3[:, t, k * P:(k + 1) * P], ident[:])
                last.then_inc(N3["turned"], 1)
            pe.wait_ge(N3["normed"], NT + 2)
            for m in range(2):
                last = nc.tensor.transpose(bank[2][:, m * P:(m + 1) * P], mem[:, m, :], ident[:])
            last.then_inc(N3["turned"], 1)
            pe.wait_ge(N3["copied"], NT + 1)
            for h in range(H3):
                if h >= 2:
                    pe.wait_ge(N3["kv_copied"], h - 1)
                mm(bank[4 + h % 2][:, 0:MEM], wk3[:, h * HD3:(h + 1) * HD3], memT[:]).then_inc(N3["kv_ready"], 1)
            for c in range(4):
                pe.wait_ge(N3["kv_copied"], H3 + c - 1)
                mm(bank[4 + c % 2][:], memT[:, (c // 2) * P:(c // 2 + 1) * P], wv3[:, (c % 2) * 512:(c % 2 + 1) * 512]
                   ).then_inc(N3["kv_ready"], 1)

        wq_s = part(3, [P, KD, HD3])
        v3_s = part(3, [P, 2, HD3])
        wo3_s = part(3, [P, D])
        head3_ready = sem("mem_head_ready")
        head3_used = sem("mem_head_used")

        def tensor_attention3(pe, h):
            n = N3
            pe.wait_ge(head3_ready, h + 1)
            for i in range(2):
                pe.wait_ge(n["o_added"], h * 8 + 4 * i + 4)
                for k in range(KD):
                    last = mm(bank[2 * i][:], wq_s[:, k, :], aoT[:, k, i * 512:(i + 1) * 512], k == 0, k == KD - 1)
                last.then_inc(n["q_ready"], 1)
            for st in range(STEPS3):
                for i in range(2):
                    j = st * 2 + i
                    pe.wait_ge(n["xi_ready"], h * 8 + j + 1)
                    for t in range(TPS):
                        last = mm(bank[2 * i + t // 2][:, (t % 2) * MEM:(t % 2 + 1) * MEM], xi[i][:, t * P:(t + 1) * P],
                                  K3[:, bass.ds(h, 1), :])
                    last.then_inc(n["sc_ready"], 1)
                for i in range(2):
                    j = st * 2 + i
                    pe.wait_ge(n["w_ready"], h * 6 + j + 1)
                    for m in range(2):
                        for t in range(TPS):
                            last = nc.tensor.transpose(bank[2 * i + m][:, t * P:(t + 1) * P],
                                                       w3[i][:, t, m * P:(m + 1) * P], ident[:])
                    last.then_inc(n["w_T"], 1)
                    pe.wait_ge(n["wT_ready"], h * 6 + j + 1)
                    for m in range(2):
                        last = mm(bank[2 * i][:], v3_s[:, m, :], wT3[i][:, m, :], m == 0, m == 1)
                    last.then_inc(n["q_ready"], 1)
            for i in range(2):
                pe.wait_ge(n["xi_ready"], h * 8 + 6 + i + 1)
                for t in range(TPS):
                    if t >= 2:
                        pe.wait_ge(n["o_added"], h * 8 + 4 * i + t + 7)
                    last = mm(bank[2 * i + t % 2][:, 0:D], xi[i][:, t * P:(t + 1) * P], wo3_s[:])
                    last.then_inc(n["o_ready"], 1)
            pe.drain().then_inc(head3_used, 1)

        def scalar_attention3(act, h):
            n = N3

            def take_xi(i, j):
                act.wait_ge(n["q_ready"], h * 8 + j + 1)
                act.activation(xi[i][:], bank[2 * i][:], ACT.Copy).then_inc(n["xi_ready"], 1)

            for i in range(2):
                take_xi(i, i)
            for st in range(STEPS3):
                for it in range(NEWTON + 1):
                    for i in range(2):
                        j = st * 2 + i
                        act.wait_ge(n["tau_ready"], h * 6 * (NEWTON + 1) + st * 2 * (NEWTON + 1) + it * 2 + i + 1)
                        for t in range(TPS):
                            if it < NEWTON:
                                act.activation(re3[:, i, t, :], sc3[i][:, t, :], ACT.Relu, bias=tau[:, i, t:t + 1],
                                               accum_out=s1[:, i, t:t + 1])
                            else:
                                act.activation(re3[:, i, t, :], sc3[i][:, t, :], ACT.Relu, bias=tau[:, i, t:t + 1])
                        act.drain().then_inc(n["w_rel"], 1)
                for i in range(2):
                    j = st * 2 + i
                    act.wait_ge(n["w_T"], h * 6 + j + 1)
                    for m in range(2):
                        act.activation(wT3[i][:, m, :], bank[2 * i + m][:], ACT.Copy)
                    act.drain().then_inc(n["wT_ready"], 1)
                    take_xi(i, 2 + j)

        def vector_attention3(dve, h):
            n = N3
            with_tau = h * 6 * (NEWTON + 1)
            for st in range(STEPS3):
                for i in range(2):
                    j = st * 2 + i
                    dve.wait_ge(n["sc_ready"], h * 6 + j + 1)
                    for c in range(2):
                        sc = bank[2 * i + c][:].rearrange("p (t m) -> p t m", m=MEM)
                        dve.tensor_reduce(mx3[:, i, 2 * c:2 * c + 2], sc, AX.X, ALU.max)
                    dve.memset(tau[:, i, :], 1.0)
                    dve.drain()
                    for c in range(2):
                        sc = bank[2 * i + c][:].rearrange("p (t m) -> p t m", m=MEM)
                        dve.tensor_tensor(sc3[i][:, 2 * c:2 * c + 2, :], sc,
                                          mx3[:, i, 2 * c:2 * c + 2].unsqueeze(2).to_broadcast([P, 2, MEM]), ALU.subtract)
                    dve.drain().then_inc(n["tau_ready"], 1)
                for it in range(NEWTON):
                    for i in range(2):
                        r = with_tau + st * 2 * (NEWTON + 1) + it * 2 + i + 1
                        dve.wait_ge(n["w_rel"], r)
                        for t in range(TPS):
                            dve.tensor_tensor_reduce(w3[i][:, t, :], re3[:, i, t, :], re3[:, i, t, :], 1.0, 0.0, ALU.mult, ALU.add,
                                                     s2[:, i, t:t + 1])
                        dve.drain()
                        dve.scalar_tensor_tensor(nb[:, i, :], s2[:, i, :], 3.0, s1[:, i, :], ALU.add, ALU.mult)
                        dve.tensor_tensor(na[:, i, :], s2[:, i, :], s2[:, i, :], ALU.mult)
                        dve.drain()
                        dve.reciprocal(nb[:, i, :], nb[:, i, :])
                        dve.drain()
                        dve.scalar_tensor_tensor(na[:, i, :], na[:, i, :], -1.0, nb[:, i, :], ALU.add, ALU.mult)
                        dve.drain()
                        dve.tensor_tensor(tau[:, i, :], tau[:, i, :], na[:, i, :], ALU.subtract)
                        dve.drain()
                        dve.tensor_scalar(tau[:, i, :], tau[:, i, :], MEM ** -0.5, 1.0, ALU.max, ALU.min)
                        dve.drain().then_inc(n["tau_ready"], 1)
                for i in range(2):
                    r = with_tau + st * 2 * (NEWTON + 1) + NEWTON * 2 + i + 1
                    dve.wait_ge(n["w_rel"], r)
                    dve.tensor_tensor(w3[i][:], re3[:, i, :, :], re3[:, i, :, :], ALU.mult)
                    dve.drain().then_inc(n["w_ready"], 1)
            for i in range(2):
                for t in range(TPS):
                    dve.wait_ge(n["o_ready"], h * 8 + 4 * i + t + 1)
                    dve.tensor_tensor(x[:, i * TPS + t, :], x[:, i * TPS + t, :], bank[2 * i + t % 2][:, 0:D], ALU.add)
                    dve.drain().then_inc(n["o_added"], 1)

        def pool_attention3(pool):
            with pool.Fori(0, H3) as h:
                pool.wait_ge(head3_used, h + 1)
                pool.tensor_copy(wq_s[:], wq3[:, :, bass.ds(h * HD3, HD3)])
                pool.tensor_copy(v3_s[:], V3[:, :, bass.ds(h * HD3, HD3)])
                pool.tensor_copy(wo3_s[:], wo3[:, bass.ds(h, 1), :])
                pool.drain().then_inc(head3_ready, 1)

        LOADS = [0, 0, 0, 0]
        loads = [
            [(ident, "ident"), (head_mask, "head_mask"), (gates, "gates"), (order_pos, "order_pos"), (wqkv[0], "wqkv0"),
             (bqkv, "bqkv"), (wo[0], "wo0"), (bo, "bo")],
            [(rope, "rope"), (wqkv[1], "wqkv1"), (wo[1], "wo1"), (router[1], "router1"), (lower, "lower"),
             (decay, "decay"), (decay_q, "decay_q"), (decay_k, "decay_k"), (lam_chunk, "lam_chunk"),
             (own_block, "own_block"), (wg1, "wg1"), (wg2, "wg2"), (norm_w, "norm_w")],
            [(causal, "causal"), (wqkv[2], "wqkv2"), (wo[2], "wo2"), (router[2], "router2"), (rbias, "rbias"),
             (dbias, "dbias"), (gu_bias, "gu_bias")],
            [(wq3, "wq3"), (wk3, "wk3"), (wv3, "wv3"), (wo3, "wo3"), (mem, "mem"), (aff, "aff"), (lbeta, "lbeta"),
             (router[3], "router3")],
        ]
        for n in range(4):
            LOADS[n] = 16 * len(loads[n])
        LN_S = 6.238324625039508
        out_stored = sem("out_stored")
        PAIRS_IN = 8

        def load_broadcast(name):
            return a[name].shape[0] == 1

        block = ctx.enter_context(nc.Block())

        @block.sync
        def _(sp):
            sp.dma_start(x[:], a["x"]).then_inc(x_loaded, 16)
            for n in range(4):
                if n == 3:
                    sp.wait_ge(phase_done, 4 * 13)
                for dst, name in loads[n]:
                    src = a[name]
                    if load_broadcast(name):
                        src = src.to_broadcast([P] + list(src.shape[1:]))
                    sp.dma_start(dst[:], src).then_inc(loaded[n], 16)
                if n == 2:
                    sync_ffn(sp, 0, 0, CHUNKS[0] // 2)
                    sync_ffn(sp, 1, 0, CHUNKS[1] // 2)
            for n in range(2, 4):
                sync_ffn(sp, n, 0, CHUNKS[n] // 2)
            sp.wait_ge(phase_done, 4 * BARRIERS)
            sp.dma_start(out, x[:]).then_inc(out_stored, 16)
            sp.wait_ge(out_stored, 16)

        def ffn_loop(eng, pair, n, first=0, count=None):
            with eng.Fori(first, first + (count or CHUNKS[n] // 2 - first)) as p:
                pair(eng, n, p)

        @block.tensor
        def _(pe):
            pe.wait_ge(loaded[0], LOADS[0])
            for n in range(3):
                tensor_norm(pe, n)
                barrier(pe)
                pe.wait_ge(loaded[n], LOADS[n])
                if n == 2:
                    pe.wait_ge(loaded[1], LOADS[1])
                tensor_project(pe, n)
                barrier(pe)
                if n == 0:
                    barrier(pe)
                if n == 1:
                    tensor_linear(pe)
                else:
                    tensor_heads(pe, n)
                barrier(pe)
                if n != 1:
                    barrier(pe)
                tensor_out(pe, n)
                barrier(pe)
                if n:
                    tensor_route(pe, n)
                    barrier(pe)
                if n == 2:
                    tensor_bias2(pe)
                    barrier(pe)
                tensor_ffn_start(pe, n)
                ffn_loop(pe, tensor_ffn_pair, n)
                barrier(pe)
            tensor_norm(pe, 3)
            barrier(pe)
            pe.wait_ge(loaded[3], LOADS[3])
            tensor_norm3(pe)
            barrier(pe)
            tensor_route(pe, 3)
            barrier(pe)
            tensor_ffn_start(pe, 3)
            pe.drain().then_inc(head3_used, 1)
            with pe.Fori(0, H3) as h:
                tensor_attention3(pe, h)
                tensor_ffn_pair(pe, 3, h)
            ffn_loop(pe, tensor_ffn_pair, 3, PAIRS_IN)
            barrier(pe)

        @block.scalar
        def _(act):
            scalar_gates(act)
            for n in range(3):
                scalar_norm(act, n)
                barrier(act)
                scalar_project(act, n)
                barrier(act)
                if n == 0:
                    barrier(act)
                if n == 1:
                    scalar_linear(act)
                else:
                    scalar_heads(act, n)
                barrier(act)
                if n == 0:
                    scalar_rows(act)
                if n != 1:
                    barrier(act)
                scalar_out(act, n)
                barrier(act)
                if n:
                    scalar_route(act, n)
                    barrier(act)
                if n == 2:
                    barrier(act)
                ffn_loop(act, scalar_ffn_pair, n)
                barrier(act)
            scalar_norm(act, 3)
            barrier(act)
            act.wait_ge(loaded[3], LOADS[3])
            scalar_norm3(act)
            barrier(act)
            scalar_route(act, 3)
            barrier(act)
            with act.Fori(0, H3) as h:
                scalar_attention3(act, h)
                scalar_ffn_pair(act, 3, h)
            ffn_loop(act, scalar_ffn_pair, 3, PAIRS_IN)
            barrier(act)

        @block.vector
        def _(dve):
            dve.wait_ge(loaded[0], LOADS[0])
            vector_gates(dve)
            for n in range(3):
                vector_norm(dve, n)
                barrier(dve)
                if n:
                    dve.wait_ge(loaded[n], LOADS[n])
                vector_project(dve, n)
                barrier(dve)
                if n == 0:
                    vector_diffs(dve)
                    barrier(dve)
                if n == 1:
                    vector_linear(dve)
                else:
                    vector_heads(dve, n)
                barrier(dve)
                if n == 0:
                    vector_rows(dve)
                if n == 2:
                    vector_divide(dve)
                if n != 1:
                    barrier(dve)
                vector_out(dve, n)
                barrier(dve)
                if n:
                    vector_route(dve, n)
                    barrier(dve)
                if n == 2:
                    vector_bias2(dve)
                    barrier(dve)
                vector_ffn_start(dve, n)
                ffn_loop(dve, vector_ffn_pair, n)
                barrier(dve)
            vector_norm(dve, 3)
            barrier(dve)
            dve.wait_ge(loaded[3], LOADS[3])
            vector_norm3(dve)
            barrier(dve)
            vector_route(dve, 3)
            barrier(dve)
            vector_ffn_start(dve, 3)
            dve.drain().then_inc(N3["o_added"], 8)
            with dve.Fori(0, H3) as h:
                vector_attention3(dve, h)
                vector_ffn_pair(dve, 3, h)
            ffn_loop(dve, vector_ffn_pair, 3, PAIRS_IN)
            barrier(dve)

        @block.gpsimd
        def _(pool):
            pool.wait_ge(gates_ready, 1)
            for n in range(3):
                pool_norm(pool, n)
                barrier(pool)
                barrier(pool)
                if n == 0:
                    barrier(pool)
                if n == 1:
                    pool_linear(pool)
                else:
                    pool_heads(pool, n)
                barrier(pool)
                if n == 0:
                    pool_rows(pool)
                if n != 1:
                    barrier(pool)
                barrier(pool)
                if n:
                    barrier(pool)
                if n == 2:
                    barrier(pool)
                barrier(pool)
            pool_norm(pool, 3)
            barrier(pool)
            pool_norm3(pool)
            barrier(pool)
            barrier(pool)
            pool_attention3(pool)
            barrier(pool)




def _constants(np):
    p = np.arange(P)
    c = {"ident": np.eye(P, dtype=np.float32)}
    c["head_mask"] = (p[:, None] // HD == np.arange(GH)[None, :]).astype(np.float32)
    c["causal"] = np.where(p[None, :] > p[:, None], np.float32(MASKED), np.float32(0))
    c["own_block"] = (p[:, None] // HD == p[None, :] // HD).astype(np.float32)
    pos = (np.arange(TPS)[None, :] * P + p[:, None]).astype(np.float32)
    c["order_pos"] = (pos / np.float32(S) * np.float32(0.05)).astype(np.float32)
    half = HD // 2
    th1 = np.float32(10000.0) ** (np.float32(-2.0) * np.arange(half, dtype=np.float32) / np.float32(HD))
    th2 = np.float32(1.0) / np.float32(10000.0) ** (np.arange(0, HD, 2, dtype=np.float32) / np.float32(HD))
    rope = np.zeros((P, 2, TPS, 2, half), np.float32)
    for i, th in enumerate((th1, th2)):
        ang = (pos[:, :, None] * th.astype(np.float32)).astype(np.float32)
        rope[:, i, :, 0, :] = np.cos(ang)
        rope[:, i, :, 1, :] = np.sin(ang)
    c["rope"] = rope
    lam = -(2.0 ** (-8.0 * (np.arange(H) + 1.0) / H))
    d = p[None, None, :] - p[:, None, None]
    c["decay"] = np.where(d >= 0, np.exp(lam[None, :, None] * np.maximum(d, 0)), 0.0).astype(np.float32)
    c["decay_q"] = np.exp(lam[None, :] * (p[:, None] + 1.0)).astype(np.float32)
    c["decay_k"] = np.exp(lam[None, :] * (P - 1.0 - p[:, None])).astype(np.float32)
    lc = np.exp(lam * P).reshape(NG, GH)
    c["lam_chunk"] = np.ascontiguousarray(np.broadcast_to(lc[:, p // HD].T[:, :, None], (P, NG, P))).astype(np.float32)
    e = np.arange(16)
    c["lower"] = np.broadcast_to((e[None, :] < e[:, None]).astype(np.float32)[None], (1, 16, 16)).copy()
    for n, w in ((1, 176), (2, 256), (3, 176)):
        unit = np.arange(CHUNKS[n] * P)
        owner = np.minimum(unit // w, EXPERTS[n])
        sel = np.zeros((CHUNKS[n], CR, P), np.float32)
        for part in range(3):
            sel[unit // P, part * NE + owner, unit % P] = 1
        c[f"sel{n}"] = sel
    return c


def _rows(np, w):
    return np.ascontiguousarray(w.reshape(-1, P, w.shape[1]).transpose(1, 0, 2))


def kernel(**inputs):
    import ml_dtypes
    import numpy as np
    import concourse.bacc as bacc
    from concourse.bass_utils import run_bass_kernel_spmd as run

    i = {k: np.asarray(v) for k, v in inputs.items()}
    a = _constants(np)
    for n in (1, 2, 3):
        a[f"sel{n}"] = a[f"sel{n}"].astype(ml_dtypes.bfloat16)

    def row(*names):
        return np.concatenate([i[k].reshape(-1) for k in names])[None, :]

    a["x"] = np.ascontiguousarray(i["L0_attn_hidden_states"].reshape(NT, P, D).transpose(1, 0, 2))
    a["wqkv0"] = _rows(np, np.concatenate([i[f"L0_attn_W{c}"].T for c in "qkv"], 1))
    a["bqkv"] = row("L0_attn_bq", "L0_attn_bk", "L0_attn_bv")
    a["wo0"], a["bo"] = _rows(np, i["L0_attn_Wo"].T), row("L0_attn_bo")
    a["gates"] = row(*[f"L0_attn_{c}_gate" for c in ("truth", "balance", "order", "justice", "harmony")])
    a["wqkv1"] = _rows(np, np.concatenate([i[f"L1_attn_W{c}"] for c in "qkv"], 1))
    a["wo1"], a["router1"] = _rows(np, i["L1_attn_Wo"]), _rows(np, i["L1_ffn_gate_w"])
    a["wg1"], a["wg2"] = _rows(np, i["L1_attn_Wg1"]), i["L1_attn_Wg2"]
    a["norm_w"] = row("L1_attn_norm_weight")
    wk = np.repeat(i["L2_attn_wk"].reshape(D, 4, HD), 4, axis=1).reshape(D, D)
    a["wqkv2"] = _rows(np, np.concatenate([i["L2_attn_wq"], wk, i["L2_attn_wv"]], 1))
    a["wo2"], a["router2"] = _rows(np, i["L2_attn_wo"]), _rows(np, i["L2_ffn_router_weight"].T)
    a["rbias"], a["dbias"] = row("L2_ffn_router_bias"), i["L2_ffn_down_proj_bias"]
    a["wq3"] = _rows(np, i["L3_attn_Wq"].T)
    a["wk3"], a["wv3"] = i["L3_attn_Wk"].T, i["L3_attn_Wv"].T
    a["wo3"] = _rows(np, i["L3_attn_Wo"].T)
    a["mem"] = _rows(np, i["L3_attn_memory"])
    a["aff"] = np.concatenate([i["L3_attn_g_state"].reshape(2, P).T, i["L3_attn_b_state"].reshape(2, P).T,
                               i["L3_attn_g_mem"][:, None], i["L3_attn_b_mem"][:, None]], 1)
    a["lbeta"] = row("L3_attn_log_beta")
    a["router3"] = _rows(np, np.concatenate([i["L3_ffn_gate_w"], i["L3_ffn_shared_gate_vec"]], 0).T)

    def wide(w):
        return w.transpose(1, 0, 2).reshape(D, -1)

    ffn = [(i["L0_ffn_w_gate"].T, i["L0_ffn_w_up"].T, i["L0_ffn_w_down"].T, None)]
    ffn.append((np.concatenate([wide(i["L1_ffn_w_gate"]), i["L1_ffn_sw_gate"]], 1),
                np.concatenate([wide(i["L1_ffn_w_up"]), i["L1_ffn_sw_up"]], 1),
                np.concatenate([i["L1_ffn_w_down"].reshape(-1, D), i["L1_ffn_sw_down"]], 0), None))
    gu, bias = i["L2_ffn_gate_up_proj"], i["L2_ffn_gate_up_proj_bias"]
    ffn.append((wide(gu[:, :, 0::2]), wide(gu[:, :, 1::2]), i["L2_ffn_down_proj"].reshape(-1, D),
                (bias[:, 0::2].reshape(-1), bias[:, 1::2].reshape(-1))))
    eg, sg = i["L3_ffn_expert_gate_up"].transpose(0, 2, 1), i["L3_ffn_shared_gate_up"]
    ffn.append((np.concatenate([wide(eg[:, :, :176]), sg[:704].T], 1),
                np.concatenate([wide(eg[:, :, 176:]), sg[704:].T], 1),
                np.concatenate([i["L3_ffn_expert_down"].transpose(0, 2, 1).reshape(-1, D), i["L3_ffn_shared_down"].T], 0),
                None))
    a["gu"] = np.zeros((sum(CHUNKS), P, GUW), np.float32)
    a["down"] = np.zeros((sum(CHUNKS), P, D), np.float32)
    first = 0
    for n, (g, u, d, b) in enumerate(ffn):
        hidden, width = g.shape[1], CHUNKS[n] * P
        for at, w in ((0, g), (2 * P, u)):
            full = np.zeros((D, width), np.float32)
            full[:, :hidden] = w
            parts = full.reshape(KD, P, CHUNKS[n], P).transpose(2, 1, 0, 3).reshape(CHUNKS[n], P, D)
            a["gu"][first:first + CHUNKS[n], :, at:at + D] = parts
        if b is not None:
            a["gu_bias"] = np.stack([c.reshape(CHUNKS[n], P).T for c in b], 2)
        full = np.zeros((width, D), np.float32)
        full[:hidden] = d
        a["down"][first:first + CHUNKS[n]] = full.reshape(CHUNKS[n], P, D)
        first += CHUNKS[n]

    nc = bacc.Bacc("TRN2", target_bir_lowering=False, num_devices=1)
    arrays = {k: np.ascontiguousarray(v) for k, v in a.items()}
    aps = {k: nc.dram_tensor(f"in_{k}", v.shape, mybir.dt.from_np(v.dtype), kind="ExternalInput").ap()
           for k, v in arrays.items()}
    out = nc.dram_tensor("out", (P, NT, D), F32, kind="ExternalOutput").ap()
    build(nc, aps, out)
    r = run(nc, [{f"in_{k}": v for k, v in arrays.items()}], core_ids=[0])
    return r.results[0]["out"].transpose(1, 0, 2).reshape(B, S, D)
```

```python
from contextlib import ExitStack

import concourse.bass as bass
from concourse import mybir

F32 = mybir.dt.float32
BF16 = mybir.dt.bfloat16
ALU = mybir.AluOpType
ACT = mybir.ActivationFunctionType
AX = mybir.AxisListType

P = 128
D = 256
KD = D // P
AREA = 17800
WAREA = 6144
B, S = 2, 512
TOK = B * S
NT = TOK // P
TPS = S // P
H, HD = 16, 16
GH = P // HD
NG = H // GH
VW = HD + 1
NE = 17
CR = 3 * NE
GUW = 2 * D
EXPERTS = (0, 8, 8, 16)
TOPK = (0, 2, 2, 4)
CHUNKS = (8, 14, 16, 28)
LN_EPS = 1e-5
MASKED = -1e30
H3, HD3 = 8, 128
MEM = 256
RELU_TILES = 2
STEPS3 = 3
BARRIERS = 25
NEWTON = 5


def build(nc, a, out):
    with ExitStack() as ctx:
        def sb(name, shape, dt=F32):
            return ctx.enter_context(nc.sbuf_tensor(name, shape, dt))

        area = sb("area", [P, AREA])
        taken = {0: 0, 1: 0, 3: 0}
        warea = sb("warea", [P, WAREA])
        wtaken = {0: 0, 3: 0}

        def part(layer, shape, area=area, taken=taken, AREA=AREA):
            size = 1
            for k in shape[1:]:
                size *= k
            at = taken[layer]
            taken[layer] = at + size
            assert at + size <= AREA
            names = "abcd"[:len(shape) - 1]
            return area[:, at:at + size].rearrange(f"p ({' '.join(names)}) -> p {' '.join(names)}",
                                                   **dict(zip(names, shape[1:])))

        def wpart(layer, shape):
            return part(layer, shape, warea, wtaken, WAREA)

        def sem(name):
            return ctx.enter_context(nc.semaphore(name))

        bank = [ctx.enter_context(nc.psum_tensor(f"bank{i}", [P, 512], F32)) for i in range(8)]

        ident = sb("ident", [P, P])
        identb = sb("identb", [P, P], BF16)
        head_mask = sb("head_mask", [P, GH])
        causal = sb("causal", [P, P])
        rope = sb("rope", [P, 2, TPS, 2, HD // 2])
        half_neg = sb("half_neg", [P, NT * H])
        wqkv = [wpart(0, [P, KD, 768]), wpart(0, [P, KD, 768]), sb("wqkv2", [P, KD, 576])]
        wo = [sb(f"wo{n}", [P, KD, D]) for n in range(3)]
        bqkv = wpart(0, [P, 768])
        bo = sb("bo", [P, D])
        gates = sb("gates", [P, 5])
        router = [None, sb("router1", [P, KD, 8]), sb("router2", [P, KD, 8]), sb("router3", [P, KD, NE])]
        rbias = sb("rbias", [P, 8])
        dbias = sb("dbias", [8, D])
        gu_bias = sb("gu_bias", [P, CHUNKS[2], 2])
        lower = sb("lower", [P, 16, 16])
        decay = wpart(0, [P, H, P])
        decay_q = sb("decay_q", [P, H])
        decay_k = sb("decay_k", [P, H])
        lam_chunk = sb("lam_chunk", [P, NG, P])
        own_block = sb("own_block", [P, P])
        wg1 = sb("wg1", [P, KD, HD])
        wg2 = sb("wg2", [HD, D])
        norm_w = sb("norm_w", [P, D])

        x = sb("x", [P, NT, D])
        xnT = sb("xnT", [P, KD, TOK])
        xn = sb("xn", [P, 2, D])
        st6 = sb("st6", [P, NT, 6])
        mv = sb("mv", [P, NT, 2])
        rstd = sb("rstd", [P, NT])
        nmr = sb("nmr", [P, NT])
        tok = sb("tok", [P, 2, 512])
        tmp = sb("tmp", [P, 2, 512])
        qT = part(0, [P, B * NG, S])
        kT = part(0, [P, B * NG, S])
        v = part(0, [P, B * H + 2, TPS, VW])
        taken[1] = taken[0]
        kdT = part(0, [P, B * NG, S])
        raw = part(0, [P, B * H + 2, TPS, VW])
        ao = sb("ao", [P, NT, D])
        aoT = sb("aoT", [P, KD, TOK])
        logits = sb("logits", [P, NT, 16])
        probs = sb("probs", [P, NT, 16])
        comb = sb("comb", [P, NT, NE])
        combp = sb("combp", [P, NT, CR], BF16)
        combT = sb("combT", [CR, TOK], BF16)
        rank = sb("rank", [P, 16, 16])
        rank2 = sb("rank2", [P, 16, 16])
        rowm = sb("rowm", [P, NT])
        rowz = sb("rowz", [P, NT])
        rankn = sb("rankn", [P, NT, 16])
        shared = sb("shared", [P, NT])

        wgu = [sb(f"wgu{c}", [P, GUW]) for c in range(2)]
        wd = sb("wd", [P, 2, D])
        sel = [sb(f"sel{c}", [CR, P], BF16) for c in range(2)]
        th = sb("th", [P, 2, 512])
        gl = sb("gl", [P, 2, 512])
        up = sb("up", [P, 2, 512])
        hT = sb("hT", [P, 4, 512])

        phase_done = sem("phase_done")
        loaded = [sem(f"weights{n}_loaded") for n in range(4)]
        x_loaded = sem("x_loaded")
        gates_loaded = sem("gates_loaded")
        ident_loaded = sem("ident_loaded")
        phases = {}

        def barrier(eng):
            n = phases[eng.engine] = phases.get(eng.engine, 0) + 1
            eng.drain().then_inc(phase_done, 1)
            eng.wait_ge(phase_done, 4 * n)

        def mm(o, l, r, start=True, stop=True):
            return nc.tensor.matmul(o, l, r, start=start, stop=stop)

        def total(n):
            pairs = CHUNKS[n] // 2
            t = {"stats_ready": 1, "rstd_ready": 1, "xn_ready": NT, "xn_T": NT, "xnT_ready": NT}
            for k in ("qk_ready", "v_ready", "qk_tok", "qk_T", "qk_copied", "v_copied", "ao_T", "aoT_ready",
                      "o_ready", "o_added"):
                t[k] = NT if n < 3 else 0
            for k in ("logits_ready", "logits_copied"):
                t[k] = NT if n == 3 else 0
            t["route_exp"] = 2 if n else 0
            t["comb_T"] = (0, 2, 3, 2)[n]
            for k in ("guA_loaded", "guB_loaded"):
                t[k] = (32 if n else 16) * pairs
            t["down_loaded"] = 16 * pairs
            for k in ("guA_used", "guB_used", "down_used"):
                t[k] = pairs
            for k in ("gate_ready", "up_ready", "tanh_ready", "gate_used", "up_used", "h_ready", "part_ready",
                      "part_added"):
                t[k] = 4 * pairs
            for k in ("comb_ready", "comb_used"):
                t[k] = 4 * pairs if n else 0
            t["gate_clipped"] = 4 * pairs if n == 2 else 0
            return t

        LS = {k: sem(k) for k in total(0)}
        AT = [{k: sum(total(m)[k] for m in range(n)) for k in total(0)} for n in range(4)]

        def vector_norm(dve, n):
            s, at = LS, AT[n]
            if n == 0:
                dve.wait_ge(x_loaded, 16)
            for t in range(NT):
                dve.bn_stats(st6[:, t, :], x[:, t, :])
            dve.drain()
            for t in range(NT):
                last = dve.bn_aggr(mv[:, t, :], st6[:, t, :])
            last.then_inc(s["stats_ready"], 1)
            for t in range(NT):
                dve.wait_ge(s["xn_T"], at["xn_T"] + t + 1)
                dve.tensor_copy(xnT[:, :, t * P:(t + 1) * P],
                                bank[t % 2][:, 0:D].rearrange("p (k t) -> p k t", k=KD)).then_inc(s["xnT_ready"], 1)

        def pool_norm(pool, n):
            s, at = LS, AT[n]
            pool.wait_ge(s["stats_ready"], at["stats_ready"] + 1)
            pool.tensor_scalar(rstd[:], mv[:, :, 1], LN_EPS, None, ALU.add)
            pool.drain()
            pool.tensor_tensor(rstd[:], rstd[:], half_neg[:, 0:NT], ALU.pow)
            pool.drain()
            pool.tensor_tensor(nmr[:], mv[:, :, 0], rstd[:], ALU.mult)
            pool.drain()
            pool.tensor_scalar(nmr[:], nmr[:], -1.0, None, ALU.mult).then_inc(s["rstd_ready"], 1)

        def scalar_norm(act, n):
            s, at = LS, AT[n]
            act.wait_ge(s["rstd_ready"], at["rstd_ready"] + 1)
            for t in range(NT):
                if t >= 2:
                    act.wait_ge(s["xn_T"], at["xn_T"] + t - 1)
                act.activation(xn[:, t % 2, :], x[:, t, :], ACT.Identity, bias=nmr[:, t:t + 1],
                               scale=rstd[:, t:t + 1]).then_inc(s["xn_ready"], 1)

        def tensor_norm(pe, n):
            s, at = LS, AT[n]
            for t in range(NT):
                pe.wait_ge(s["xn_ready"], at["xn_ready"] + t + 1)
                if t >= 2:
                    pe.wait_ge(s["xnT_ready"], at["xnT_ready"] + t - 1)
                for k in range(KD):
                    last = nc.tensor.transpose(bank[t % 2][:, k * P:(k + 1) * P], xn[:, t % 2, k * P:(k + 1) * P],
                                               ident[:])
                last.then_inc(s["xn_T"], 1)

        def heads_of(t):
            b = t // TPS
            return slice(b * H, (b + 1) * H)

        def v_of(t, first=0, count=H):
            at = 2 + t // TPS * H + first
            return v[:, at:at + count, t % TPS, :]

        def group_of(t):
            b, c = t // TPS, t % TPS
            return (slice(None), slice(b * NG, (b + 1) * NG), slice(c * P, (c + 1) * P))

        def tensor_project(pe, n):
            s, at = LS, AT[n]
            vw = wqkv[n].shape[2] - 512

            def turn(t):
                pe.wait_ge(s["qk_tok"], at["qk_tok"] + t + 1)
                if t >= 2:
                    pe.wait_ge(s["qk_copied"], at["qk_copied"] + t - 1)
                for c in range(4):
                    last = nc.tensor.transpose(bank[4 + t % 2][:, c * P:(c + 1) * P],
                                               tok[:, t % 2, c * P:(c + 1) * P], ident[:])
                last.then_inc(s["qk_T"], 1)

            for t in range(NT):
                pe.wait_ge(s["xnT_ready"], at["xnT_ready"] + t + 1)
                if t >= 2:
                    pe.wait_ge(s["qk_tok"], at["qk_tok"] + t - 1)
                ts = slice(t * P, (t + 1) * P)
                for k in range(KD):
                    last = mm(bank[t % 2][:], xnT[:, k, ts], wqkv[n][:, k, 0:512], k == 0, k == KD - 1)
                last.then_inc(s["qk_ready"], 1)
                if t >= 2:
                    pe.wait_ge(s["v_copied"], at["v_copied"] + t - 1)
                for k in range(KD):
                    last = mm(bank[2 + t % 2][:, 0:vw], xnT[:, k, ts], wqkv[n][:, k, 512:], k == 0, k == KD - 1)
                if n:
                    for k in range(KD):
                        last = mm(bank[2 + t % 2][:, D:D + 8], xnT[:, k, ts], router[n][:, k, :], k == 0, k == KD - 1)
                last.then_inc(s["v_ready"], 1)
                if t:
                    turn(t - 1)
            turn(NT - 1)

        def vector_project(dve, n):
            s, at = LS, AT[n]
            for t in range(NT):
                dve.wait_ge(s["qk_ready"], at["qk_ready"] + t + 1)
                if t >= 2:
                    dve.wait_ge(s["qk_T"], at["qk_T"] + t - 1)
                o, qk = tok[:, t % 2, :], bank[t % 2]
                if n == 0:
                    dve.tensor_tensor(o, qk[:], bqkv[:, 0:512], ALU.add).then_inc(s["qk_tok"], 1)
                else:
                    src = qk[:]
                    if n == 1:
                        dve.wait_ge(silu_tanh, t + 1)
                        dve.scalar_tensor_tensor(tmp[:, 0, :], th[:, t % 2, :], 1.0, qk[:], ALU.add, ALU.mult)
                        dve.drain()
                        dve.tensor_scalar(tmp[:, 0, :], tmp[:, 0, :], 0.5, None, ALU.mult)
                        dve.drain()
                        src = tmp[:, 0, :]
                    sh = src.rearrange("p (h a e) -> p h a e", a=2, e=HD // 2)
                    oh = o.rearrange("p (h a e) -> p h a e", a=2, e=HD // 2)
                    mh = tmp[:, 1, :].rearrange("p (h a e) -> p h a e", a=2, e=HD // 2)
                    cs = [rope[:, n - 1, t % TPS, i, :].unsqueeze(1).to_broadcast([P, 2 * H, HD // 2]) for i in (0, 1)]
                    for a2 in (0, 1):
                        dve.tensor_tensor(oh[:, :, a2, :], sh[:, :, a2, :], cs[0], ALU.mult)
                        dve.tensor_tensor(mh[:, :, a2, :], sh[:, :, 1 - a2, :], cs[1], ALU.mult)
                    dve.drain()
                    dve.tensor_tensor(oh[:, :, 0, :], oh[:, :, 0, :], mh[:, :, 0, :], ALU.subtract)
                    dve.tensor_tensor(oh[:, :, 1, :], oh[:, :, 1, :], mh[:, :, 1, :], ALU.add)
                    dve.drain().then_inc(s["qk_tok"], 1)
                if n == 0:
                    dve.drain()
                    dve.tensor_tensor(tmp[:, 0, 0:D], tok[:, t % 2, D:], tok[:, t % 2, D:], ALU.mult)
                    dve.drain()
                    dve.tensor_reduce(knorm[:, heads_of(t), t % TPS], tmp[:, 0, 0:D].rearrange("p (h e) -> p h e", e=HD), AX.X, ALU.add)
                if n == 1:
                    dve.drain()
                    dve.tensor_tensor(kd[:, t, :].rearrange("p (h e) -> p h e", e=HD),
                                      tok[:, t % 2, D:].rearrange("p (h e) -> p h e", e=HD),
                                      decay_k[:].unsqueeze(2).to_broadcast([P, H, HD]), ALU.mult)
                dve.wait_ge(s["v_ready"], at["v_ready"] + t + 1)
                vb = bank[2 + t % 2]
                if n == 0:
                    dve.tensor_tensor(tmp[:, 1, 0:D], vb[:, 0:D], bqkv[:, 512:], ALU.add)
                    dve.drain().then_inc(s["v_copied"], 1)
                    dve.tensor_scalar(v_of(t)[:, :, 0:HD], tmp[:, 1, 0:D].rearrange("p (h e) -> p h e", e=HD),
                                      order_exp[:, t % TPS:t % TPS + 1], None, ALU.mult)
                    dve.tensor_copy(v_of(t)[:, :, HD], order_exp[:, t % TPS:t % TPS + 1].to_broadcast([P, H]))
                elif n == 1:
                    dve.tensor_copy(v_of(t)[:, :, 0:HD], vb[:, 0:D].rearrange("p (h e) -> p h e", e=HD))
                    dve.tensor_copy(logits[:, t, 0:8], vb[:, D:D + 8]).then_inc(s["v_copied"], 1)
                else:
                    for r in range(4):
                        dve.tensor_copy(v_of(t).rearrange("p (h r) e -> p h r e", r=4)[:, :, r, 0:HD],
                                        vb[:, 0:64].rearrange("p (h e) -> p h e", e=HD))
                    dve.tensor_tensor(logits[:, t, 0:8], vb[:, D:D + 8], rbias[:], ALU.add).then_inc(s["v_copied"], 1)
            if n == 2:
                dve.memset(v[:, 2:, :, HD:VW], 1.0)

        def scalar_project(act, n):
            s, at = LS, AT[n]

            def out_T(t):
                act.wait_ge(s["qk_T"], at["qk_T"] + t + 1)
                src = bank[4 + t % 2][:].rearrange("p (q t) -> p q t", t=P)
                act.activation(qT[group_of(t)], src[:, 0:NG, :], ACT.Copy)
                act.activation(kT[group_of(t)], src[:, NG:, :], ACT.Copy)
                act.drain().then_inc(s["qk_copied"], 1)

            for t in range(NT):
                if n == 1:
                    act.wait_ge(s["qk_ready"], at["qk_ready"] + t + 1)
                    if t >= 2:
                        act.wait_ge(s["qk_tok"], at["qk_tok"] + t - 1)
                    act.activation(th[:, t % 2, :], bank[t % 2][:], ACT.Tanh, scale=0.5).then_inc(silu_tanh, 1)
                    if t:
                        out_T(t - 1)
                else:
                    out_T(t)
            if n == 1:
                out_T(NT - 1)

        silu_tanh = sem("silu_tanh")
        knorm = sb("knorm", [P, B * H, TPS])
        kd = part(1, [P, NT, D])
        order_exp = sb("order_exp", [P, TPS])

        def tensor_out(pe, n):
            s, at = LS, AT[n]
            for t in range(NT):
                if t >= 2:
                    pe.wait_ge(s["aoT_ready"], at["aoT_ready"] + t - 1)
                for k in range(KD):
                    last = nc.tensor.transpose(bank[t % 2][:, k * P:(k + 1) * P], ao[:, t, k * P:(k + 1) * P], ident[:])
                last.then_inc(s["ao_T"], 1)
                if t:
                    tensor_out_product(pe, n, t - 1)
            tensor_out_product(pe, n, NT - 1)

        def tensor_out_product(pe, n, t):
            s, at = LS, AT[n]
            pe.wait_ge(s["aoT_ready"], at["aoT_ready"] + t + 1)
            if t >= 2:
                pe.wait_ge(s["o_added"], at["o_added"] + t - 1)
            for k in range(KD):
                last = mm(bank[2 + t % 2][:, 0:D], aoT[:, k, t * P:(t + 1) * P], wo[n][:, k, :], k == 0, k == KD - 1)
            last.then_inc(s["o_ready"], 1)

        def scalar_out(act, n):
            s, at = LS, AT[n]
            for t in range(NT):
                act.wait_ge(s["ao_T"], at["ao_T"] + t + 1)
                act.activation(aoT[:, :, t * P:(t + 1) * P], bank[t % 2][:, 0:D].rearrange("p (k t) -> p k t", k=KD),
                               ACT.Copy).then_inc(s["aoT_ready"], 1)

        def vector_out(dve, n):
            s, at = LS, AT[n]
            if n == 0:
                dve.tensor_tensor(x[:], x[:], bo[:].unsqueeze(1).to_broadcast([P, NT, D]), ALU.add)
                dve.drain()
            for t in range(NT):
                dve.wait_ge(s["o_ready"], at["o_ready"] + t + 1)
                dve.tensor_tensor(x[:, t, :], x[:, t, :], bank[2 + t % 2][:, 0:D], ALU.add).then_inc(s["o_added"], 1)

        SB, FB, TB, OB = 0, 4, 6, 7
        U = 2 * TPS
        qm = [part(0, [P, S]) for i in range(2)]
        eA = part(0, [P, 2, S])
        eP = [part(0, [P, S]) for i in range(2)]
        eT = [part(0, [P, S]) for i in range(2)]
        row8 = sb("row8", [P, 3, U])
        nbias = sb("nbias", [P, 4, 2])
        cpair = sb("cpair", [P, 2, 2])
        neg_max_all = sb("neg_max", [P, B * H + 2, TPS])
        neg_max = neg_max_all[:, 2:, :]
        sum_exp_all = sb("sum_exp", [P, B * H + 2, TPS])
        sum_exp = sum_exp_all[:, 2:, :]
        sum_es_all = sb("sum_es", [P, B * H + 2, TPS])
        sum_es = sum_es_all[:, 2:, :]
        sum_diff_all = sb("sum_diff", [P, B * H + 2, TPS])
        sum_diff = sum_diff_all[:, 2:, :]
        sum_s_all = sb("sum_s", [P, B * H + 2, TPS])
        sum_s = sum_s_all[:, 2:, :]
        AS = {k: sem(k) for k in ("qm_ready", "score_ready", "diff_ready", "bias_ready", "expP_ready",
                                  "scores_summed", "diff_read", "mean_read", "turned", "eT_ready", "head_ready",
                                  "head_copied")}
        CREDIT = {"score_ready": 8, "diff_ready": 8, "expP_ready": 4, "scores_summed": 3, "diff_read": 2,
                  "mean_read": 2, "turned": 1, "eT_ready": 1, "head_copied": 1}
        TILES = H * B * TPS
        HEADS_AT = [dict.fromkeys(AS, 0), None,
                    dict.fromkeys(AS, TILES) | {"qm_ready": H * B, "head_ready": H * B + 1, "head_copied": H * B + 2,
                                                "turned": TILES + 1, "eT_ready": TILES + 1}]

        def head_loops(eng, body):
            with eng.Fori(0, B * NG) as bg:
                with eng.Fori(0, GH // 2) as hp:
                    body(bg, hp, bg * (GH // 2) + hp)

        def head_credits(eng, n, names):
            if n == 0:
                for k in names:
                    eng.drain().then_inc(AS[k], CREDIT[k])

        def tensor_heads(pe, n):
            s, at = AS, HEADS_AT[n]
            head_credits(pe, n, ("score_ready", "diff_ready", "turned"))

            def score(bg, i, u):
                hh, j = u // TPS, u % TPS
                if j == 0:
                    pe.wait_ge(s["qm_ready"], at["qm_ready"] + i * 2 + hh + 1)
                w = S if n == 0 else (j + 1) * P
                q = qm[hh][:, j * P:(j + 1) * P]
                pe.wait_ge(s["expP_ready"], at["expP_ready"] + i * U + u + 1)
                if n == 0:
                    pe.wait_ge(s["scores_summed"], at["scores_summed"] + i * U + u + 1)
                last = mm(bank[SB + u % 4][:, 0:w], q, kT[:, bass.ds(bg, 1), 0:w], True, n == 0)
                if n == 2:
                    last = mm(bank[SB + u % 4][:, j * P:w], ident[:], causal[:], False, True)
                last.then_inc(s["score_ready"], 1)
                if n == 0:
                    pe.wait_ge(s["diff_read"], at["diff_read"] + i * U + u + 1)
                    pe.wait_ge(s["mean_read"], at["mean_read"] + i * U + u + 1)
                    mm(bank[FB + u % 2][:], q, kdT[:, bass.ds(bg, 1), :]).then_inc(s["diff_ready"], 1)

            def turn(i, u):
                j = u % TPS
                pe.wait_ge(s["expP_ready"], at["expP_ready"] + i * U + u + 5)
                pe.wait_ge(s["eT_ready"], at["eT_ready"] + i * U + u + 2)
                for c in range(TPS if n == 0 else j + 1):
                    last = nc.tensor.transpose(bank[TB][:, c * P:(c + 1) * P], eP[u % 2][:, c * P:(c + 1) * P], ident[:])
                last.then_inc(s["turned"], 1)

            def weigh(i, u):
                hh, j = u // TPS, u % TPS
                pe.wait_ge(s["eT_ready"], at["eT_ready"] + i * U + u + 3)
                if j == 0:
                    pe.wait_ge(s["head_copied"], at["head_copied"] + i * 2 + hh + 2)
                last_c = TPS - 1 if n == 0 else j
                for c in range(last_c + 1):
                    last = mm(bank[OB][:, j * VW:(j + 1) * VW], eT[u % 2][:, c * P:(c + 1) * P],
                              v[:, bass.ds(i * 2 + hh + 2, 1), c, :], c == 0, c == last_c)
                if j == TPS - 1:
                    last.then_inc(s["head_ready"], 1)

            def body(bg, hp, i):
                for u in range(U):
                    score(bg, i, u)
                    turn(i, u - 1)
                    weigh(i, u - 2)

            pe.wait_ge(s["mean_read" if n == 0 else "head_copied"], at["mean_read" if n == 0 else "head_copied"] + 1)
            head_loops(pe, body)
            end = B * H // 2
            turn(end, -1)
            weigh(end, -2)
            weigh(end, -1)

        def pool_heads(pool, n):
            s, at = AS, HEADS_AT[n]

            def body(bg, hp, i):
                for hh in range(2):
                    k = "diff_ready" if n == 0 else "score_ready"
                    pool.wait_ge(s[k], at[k] + (i * 2 + hh) * TPS + TPS)
                    pool.tensor_tensor(qm[hh], qT[:, bass.ds(bg, 1), :].rearrange("p a s -> p (a s)"),
                                       head_mask[:, bass.ds(hp * 2 + hh, 1)].to_broadcast([P, S]), ALU.mult
                                       ).then_inc(s["qm_ready"], 1)
                if n == 0:
                    kn = knorm[:, bass.ds(i * 2, 2), :]
                    pool.tensor_tensor(kn, kn, half_pos[:].rearrange("p (h j) -> p h j", j=TPS), ALU.pow)

            head_loops(pool, body)

        def scalar_heads(act, n):
            s, at = AS, HEADS_AT[n]
            head_credits(act, n, ("expP_ready", "diff_read"))

            def body(bg, hp, i):
                for u in range(U):
                    hh, j = u // TPS, u % TPS
                    w = S if n == 0 else (j + 1) * P
                    row = (slice(None), bass.ds(i * 2 + hh + 2, 1), slice(j, j + 1))
                    act.wait_ge(s["bias_ready"], at["bias_ready"] + i * U + u + 1)
                    if n == 0:
                        act.wait_ge(s["scores_summed"], at["scores_summed"] + i * U + u + 3)
                        act.activation(eA[:, u % 2, :], bank[SB + u % 4][:], ACT.Exp, bias=nbias[:, u % 4, 0:1],
                                       scale=HD ** -0.5, accum_out=sum_exp_all[row])
                    act.wait_ge(s["turned"], at["turned"] + i * U + u + 1)
                    act.activation(eP[u % 2][:, 0:w], bank[SB + u % 4][:, 0:w], ACT.Exp, bias=nbias[:, u % 4, 1:2],
                                   scale=cpair[:, n // 2, 1:2]).then_inc(s["expP_ready"], 1)
                    if n == 0:
                        act.wait_ge(s["mean_read"], at["mean_read"] + i * U + u + 3)
                        act.activation(bank[FB + u % 2][:, 0:S - 1], bank[FB + u % 2][:, 0:S - 1], ACT.Abs,
                                       accum_out=sum_diff_all[row]).then_inc(s["diff_read"], 1)

            head_loops(act, body)

        def vector_heads(dve, n):
            s, at = AS, HEADS_AT[n]
            for z in (eP[1], eT[0], eT[1], v[:, 0:2, :, :], bank[OB][:, 0:TPS * VW], bank[SB + 3][:], eA[:, 1, :],
                      row8[:]):
                dve.memset(z, 0.0)
            head_credits(dve, n, ("head_copied", "eT_ready", "scores_summed", "mean_read"))
            if n == 2:
                dve.drain().then_inc(s["head_copied"], 1)

            def maximum(i, u):
                j = u % TPS
                w = S if n == 0 else (j + 1) * P
                dve.wait_ge(s["score_ready"], at["score_ready"] + i * U + u + 9)
                dve.tensor_reduce(row8[:, 0, u:u + 1], bank[SB + u % 4][:, 0:w], AX.X, ALU.max, negate=True)
                dve.drain()
                dve.tensor_tensor(nbias[:, u % 4, :], row8[:, 0, u:u + 1].to_broadcast([P, 2]), cpair[:, n // 2, :],
                                  ALU.mult).then_inc(s["bias_ready"], 1)
                if n == 0:
                    dve.wait_ge(s["diff_ready"], at["diff_ready"] + i * U + u + 9)
                    dve.tensor_copy(row8[:, 2, u:u + 1], bank[FB + u % 2][:, S - 1:S]).then_inc(s["mean_read"], 1)

            def entropy(i, u):
                dve.wait_ge(s["expP_ready"], at["expP_ready"] + i * U + u + 5)
                dve.tensor_tensor_reduce(eA[:, u % 2, :], eA[:, u % 2, :], bank[SB + u % 4][:], 1.0, 0.0, ALU.mult,
                                         ALU.add, row8[:, 1, u % U:u % U + 1]).then_inc(s["scores_summed"], 1)

            def copy_T(i, u):
                j = u % TPS
                w = S if n == 0 else (j + 1) * P
                dve.wait_ge(s["turned"], at["turned"] + i * U + u + 3)
                dve.tensor_copy(eT[u % 2][:, 0:w], bank[TB][:, 0:w]).then_inc(s["eT_ready"], 1)

            def copy_head(i, hh):
                dve.wait_ge(s["head_ready"], at["head_ready"] + i * 2 + hh + 2)
                dve.tensor_copy(raw[:, bass.ds(i * 2 + hh + 2, 1), :, :],
                                bank[OB][:, 0:TPS * VW].rearrange("p (o j e) -> p o j e", o=1, e=VW)
                                ).then_inc(s["head_copied"], 1)

            def keep(q, stat, i):
                dve.tensor_copy(stat[:, bass.ds(i * 2 + 2, 2), :], row8[:, q, :].rearrange("p (h j) -> p h j", j=TPS))

            def body(bg, hp, i):
                for u in range(U):
                    if u == 2:
                        copy_head(i, -1)
                    if u == TPS + 2:
                        copy_head(i, 0)
                    maximum(i, u)
                    if n == 0:
                        entropy(i, u - 1)
                    copy_T(i, u - 1)
                    if n == 0 and u == 0:
                        dve.drain()
                        keep(1, sum_es_all, i - 1)
                if n == 0:
                    dve.drain()
                    keep(0, neg_max_all, i)
                    keep(2, sum_s_all, i)
                    dve.drain()

            head_loops(dve, body)
            end = B * H // 2
            if n == 0:
                entropy(end, -1)
            copy_T(end, -1)
            if n == 0:
                dve.drain()
                keep(1, sum_es_all, end - 1)
            copy_head(end, -1)

        rowc = sb("rowc", [P, B * H, TPS])
        rowt = sb("rowt", [P, B * H, TPS])
        rowu = sb("rowu", [P, B * H, TPS])
        lnz = sb("lnz", [P, B * H, TPS])
        rfac = sb("rfac", [P, B * H, TPS])
        half_pos = sb("half_pos", [P, 2 * TPS])
        zeros = sb("zeros", [P, 1])
        lnz_ready = sem("lnz_ready")
        row_ready = sem("row_ready")
        fac_ready = sem("fac_ready")
        gate_exp = sem("gate_exp")
        gates_ready = sem("gates_ready")
        order_ready = sem("order_ready")
        order_pos = sb("order_pos", [P, TPS])
        gt = sb("gt", [P, 16])

        def scalar_gates(act):
            act.wait_ge(gates_loaded, 32)
            act.activation(gt[:, 0:5], gates[:], ACT.Exp, scale=-1.0).then_inc(gate_exp, 1)
            act.wait_ge(gates_ready, 1)
            act.activation(order_exp[:], order_pos[:], ACT.Exp, scale=gt[:, 7:8]).then_inc(order_ready, 1)

        def vector_gates(dve):
            dve.wait_ge(gate_exp, 1)
            dve.tensor_scalar(gt[:, 0:5], gt[:, 0:5], 1.0, None, ALU.add)
            dve.drain()
            dve.reciprocal(gt[:, 5:10], gt[:, 0:5])
            dve.drain()
            dve.tensor_scalar(cpair[:, 0, 1:2], gt[:, 8:9], -0.1 * HD ** -0.5, HD ** -0.5, ALU.mult, ALU.add)
            dve.memset(cpair[:, 0, 0:1], HD ** -0.5)
            dve.memset(cpair[:, 1, :], HD ** -0.5)
            dve.memset(half_neg[:], -0.5)
            dve.memset(half_pos[:], 0.5)
            dve.memset(comb[:], 0.0)
            dve.tensor_copy(identb[:], ident[:])
            dve.drain().then_inc(gates_ready, 1)
            dve.wait_ge(order_ready, 1)

        def vector_diffs(dve):
            for bg in range(B * NG):
                dve.tensor_tensor(kdT[:, bg, 0:S - 1], kT[:, bg, 1:S], kT[:, bg, 0:S - 1], ALU.subtract)
                dve.tensor_reduce(kdT[:, bg, S - 1:S], kT[:, bg, :], AX.X, ALU.add)

        def scalar_rows(act):
            act.activation(lnz[:], sum_exp, ACT.Ln).then_inc(lnz_ready, 1)
            act.wait_ge(row_ready, 1)
            act.activation(rfac[:], rowt[:], ACT.Exp).then_inc(fac_ready, 1)

        def vector_rows(dve):
            isq = HD ** -0.5
            dve.reciprocal(rowu[:], sum_exp)
            dve.drain()
            dve.tensor_tensor(rowu[:], rowu[:], sum_es, ALU.mult)
            dve.drain()
            dve.tensor_tensor(rowu[:], rowu[:], neg_max, ALU.add)
            dve.wait_ge(lnz_ready, 1)
            dve.drain()
            dve.tensor_scalar(rowu[:], rowu[:], isq, None, ALU.mult)
            dve.drain()
            dve.tensor_tensor(rowu[:], rowu[:], lnz[:], ALU.subtract)
            dve.drain()
            dve.tensor_scalar(rowu[:], rowu[:], gt[:, 6:7], -0.1 / LN_S, ALU.mult, ALU.mult)
            dve.tensor_scalar(rowt[:], knorm[:], gt[:, 5:6], -0.01, ALU.mult, ALU.mult)
            dve.drain()
            dve.tensor_tensor(rowc[:], rowu[:], rowt[:], ALU.add)
            dve.drain()
            dve.tensor_scalar(rowu[:], sum_s, gt[:, 8:9], 0.1 * isq / S, ALU.mult, ALU.mult)
            dve.drain()
            dve.tensor_tensor(rowc[:], rowc[:], rowu[:], ALU.add)
            dve.drain()
            dve.tensor_scalar(rowt[:], sum_diff, gt[:, 9:10], -0.1 * isq / (S - 1), ALU.mult, ALU.mult)
            dve.drain()
            dve.tensor_tensor(rowc[:], rowc[:], rowt[:], ALU.add)
            dve.drain()
            dve.tensor_scalar(rowu[:], neg_max, cpair[:, 0, 1:2], -1.0, ALU.mult, ALU.mult)
            dve.drain()
            dve.tensor_tensor(lnz[:], rowc[:], rowu[:], ALU.add)
            dve.drain()
            dve.tensor_tensor(rowt[:], rowc[:], lnz[:], ALU.subtract)
            dve.drain()
            dve.tensor_tensor(rowt[:], rowt[:], rowu[:], ALU.add).then_inc(row_ready, 1)
            dve.wait_ge(fac_ready, 1)
            for t in range(NT):
                r = raw[:, 2:, :, :][:, heads_of(t), t % TPS, :]
                dve.tensor_tensor(r, r, rfac[:, heads_of(t), t % TPS].unsqueeze(2).to_broadcast([P, H, VW]), ALU.mult)
            dve.drain()
            vector_divide(dve)

        def vector_divide(dve):
            dve.reciprocal(rowu[:], raw[:, 2:, :, HD])
            dve.drain()
            for t in range(NT):
                dve.tensor_tensor(ao[:, t, :].rearrange("p (h e) -> p h e", e=HD), 
                                  raw[:, 2:, :, :][:, heads_of(t), t % TPS, 0:HD],
                                  rowu[:, heads_of(t), t % TPS].unsqueeze(2).to_broadcast([P, H, HD]), ALU.mult)

        qx = part(1, [P, 2, GH, P])
        sD = [part(1, [P, 4 * P]) for i in range(4)]
        state = part(1, [P, NG, P])
        stmp = part(1, [P, NG, P])
        g1T = part(1, [P, TOK])[0:HD, :]
        gsig = part(1, [P, 2, D])
        ms = sb("ms", [P, NT, H])
        L1 = {k: sem(f"lin_{k}") for k in ("g1_ready", "g1_copied", "qx_ready", "qx_used", "sc_ready", "sc_masked",
                                            "own_ready", "own_read", "st_ready", "st_done", "gate_ready", "gate_th",
                                            "gate_read", "gated", "ms_ready", "ms_root")}

        def tensor_linear(pe):
            s = L1
            for c in range(2):
                for k in range(KD):
                    last = mm(bank[c][0:HD, :], wg1[:, k, :], xnT[:, k, c * 512:(c + 1) * 512], k == 0, k == KD - 1)
                last.then_inc(s["g1_ready"], 1)
            pe.wait_ge(s["g1_copied"], 2)

            def scores(t):
                for g in range(NG):
                    pe.wait_ge(s["qx_ready"], t * NG + g + 1)
                    if t:
                        pe.wait_ge(s["sc_masked"], 2 * ((t - 1) * NG + g + 1))
                    for c in range(2):
                        last = mm(bank[2 * g + c][:], kT[group_of(t)][:, g, :],
                                  qx[:, g, 4 * c:4 * c + 4, :].rearrange("p h t -> p (h t)"))
                    last.then_inc(s["sc_ready"], 1)

            scores(0)
            for t in range(NT):
                first = t % TPS == 0
                if t:
                    pe.wait_ge(s["gate_read"], t)
                mm(bank[7][:, 0:D], g1T[:, t * P:(t + 1) * P], wg2[:]).then_inc(s["gate_ready"], 1)
                if t:
                    pe.wait_ge(s["st_done"], t)
                for g in range(NG):
                    last = mm(bank[6][:, g * P:(g + 1) * P], kd[:, t, g * P:(g + 1) * P], v_of(t, g * GH, GH)[:, :, 0:HD])
                last.then_inc(s["st_ready"], 1)
                if t >= 2:
                    pe.wait_ge(s["own_read"], t - 1)
                if not first:
                    for g in range(NG):
                        mm(bank[4 + t % 2][:, D + g * P:D + (g + 1) * P], qT[group_of(t)][:, g, :], state[:, g, :])
                for g in range(NG):
                    pe.wait_ge(s["sc_masked"], 2 * (t * NG + g + 1))
                    for hh in range(GH):
                        h = g * GH + hh
                        last = mm(bank[4 + t % 2][:, h * HD:(h + 1) * HD],
                                  sD[2 * g + hh // 4][:, (hh % 4) * P:(hh % 4 + 1) * P], v_of(t, h, 1)[:, 0, 0:HD])
                last.then_inc(s["own_ready"], 1)
                if t + 1 < NT:
                    scores(t + 1)

        def scalar_linear(act):
            s = L1
            for c in range(2):
                act.wait_ge(s["g1_ready"], c + 1)
                act.activation(g1T[:, c * 512:(c + 1) * 512], bank[c][0:HD, :], ACT.Copy).then_inc(s["g1_copied"], 1)
            for t in range(NT):
                act.wait_ge(s["gate_ready"], t + 1)
                if t >= 2:
                    act.wait_ge(s["gated"], t - 1)
                act.activation(gsig[:, t % 2, :], bank[7][:, 0:D], ACT.Tanh, scale=0.5).then_inc(s["gate_read"], 1)

        def vector_linear(dve):
            s = L1

            def mask(t):
                for g in range(NG):
                    dve.wait_ge(s["sc_ready"], t * NG + g + 1)
                    for c in range(2):
                        h = g * GH + 4 * c
                        dve.tensor_tensor(sD[2 * g + c][:], bank[2 * g + c][:],
                                          decay[:, h:h + 4, :].rearrange("p h t -> p (h t)"), ALU.mult
                                          ).then_inc(s["sc_masked"], 1)

            def normalise(t):
                dve.wait_ge(s["ms_root"], t + 1)
                o = ao[:, t, :].rearrange("p (h e) -> p h e", e=HD)
                dve.tensor_tensor(o, o, ms[:, t, :].unsqueeze(2).to_broadcast([P, H, HD]), ALU.mult)
                dve.drain()
                dve.scalar_tensor_tensor(ao[:, t, :], ao[:, t, :], 0.5, norm_w[:], ALU.mult, ALU.mult)

            mask(0)
            for t in range(NT):
                first = t % TPS == 0
                part_of = bank[4 + t % 2]
                dve.wait_ge(s["own_ready"], t + 1)
                dve.wait_ge(s["st_ready"], t + 1)
                new = bank[6][:, 0:D].rearrange("p (g e) -> p g e", g=NG)
                dve.tensor_tensor(stmp[:], new, own_block[:].unsqueeze(1).to_broadcast([P, NG, P]), ALU.mult)
                if first:
                    dve.drain()
                    dve.tensor_copy(state[:], stmp[:]).then_inc(s["st_done"], 1)
                else:
                    dve.tensor_tensor(state[:], state[:], lam_chunk[:], ALU.mult)
                    dve.drain()
                    dve.tensor_tensor(state[:], state[:], stmp[:], ALU.add).then_inc(s["st_done"], 1)
                o = ao[:, t, :].rearrange("p (h e) -> p h e", e=HD)
                if first:
                    dve.tensor_copy(ao[:, t, :], part_of[:, 0:D]).then_inc(s["own_read"], 1)
                else:
                    dve.tensor_tensor(o, part_of[:, D:2 * D].rearrange("p (h e) -> p h e", e=HD),
                                      decay_q[:].unsqueeze(2).to_broadcast([P, H, HD]), ALU.mult)
                    dve.drain()
                    dve.tensor_tensor(ao[:, t, :], ao[:, t, :], part_of[:, 0:D], ALU.add).then_inc(s["own_read"], 1)
                if t + 1 < NT:
                    mask(t + 1)
                dve.drain()
                dve.wait_ge(s["gate_read"], t + 1)
                dve.scalar_tensor_tensor(ao[:, t, :], gsig[:, t % 2, :], 1.0, ao[:, t, :], ALU.add, ALU.mult
                                         ).then_inc(s["gated"], 1)
                dve.drain()
                dve.tensor_tensor(tmp[:, 0, 0:D], ao[:, t, :], ao[:, t, :], ALU.mult)
                dve.drain()
                dve.tensor_reduce(ms[:, t, :], tmp[:, 0, 0:D].rearrange("p (h e) -> p h e", e=HD), AX.X, ALU.add)
                dve.drain()
                dve.tensor_scalar(ms[:, t, :], ms[:, t, :], 0.25 / HD, 1e-6, ALU.mult, ALU.add).then_inc(s["ms_ready"], 1)
                if t >= 2:
                    normalise(t - 2)
            normalise(NT - 2)
            normalise(NT - 1)

        def pool_linear(pool):
            def root(t):
                pool.wait_ge(L1["ms_ready"], t + 1)
                pool.tensor_tensor(ms[:, t, :], ms[:, t, :], half_neg[:, 0:H], ALU.pow).then_inc(L1["ms_root"], 1)

            for t in range(NT):
                for g in range(NG):
                    if t:
                        pool.wait_ge(L1["sc_ready"], (t - 1) * NG + g + 1)
                    pool.tensor_tensor(qx[:, g, :, :], qT[group_of(t)][:, g, :].unsqueeze(1).to_broadcast([P, GH, P]),
                                       head_mask[:].unsqueeze(2).to_broadcast([P, GH, P]), ALU.mult
                                       ).then_inc(L1["qx_ready"], 1)
                if t >= 2:
                    root(t - 2)
            root(NT - 2)
            root(NT - 1)

        def vector_route(dve, n):
            s, at = LS, AT[n]
            E = EXPERTS[n]
            if n == 3:
                for t in range(NT):
                    dve.wait_ge(s["logits_ready"], at["logits_ready"] + t + 1)
                    dve.tensor_copy(logits[:, t, 0:16], bank[t % 2][:, 0:16])
                    dve.tensor_copy(shared[:, t:t + 1], bank[t % 2][:, 16:17])
                    dve.drain().then_inc(s["logits_copied"], 1)
            lg, pr, cm = logits[:, :, 0:E], probs[:, :, 0:E], comb[:, :, 0:E]

            def wide(r):
                return r[:].unsqueeze(2).to_broadcast([P, NT, E])

            dve.drain()
            dve.tensor_reduce(rowm[:], lg, AX.X, ALU.max)
            dve.drain()
            dve.tensor_tensor(pr, lg, wide(rowm), ALU.subtract)
            dve.drain().then_inc(s["route_exp"], 1)
            dve.wait_ge(s["route_exp"], at["route_exp"] + 2)
            if n != 2:
                dve.tensor_reduce(rowz[:], pr, AX.X, ALU.add)
                dve.drain()
                dve.reciprocal(rowz[:], rowz[:])
                dve.drain()
                dve.tensor_tensor(pr, pr, wide(rowz), ALU.mult)
                dve.drain()
            key = lg if n == 2 else pr
            for t in range(NT):
                ahead = key[:, t, :].unsqueeze(1).to_broadcast([P, E, E])
                own = key[:, t, :].unsqueeze(2).to_broadcast([P, E, E])
                dve.tensor_tensor(rank[:, 0:E, 0:E], ahead, own, ALU.is_gt)
                dve.tensor_tensor(rank2[:, 0:E, 0:E], ahead, own, ALU.is_equal)
                dve.drain()
                dve.tensor_tensor(rank2[:, 0:E, 0:E], rank2[:, 0:E, 0:E], lower[:, 0:E, 0:E], ALU.mult)
                dve.drain()
                dve.tensor_tensor(rank[:, 0:E, 0:E], rank[:, 0:E, 0:E], rank2[:, 0:E, 0:E], ALU.add)
                dve.drain()
                dve.tensor_reduce(rankn[:, t, 0:E], rank[:, 0:E, 0:E], AX.X, ALU.add)
                dve.drain()
            dve.tensor_scalar(rankn[:, :, 0:E], rankn[:, :, 0:E], float(TOPK[n]), None, ALU.is_lt)
            dve.drain()
            dve.tensor_tensor(cm, rankn[:, :, 0:E], pr, ALU.mult)
            dve.drain()
            if n != 1:
                dve.tensor_reduce(rowz[:], cm, AX.X, ALU.add)
                dve.drain()
                dve.reciprocal(rowz[:], rowz[:])
                dve.drain()
                dve.tensor_tensor(cm, cm, wide(rowz), ALU.mult)
                dve.drain()
            dve.tensor_scalar(cm, cm, 0.5, None, ALU.mult)
            if n == 1:
                dve.memset(comb[:, :, E:E + 1], 0.5)
            if n == 2:
                dve.memset(comb[:, :, E:E + 1], 0.0)
            if n == 3:
                dve.tensor_scalar(comb[:, :, E], shared[:], 1.0, 0.25, ALU.add, ALU.mult)
            dve.drain()
            hi, mid, lo = (combp[:, :, i * NE:(i + 1) * NE] for i in range(3))
            rest = rank[:].rearrange("p a b -> p (a b)")[:, 0:NT * NE].rearrange("p (t e) -> p t e", e=NE)
            dve.tensor_copy(hi, comb[:])
            dve.drain()
            dve.tensor_tensor(rest, comb[:], hi, ALU.subtract)
            dve.drain()
            dve.tensor_copy(mid, rest)
            dve.drain()
            dve.tensor_tensor(lo, rest, mid, ALU.subtract)
            dve.drain().then_inc(s["comb_T"], 1)
            dve.wait_ge(s["comb_T"], at["comb_T"] + 2)
            dve.tensor_copy(combT[:], bankb)
            if n == 2:
                dve.wait_ge(s["comb_T"], at["comb_T"] + 3)
                dve.tensor_copy(combF[0:8, :], bank[6][0:8, :])
                dve.tensor_copy(combF2[0:8, :], bank[7][0:8, :])
                dve.drain()

        bankb = bank[5][0:CR, :].bitcast(BF16)
        combF = sb("combF", [8, 512])
        combF2 = sb("combF2", [8, 512])

        def scalar_route(act, n):
            s, at = LS, AT[n]
            E = EXPERTS[n]
            act.wait_ge(s["route_exp"], at["route_exp"] + 1)
            act.activation(probs[:, :, 0:E], probs[:, :, 0:E], ACT.Exp)
            if n == 3:
                act.activation(shared[:], shared[:], ACT.Tanh, scale=0.5)
            act.drain().then_inc(s["route_exp"], 1)

        def tensor_route(pe, n):
            s, at = LS, AT[n]
            if n == 3:
                for t in range(NT):
                    if t >= 2:
                        pe.wait_ge(s["logits_copied"], at["logits_copied"] + t - 1)
                    for k in range(KD):
                        last = mm(bank[t % 2][:, 0:NE], xnT[:, k, t * P:(t + 1) * P], router[3][:, k, :],
                                  k == 0, k == KD - 1)
                    last.then_inc(s["logits_ready"], 1)
            pe.wait_ge(s["comb_T"], at["comb_T"] + 1)
            for t in range(NT):
                last = nc.tensor.transpose(bankb[:, t * P:(t + 1) * P], combp[:, t, :], identb[:])
            last.then_inc(s["comb_T"], 1)
            if n == 2:
                for t in range(NT):
                    last = nc.tensor.transpose(bank[6 + t // 4][0:8, (t % 4) * P:(t % 4 + 1) * P], comb[:, t, 0:8], ident[:])
                last.then_inc(s["comb_T"], 1)


        def sync_ffn(sp, n, first, count):
            s, at = LS, AT[n]
            base = sum(CHUNKS[:n])
            with sp.Fori(first, first + count) as p:
                sp.wait_ge(s["guA_used"], at["guA_used"] + p + 1)
                sp.dma_start(wgu[0][:], a["gu"][bass.ds(p * 2 + base, 1), :, :].rearrange("a p n -> (a p) n")).then_inc(s["guA_loaded"], 16)
                if n:
                    sp.dma_start(sel[0][:], a[f"sel{n}"][bass.ds(p * 2, 1), :, :].rearrange("a p n -> (a p) n")).then_inc(s["guA_loaded"], 16)
                sp.wait_ge(s["guB_used"], at["guB_used"] + p + 1)
                sp.dma_start(wgu[1][:], a["gu"][bass.ds(p * 2 + base + 1, 1), :, :].rearrange("a p n -> (a p) n")).then_inc(s["guB_loaded"], 16)
                if n:
                    sp.dma_start(sel[1][:], a[f"sel{n}"][bass.ds(p * 2 + 1, 1), :, :].rearrange("a p n -> (a p) n")).then_inc(s["guB_loaded"], 16)
                sp.wait_ge(s["down_used"], at["down_used"] + p + 1)
                sp.dma_start(wd[:], a["down"][bass.ds(p * 2 + base, 2), :, :].rearrange("a p n -> p a n")).then_inc(s["down_loaded"], 16)

        def tensor_ffn_start(pe, n):
            s, at = LS, AT[n]
            if n == 0:
                for k in ("guA_used", "guB_used", "down_used"):
                    pe.drain().then_inc(s[k], 1)

        def gate_bank(n, u):
            return bank[u % 2 if n < 3 else 4]

        def up_bank(n, u):
            return bank[2 + u % 2 if n < 3 else 5]

        def comb_bank(n, u):
            return bank[4 + u % 2 if n < 3 else 6]

        def part_bank(n, q):
            return bank[6 + q if n < 3 else 7]

        def lag(n):
            return 1 if n < 3 else 2

        def tensor_gate_up(pe, n, p, u):
            s, at = LS, AT[n]
            half, c = u // 2, u % 2
            if half == 0:
                inc = 32 if n else 16
                pe.wait_ge(s["guB_loaded" if c else "guA_loaded"], at["guA_loaded"] + p * inc + inc)
            ts = slice(half * 512, half * 512 + 512)
            pe.wait_ge(s["gate_used"], at["gate_used"] + p * 4 + u + lag(n))
            for k in range(KD):
                last = mm(gate_bank(n, u)[:], wgu[c][:, k * P:(k + 1) * P], xnT[:, k, ts], k == 0, k == KD - 1)
            last.then_inc(s["gate_ready"], 1)
            pe.wait_ge(s["up_used"], at["up_used"] + p * 4 + u + lag(n))
            for k in range(KD):
                last = mm(up_bank(n, u)[:], wgu[c][:, (2 + k) * P:(3 + k) * P], xnT[:, k, ts], k == 0, k == KD - 1)
            last.then_inc(s["up_ready"], 1)
            if n:
                pe.wait_ge(s["comb_used"], at["comb_used"] + p * 4 + u + lag(n))
                mm(comb_bank(n, u)[:], sel[c][:], combT[:, ts]).then_inc(s["comb_ready"], 1)
            if half == 1:
                pe.drain().then_inc(s["guB_used" if c else "guA_used"], 1)

        def tensor_down(pe, n, p, half, q):
            s, at = LS, AT[n]
            if half == 0 and q == 0:
                pe.wait_ge(s["down_loaded"], at["down_loaded"] + p * 16 + 16)
            pe.wait_ge(s["h_ready"], at["h_ready"] + p * 4 + 2 * half + 2)
            pe.wait_ge(s["part_added"], at["part_added"] + p * 4 + 2 * half + q + lag(n))
            for r in range(2):
                t = 2 * q + r
                for c in range(2):
                    last = mm(part_bank(n, q)[:, r * D:(r + 1) * D], hT[:, 2 * half + c, t * P:(t + 1) * P], wd[:, c, :],
                              c == 0, c == 1)
            last.then_inc(s["part_ready"], 1)
            if half == 1 and q == 1:
                pe.drain().then_inc(s["down_used"], 1)

        def tensor_ffn(pe, n):
            def rest(p):
                tensor_gate_up(pe, n, p, 1)
                tensor_gate_up(pe, n, p, 2)
                tensor_gate_up(pe, n, p, 3)
                for q in range(2):
                    tensor_down(pe, n, p, 0, q)

            def down_1(p):
                for q in range(2):
                    tensor_down(pe, n, p, 1, q)

            tensor_gate_up(pe, n, 0, 0)
            rest(0)
            with pe.Fori(1, CHUNKS[n] // 2) as p:
                tensor_gate_up(pe, n, p, 0)
                down_1(p - 1)
                rest(p)
            down_1(CHUNKS[n] // 2 - 1)

        def scalar_unit(act, n, p, u):
            s, at = LS, AT[n]
            if n == 2:
                act.wait_ge(s["gate_clipped"], at["gate_clipped"] + p * 4 + u + 1)
                act.activation(th[:, u % 2, :], gl[:, u % 2, :], ACT.Tanh, scale=0.5 * 1.702).then_inc(s["tanh_ready"], 1)
            else:
                act.wait_ge(s["gate_ready"], at["gate_ready"] + p * 4 + u + 1)
                act.activation(th[:, u % 2, :], gate_bank(n, u)[:], ACT.Tanh, scale=0.5).then_inc(s["tanh_ready"], 1)

        def scalar_ffn(act, n):
            with act.Fori(0, CHUNKS[n] // 2) as p:
                for u in range(4):
                    scalar_unit(act, n, p, u)

        def vector_ffn_start(dve, n):
            s, at = LS, AT[n]
            if n == 0:
                for k in ("gate_used", "up_used", "part_added", "comb_used"):
                    dve.drain().then_inc(s[k], 2)

        def vector_clip(dve, p, u):
            s, at = LS, AT[2]
            dve.wait_ge(s["gate_ready"], at["gate_ready"] + p * 4 + u + 1)
            dve.tensor_scalar(gl[:, u % 2, :], gate_bank(2, u)[:], gu_bias[:, bass.ds(p * 2 + u % 2, 1), 0:1], 7.0,
                              ALU.add, ALU.min).then_inc(s["gate_clipped"], 1)
            dve.drain().then_inc(s["gate_used"], 1)

        def vector_unit(dve, n, p, u):
            s, at = LS, AT[n]
            i, h = u % 2, hT[:, u, :]
            if n == 2:
                dve.wait_ge(s["up_ready"], at["up_ready"] + p * 4 + u + 1)
                dve.tensor_scalar(up[:, i, :], up_bank(n, u)[:], gu_bias[:, bass.ds(p * 2 + u % 2, 1), 1:2], 8.0,
                                  ALU.add, ALU.min).then_inc(s["up_used"], 1)
                dve.wait_ge(s["tanh_ready"], at["tanh_ready"] + p * 4 + u + 1)
                dve.scalar_tensor_tensor(gl[:, i, :], th[:, i, :], 1.0, gl[:, i, :], ALU.add, ALU.mult)
                dve.drain()
                dve.scalar_tensor_tensor(gl[:, i, :], up[:, i, :], -6.0, gl[:, i, :], ALU.max, ALU.mult)
                dve.drain()
            else:
                dve.wait_ge(s["tanh_ready"], at["tanh_ready"] + p * 4 + u + 1)
                dve.scalar_tensor_tensor(gl[:, i, :], th[:, i, :], 1.0, gate_bank(n, u)[:], ALU.add, ALU.mult
                                         ).then_inc(s["gate_used"], 1)
                dve.drain()
                dve.wait_ge(s["up_ready"], at["up_ready"] + p * 4 + u + 1)
                if n == 0:
                    dve.scalar_tensor_tensor(h, gl[:, i, :], 0.5, up_bank(n, u)[:], ALU.mult, ALU.mult
                                             ).then_inc(s["up_used"], 1)
                else:
                    dve.tensor_tensor(gl[:, i, :], gl[:, i, :], up_bank(n, u)[:], ALU.mult).then_inc(s["up_used"], 1)
                    dve.drain()
            if n:
                dve.wait_ge(s["comb_ready"], at["comb_ready"] + p * 4 + u + 1)
                dve.tensor_tensor(h, gl[:, i, :], comb_bank(n, u)[:], ALU.mult).then_inc(s["comb_used"], 1)
            dve.drain().then_inc(s["h_ready"], 1)

        def vector_add(dve, n, p, half, q):
            s, at = LS, AT[n]
            dve.wait_ge(s["part_ready"], at["part_ready"] + p * 4 + 2 * half + q + 1)
            t = half * TPS + 2 * q
            dve.tensor_tensor(x[:, t:t + 2, :], x[:, t:t + 2, :],
                              part_bank(n, q)[:].rearrange("p (t n) -> p t n", n=D), ALU.add).then_inc(s["part_added"], 1)

        def vector_ffn(dve, n):
            pairs = CHUNKS[n] // 2

            def unit(p, u, then=None):
                if n == 2 and then:
                    vector_clip(dve, *then)
                vector_unit(dve, n, p, u)

            def rest(p, after):
                unit(p, 1, (p, 2))
                unit(p, 2, (p, 3))
                unit(p, 3, after)
                for q in range(2):
                    vector_add(dve, n, p, 0, q)

            def add_1(p):
                for q in range(2):
                    vector_add(dve, n, p, 1, q)

            if n == 2:
                dve.tensor_scalar(gu_bias[:, :, 1:2], gu_bias[:, :, 1:2], 1.0, None, ALU.add)
                dve.drain()
                vector_clip(dve, 0, 0)
            unit(0, 0, (0, 1))
            rest(0, (1, 0))
            with dve.Fori(1, pairs - 1) as p:
                unit(p, 0, (p, 1))
                add_1(p - 1)
                rest(p, (p + 1, 0))
            unit(pairs - 1, 0, (pairs - 1, 1))
            add_1(pairs - 2)
            rest(pairs - 1, None)
            add_1(pairs - 1)

        bias2_ready = sem("bias2_ready")
        bias2_added = sem("bias2_added")

        def tensor_bias2(pe):
            for t in range(NT):
                if t >= 2:
                    pe.wait_ge(bias2_added, t - 1)
                cf = (combF, combF2)[t // 4]
                mm(bank[t % 2][:, 0:D], cf[:, (t % 4) * P:(t % 4 + 1) * P], dbias[:]).then_inc(bias2_ready, 1)

        def vector_bias2(dve):
            for t in range(NT):
                dve.wait_ge(bias2_ready, t + 1)
                dve.scalar_tensor_tensor(x[:, t, :], bank[t % 2][:, 0:D], 2.0, x[:, t, :], ALU.mult, ALU.add
                                         ).then_inc(bias2_added, 1)

        wq3 = wpart(3, [P, KD, H3 * HD3])
        wk3 = wpart(3, [P, H3 * HD3])
        wv3 = wpart(3, [P, H3 * HD3])
        wo3 = wpart(3, [P, H3, D])
        mem = sb("mem", [P, 2, P])
        memT = sb("memT", [P, MEM])
        aff = sb("aff", [P, 6])
        lbeta = sb("lbeta", [P, H3])
        st3 = sb("st3", [P, NT + 2, 6])
        mv3 = sb("mv3", [P, NT + 2, 2])
        rs3 = sb("rs3", [P, NT + 2])
        nm3 = sb("nm3", [P, NT + 2])
        K3 = part(3, [P, H3, MEM])
        V3 = part(3, [P, 2, H3 * HD3])
        xi = [part(3, [P, 512]) for i in range(2)]
        sc3 = [[part(3, [P, TPS, MEM]) for i in range(2)] for g in range(2)]
        re3 = [part(3, [P, 2, TPS, MEM]) for g in range(2)]
        xn3 = re3[1].rearrange("p i t m -> p (i t m)").rearrange("p (t d) -> p t d", d=D)
        wT3 = [part(3, [P, 2, 512]) for i in range(2)]
        mx3 = sb("mx3", [P, 2, TPS])
        tau, s1, s2, na, nb = [[sb(f"{k}{g}", [P, 2, TPS]) for g in range(2)] for k in ("tau", "s1_", "s2_", "na", "nb")]
        N3 = {k: sem(f"mem_{k}") for k in ("stats", "rstd", "normed", "turned", "copied", "kv_ready", "kv_copied",
                                            "beta", "norm1", "q_ready", "xi_ready", "filled", "taken", "rel_last",
                                            "w_ready", "w_T", "wT_ready", "wq_ready", "vo_ready")}
        tau_ready = [sem(f"mem_tau_ready{g}") for g in range(2)]
        relu_ready = [sem(f"mem_relu_ready{g}") for g in range(2)]

        def scalar_norm3(act):
            for t in range(NT):
                act.activation(xn3[:, t, :], x[:, t, :], ACT.Identity, bias=nmr[:, t:t + 1], scale=rstd[:, t:t + 1])
            act.drain().then_inc(N3["norm1"], 1)
            act.activation(lbeta[:], lbeta[:], ACT.Exp)
            act.drain().then_inc(N3["beta"], 1)
            act.wait_ge(N3["rstd"], 1)
            for t in range(NT):
                act.activation(xn3[:, t, :], xn3[:, t, :], ACT.Identity, bias=nm3[:, t:t + 1], scale=rs3[:, t:t + 1]
                               ).then_inc(N3["normed"], 1)
            for m in range(2):
                act.activation(mem[:, m, :], mem[:, m, :], ACT.Identity, bias=nm3[:, NT + m:NT + m + 1],
                               scale=rs3[:, NT + m:NT + m + 1]).then_inc(N3["normed"], 1)

        def vector_norm3(dve):
            dve.wait_ge(N3["norm1"], 1)
            for t in range(NT):
                dve.bn_stats(st3[:, t, :], xn3[:, t, :])
            for m in range(2):
                dve.bn_stats(st3[:, NT + m, :], mem[:, m, :])
            dve.drain()
            for t in range(NT + 2):
                dve.bn_aggr(mv3[:, t, :], st3[:, t, :])
            dve.drain().then_inc(N3["stats"], 1)
            dve.wait_ge(N3["beta"], 1)
            dve.tensor_scalar(lbeta[:], lbeta[:], 0.5, None, ALU.mult)
            dve.drain()
            for t in range(NT):
                dve.wait_ge(N3["turned"], t + 1)
                for k in range(KD):
                    dve.tensor_scalar(aoT[:, k, t * P:(t + 1) * P], bank[t % 2][:, k * P:(k + 1) * P],
                                      aff[:, k:k + 1], aff[:, 2 + k:3 + k], ALU.mult, ALU.add)
                dve.drain().then_inc(N3["copied"], 1)
            dve.wait_ge(N3["turned"], NT + 1)
            dve.tensor_scalar(memT[:], bank[2][:, 0:MEM], aff[:, 4:5], aff[:, 5:6], ALU.mult, ALU.add)
            dve.drain().then_inc(N3["copied"], 1)
            for h in range(H3):
                dve.wait_ge(N3["kv_ready"], h + 1)
                dve.tensor_scalar(K3[:, h, :], bank[4 + h % 2][:, 0:MEM], lbeta[:, h:h + 1], None, ALU.mult
                                  ).then_inc(N3["kv_copied"], 1)
            for c in range(4):
                dve.wait_ge(N3["kv_ready"], H3 + c + 1)
                dve.tensor_copy(V3[:, c // 2, (c % 2) * 512:(c % 2 + 1) * 512], bank[4 + c % 2][:]
                                ).then_inc(N3["kv_copied"], 1)

        def pool_norm3(pool):
            pool.wait_ge(N3["stats"], 1)
            pool.tensor_scalar(rs3[:], mv3[:, :, 1], LN_EPS, None, ALU.add)
            pool.drain()
            pool.tensor_tensor(rs3[:], rs3[:], half_neg[:, 0:NT + 2], ALU.pow)
            pool.drain()
            pool.tensor_tensor(nm3[:], mv3[:, :, 0], rs3[:], ALU.mult)
            pool.drain()
            pool.tensor_scalar(nm3[:], nm3[:], -1.0, None, ALU.mult)
            pool.drain().then_inc(N3["rstd"], 1)

        def tensor_norm3(pe):
            for t in range(NT):
                pe.wait_ge(N3["normed"], t + 1)
                if t >= 2:
                    pe.wait_ge(N3["copied"], t - 1)
                for k in range(KD):
                    last = nc.tensor.transpose(bank[t % 2][:, k * P:(k + 1) * P], xn3[:, t, k * P:(k + 1) * P], ident[:])
                last.then_inc(N3["turned"], 1)
            pe.wait_ge(N3["normed"], NT + 2)
            for m in range(2):
                last = nc.tensor.transpose(bank[2][:, m * P:(m + 1) * P], mem[:, m, :], ident[:])
            last.then_inc(N3["turned"], 1)
            pe.wait_ge(N3["copied"], NT + 1)
            for h in range(H3):
                if h >= 2:
                    pe.wait_ge(N3["kv_copied"], h - 1)
                mm(bank[4 + h % 2][:, 0:MEM], wk3[:, h * HD3:(h + 1) * HD3], memT[:]).then_inc(N3["kv_ready"], 1)
            for c in range(4):
                pe.wait_ge(N3["kv_copied"], H3 + c - 1)
                mm(bank[4 + c % 2][:], memT[:, (c // 2) * P:(c // 2 + 1) * P], wv3[:, (c % 2) * 512:(c % 2 + 1) * 512]
                   ).then_inc(N3["kv_ready"], 1)

        assert CHUNKS[3] // 2 == H3 // 2 * STEPS3 + 2
        USAGE = {"step00": 0, "step10": 1, "step01": 2, "step11": 3, "end0": 4, "start0": 5, "end1": 6, "start1": 7}
        wq_s = [part(3, [P, KD, HD3]) for g in range(2)]
        v3_s = [part(3, [P, 2, HD3]) for g in range(2)]
        wo3_s = [part(3, [P, D]) for g in range(2)]

        def usage(hp, what, final=False):
            return 2 + hp * 8 + USAGE[what] - (final and what == "end1")

        def weights_at(hp, g, st):
            return hp * 6 + 2 * st + g

        def tensor_query(pe, g, pair, us):
            pe.wait_ge(N3["wq_ready"], pair + 1)
            for i in range(2):
                pe.wait_ge(N3["taken"], us * 2 + i + 1)
                for k in range(KD):
                    last = mm(bank[2 * i][:], wq_s[g][:, k, :], aoT[:, k, i * 512:(i + 1) * 512], k == 0, k == KD - 1)
                last.then_inc(N3["q_ready"], 1)

        def tensor_score(pe, g, pair, us):
            for i in range(2):
                pe.wait_ge(N3["xi_ready"], us * 2 + i + 1)
                for t in range(TPS):
                    last = mm(bank[2 * i + t // 2][:, (t % 2) * MEM:(t % 2 + 1) * MEM], xi[i][:, t * P:(t + 1) * P],
                              K3[:, bass.ds(pair * 2 + g, 1), :])
                last.then_inc(N3["filled"], 1)

        def tensor_state(pe, g, us, wn):
            for i in range(2):
                pe.wait_ge(N3["taken"], us * 2 + i + 1)
                pe.wait_ge(N3["w_ready"], wn * 2 + i + 1)
                for m in range(2):
                    for t in range(TPS):
                        last = nc.tensor.transpose(bank[2 * i + m][:, t * P:(t + 1) * P],
                                                   re3[g][:, i, t, m * P:(m + 1) * P], ident[:])
                last.then_inc(N3["w_T"], 1)
            for i in range(2):
                pe.wait_ge(N3["wT_ready"], wn * 2 + i + 1)
                for m in range(2):
                    last = mm(bank[2 * i][:], v3_s[g][:, m, :], wT3[i][:, m, :], m == 0, m == 1)
                last.then_inc(N3["q_ready"], 1)

        def tensor_give(pe, g, us):
            for i in range(2):
                pe.wait_ge(N3["xi_ready"], us * 2 + i + 1)
                for t in range(TPS):
                    last = mm(bank[2 * i + t // 2][:, (t % 2) * D:(t % 2 + 1) * D], xi[i][:, t * P:(t + 1) * P],
                              wo3_s[g][:])
                last.then_inc(N3["filled"], 1)

        def tensor_turn3(pe, hp, final=False):
            for st in range(STEPS3):
                p = hp * STEPS3 + st + 2
                for g in range(2):
                    us = usage(hp, f"step{g}{st}" if st < 2 else f"end{g}", final)
                    if st == 0:
                        pe.wait_ge(N3["vo_ready"], hp * 2 + g + 1)
                    tensor_state(pe, g, us, weights_at(hp, g, st))
                    if st < 2:
                        tensor_score(pe, g, hp, us)
                    else:
                        tensor_give(pe, g, us)
                        if not final:
                            tensor_query(pe, g, hp + 1, us + 1)
                            tensor_score(pe, g, hp + 1, us + 1)
                    if g == 0:
                        tensor_down(pe, 3, p - 1, 1, 0)
                        tensor_down(pe, 3, p - 1, 1, 1)
                        tensor_gate_up(pe, 3, p, 0)
                tensor_units3(pe, p)

        def tensor_units3(pe, p):
            tensor_gate_up(pe, 3, p, 1)
            tensor_gate_up(pe, 3, p, 2)
            tensor_down(pe, 3, p, 0, 0)
            tensor_gate_up(pe, 3, p, 3)
            tensor_down(pe, 3, p, 0, 1)

        def tensor_layer3(pe):
            tensor_query(pe, 0, 0, 0)
            tensor_score(pe, 0, 0, 0)
            tensor_gate_up(pe, 3, 0, 0)
            tensor_query(pe, 1, 0, 1)
            tensor_score(pe, 1, 0, 1)
            tensor_units3(pe, 0)
            tensor_gate_up(pe, 3, 1, 0)
            tensor_down(pe, 3, 0, 1, 0)
            tensor_down(pe, 3, 0, 1, 1)
            tensor_units3(pe, 1)
            with pe.Fori(0, H3 // 2 - 1) as hp:
                tensor_turn3(pe, hp)
            tensor_turn3(pe, H3 // 2 - 1, final=True)
            tensor_down(pe, 3, CHUNKS[3] // 2 - 1, 1, 0)
            tensor_down(pe, 3, CHUNKS[3] // 2 - 1, 1, 1)

        def scalar_take(act, us):
            for i in range(2):
                act.wait_ge(N3["q_ready"], us * 2 + i + 1)
                act.activation(xi[i][:], bank[2 * i][:], ACT.Copy).then_inc(N3["xi_ready"], 1)

        def scalar_newton(act, g, step, it, units=(0, 1)):
            act.wait_ge(tau_ready[g], step * (NEWTON + 1) + it + 1)
            for i in units:
                for t in range(TPS):
                    last = act.activation(re3[g][:, i, t, :], sc3[g][i][:, t, :], ACT.Relu, bias=tau[g][:, i, t:t + 1],
                                          accum_out=s1[g][:, i, t:t + 1])
                    if (t + 1) % RELU_TILES == 0:
                        last.then_inc(relu_ready[g], 1)

        def scalar_last(act, g, step):
            act.wait_ge(tau_ready[g], step * (NEWTON + 1) + NEWTON + 1)
            for i in range(2):
                for t in range(TPS):
                    last = act.activation(re3[g][:, i, t, :], sc3[g][i][:, t, :], ACT.Relu, bias=tau[g][:, i, t:t + 1])
                last.then_inc(N3["rel_last"], 1)

        def scalar_copy_weights(act, wn):
            for i in range(2):
                act.wait_ge(N3["w_T"], wn * 2 + i + 1)
                act.activation(wT3[i][:, 0, :], bank[2 * i][:], ACT.Copy)
                act.activation(wT3[i][:, 1, :], bank[2 * i + 1][:], ACT.Copy).then_inc(N3["wT_ready"], 1)

        def scalar_turn3(act, hp, final=False):
            for st in range(STEPS3):
                step = hp * STEPS3 + st
                p = step + 2
                more = st < 2 or not final
                us = [usage(hp, f"step{g}{st}" if st < 2 else f"end{g}", final) for g in range(2)]
                scalar_last(act, 0, step)
                scalar_unit(act, 3, p - 1, 3)
                scalar_newton(act, 1, step, 2)
                scalar_copy_weights(act, weights_at(hp, 0, st))
                scalar_newton(act, 1, step, 3, (0,))
                scalar_take(act, us[0])
                scalar_newton(act, 1, step, 3, (1,))
                scalar_newton(act, 1, step, 4)
                if more:
                    if st == 2:
                        scalar_take(act, us[0] + 1)
                    scalar_newton(act, 0, step + 1, 0)
                scalar_last(act, 1, step)
                scalar_unit(act, 3, p, 0)
                if more:
                    scalar_newton(act, 0, step + 1, 1)
                scalar_copy_weights(act, weights_at(hp, 1, st))
                if more:
                    scalar_newton(act, 0, step + 1, 2, (0,))
                scalar_take(act, us[1])
                if more:
                    scalar_newton(act, 0, step + 1, 2, (1,))
                    scalar_newton(act, 0, step + 1, 3)
                    if st == 2:
                        scalar_take(act, us[1] + 1)
                scalar_unit(act, 3, p, 1)
                if more:
                    scalar_newton(act, 1, step + 1, 0)
                    scalar_newton(act, 0, step + 1, 4)
                scalar_unit(act, 3, p, 2)
                if more:
                    scalar_newton(act, 1, step + 1, 1)

        def scalar_layer3(act):
            scalar_take(act, 0)
            scalar_newton(act, 0, 0, 0)
            scalar_unit(act, 3, 0, 0)
            scalar_take(act, 1)
            for it in range(1, 4):
                scalar_newton(act, 0, 0, it)
                scalar_unit(act, 3, 0, it)
            scalar_newton(act, 1, 0, 0)
            scalar_unit(act, 3, 1, 0)
            scalar_newton(act, 0, 0, 4)
            scalar_unit(act, 3, 1, 1)
            scalar_newton(act, 1, 0, 1)
            scalar_unit(act, 3, 1, 2)
            with act.Fori(0, H3 // 2 - 1) as hp:
                scalar_turn3(act, hp)
            scalar_turn3(act, H3 // 2 - 1, final=True)
            scalar_unit(act, 3, CHUNKS[3] // 2 - 1, 3)

        def vector_scores(dve, g, us):
            for i in range(2):
                dve.wait_ge(N3["filled"], us * 2 + i + 1)
                sc = [bank[2 * i + c][:].rearrange("p (t m) -> p t m", m=MEM) for c in range(2)]
                for c in range(2):
                    dve.tensor_reduce(mx3[:, i, 2 * c:2 * c + 2], sc[c], AX.X, ALU.max)
                dve.drain()
                for c in range(2):
                    last = dve.tensor_tensor(sc3[g][i][:, 2 * c:2 * c + 2, :], sc[c],
                                             mx3[:, i, 2 * c:2 * c + 2].unsqueeze(2).to_broadcast([P, 2, MEM]),
                                             ALU.subtract)
                last.then_inc(N3["taken"], 1)
            dve.memset(tau[g][:], 1.0).then_inc(tau_ready[g], 1)

        def vector_newton(dve, g, step, it):
            for i in range(2):
                for t in range(TPS):
                    if t % RELU_TILES == 0:
                        dve.wait_ge(relu_ready[g], ((step * NEWTON + it) * 2 + i) * (TPS // RELU_TILES) + t // RELU_TILES + 1)
                    dve.tensor_tensor_reduce(re3[g][:, i, t, :], re3[g][:, i, t, :], re3[g][:, i, t, :], 1.0, 0.0,
                                             ALU.mult, ALU.add, s2[g][:, i, t:t + 1])
            dve.drain()
            dve.scalar_tensor_tensor(nb[g][:], s2[g][:], 3.0, s1[g][:], ALU.add, ALU.mult)
            dve.tensor_tensor(na[g][:], s2[g][:], s2[g][:], ALU.mult)
            dve.drain()
            dve.reciprocal(nb[g][:], nb[g][:])
            dve.drain()
            dve.scalar_tensor_tensor(na[g][:], na[g][:], -1.0, nb[g][:], ALU.add, ALU.mult)
            dve.drain()
            dve.tensor_tensor(tau[g][:], tau[g][:], na[g][:], ALU.subtract).then_inc(tau_ready[g], 1)

        def vector_output3(dve, us):
            dve.drain()
            for i in range(2):
                dve.wait_ge(N3["filled"], us * 2 + i + 1)
                for c in range(2):
                    t = i * TPS + 2 * c
                    last = dve.tensor_tensor(x[:, t:t + 2, :], x[:, t:t + 2, :],
                                             bank[2 * i + c][:].rearrange("p (t n) -> p t n", n=D), ALU.add)
                last.then_inc(N3["taken"], 1)
            dve.drain()

        def vector_turn3(dve, hp, final=False):
            for st in range(STEPS3):
                step = hp * STEPS3 + st
                p = step + 2
                more = st < 2 or not final
                us = [usage(hp, f"step{g}{st}" if st < 2 else f"end{g}", final) for g in range(2)]
                vector_newton(dve, 1, step, 2)
                vector_unit(dve, 3, p - 1, 3)
                vector_newton(dve, 1, step, 3)
                if st == 2:
                    vector_output3(dve, us[0])
                    vector_newton(dve, 1, step, 4)
                    if more:
                        vector_scores(dve, 0, us[0] + 1)
                    vector_add(dve, 3, p - 1, 1, 0)
                else:
                    vector_add(dve, 3, p - 1, 1, 0)
                    vector_scores(dve, 0, us[0])
                    vector_newton(dve, 1, step, 4)
                if more:
                    vector_newton(dve, 0, step + 1, 0)
                vector_add(dve, 3, p - 1, 1, 1)
                vector_unit(dve, 3, p, 0)
                if more:
                    vector_newton(dve, 0, step + 1, 1)
                if st == 2:
                    vector_output3(dve, us[1])
                    if more:
                        vector_newton(dve, 0, step + 1, 2)
                        vector_newton(dve, 0, step + 1, 3)
                        vector_scores(dve, 1, us[1] + 1)
                else:
                    vector_newton(dve, 0, step + 1, 2)
                    vector_scores(dve, 1, us[1])
                    vector_newton(dve, 0, step + 1, 3)
                vector_unit(dve, 3, p, 1)
                if more:
                    vector_newton(dve, 1, step + 1, 0)
                    vector_newton(dve, 0, step + 1, 4)
                vector_unit(dve, 3, p, 2)
                vector_add(dve, 3, p, 0, 0)
                if more:
                    vector_newton(dve, 1, step + 1, 1)
                vector_add(dve, 3, p, 0, 1)

        def vector_layer3(dve):
            dve.drain().then_inc(N3["taken"], 2)
            vector_scores(dve, 0, 0)
            vector_newton(dve, 0, 0, 0)
            vector_unit(dve, 3, 0, 0)
            vector_scores(dve, 1, 1)
            for it in range(1, 4):
                vector_newton(dve, 0, 0, it)
                vector_unit(dve, 3, 0, it)
                if it > 1:
                    vector_add(dve, 3, 0, 0, it - 2)
            vector_newton(dve, 1, 0, 0)
            vector_unit(dve, 3, 1, 0)
            vector_add(dve, 3, 0, 1, 0)
            vector_newton(dve, 0, 0, 4)
            vector_add(dve, 3, 0, 1, 1)
            vector_unit(dve, 3, 1, 1)
            vector_newton(dve, 1, 0, 1)
            vector_unit(dve, 3, 1, 2)
            vector_add(dve, 3, 1, 0, 0)
            vector_add(dve, 3, 1, 0, 1)
            with dve.Fori(0, H3 // 2 - 1) as hp:
                vector_turn3(dve, hp)
            vector_turn3(dve, H3 // 2 - 1, final=True)
            vector_unit(dve, 3, CHUNKS[3] // 2 - 1, 3)
            vector_add(dve, 3, CHUNKS[3] // 2 - 1, 1, 0)
            vector_add(dve, 3, CHUNKS[3] // 2 - 1, 1, 1)

        def pool_square(pool, g, wn):
            for i in range(2):
                pool.wait_ge(N3["rel_last"], wn * 2 + i + 1)
                pool.tensor_tensor(re3[g][:, i, :, :], re3[g][:, i, :, :], re3[g][:, i, :, :], ALU.mult
                                   ).then_inc(N3["w_ready"], 1)

        def pool_query_weights(pool, pair):
            for g in range(2):
                pool.tensor_copy(wq_s[g][:], wq3[:, :, bass.ds((pair * 2 + g) * HD3, HD3)])
            pool.drain().then_inc(N3["wq_ready"], 1)

        def pool_value_weights(pool, pair, g):
            pool.tensor_copy(v3_s[g][:], V3[:, :, bass.ds((pair * 2 + g) * HD3, HD3)])
            pool.tensor_copy(wo3_s[g][:], wo3[:, bass.ds(pair * 2 + g, 1), :].rearrange("p a d -> p (a d)"))
            pool.drain().then_inc(N3["vo_ready"], 1)

        def pool_turn3(pool, hp, final=False):
            for st in range(STEPS3):
                for g in range(2):
                    pool_square(pool, g, weights_at(hp, g, st))
                    if st == 0 and g == 1 and not final:
                        pool.wait_ge(N3["filled"], usage(hp, "step00") * 2)
                        pool_query_weights(pool, hp + 1)
            if not final:
                for g in range(2):
                    pool.wait_ge(N3["filled"], usage(hp, f"end{g}") * 2 + 2)
                    pool_value_weights(pool, hp + 1, g)

        def pool_layer3(pool):
            pool_query_weights(pool, 0)
            for g in range(2):
                pool_value_weights(pool, 0, g)
            with pool.Fori(0, H3 // 2 - 1) as hp:
                pool_turn3(pool, hp)
            pool_turn3(pool, H3 // 2 - 1, final=True)

        LOADS = [0, 0, 0, 0]
        loads = [
            [(wqkv[0], "wqkv0"), (bqkv, "bqkv"), (head_mask, "head_mask"), (wo[0], "wo0"), (bo, "bo")],
            [(rope, "rope"), (wqkv[1], "wqkv1"), (wo[1], "wo1"), (router[1], "router1"), (lower, "lower"),
             (decay, "decay"), (decay_q, "decay_q"), (decay_k, "decay_k"), (lam_chunk, "lam_chunk"),
             (own_block, "own_block"), (wg1, "wg1"), (wg2, "wg2"), (norm_w, "norm_w")],
            [(causal, "causal"), (wqkv[2], "wqkv2"), (wo[2], "wo2"), (router[2], "router2"), (rbias, "rbias"),
             (dbias, "dbias"), (gu_bias, "gu_bias")],
            [(wq3, "wq3"), (wk3, "wk3"), (wv3, "wv3"), (wo3, "wo3"), (mem, "mem"), (aff, "aff"), (lbeta, "lbeta"),
             (router[3], "router3")],
        ]
        for n in range(4):
            LOADS[n] = 16 * len(loads[n])
        LN_S = 6.238324625039508
        out_stored = sem("out_stored")

        def load_broadcast(name):
            return a[name].shape[0] == 1

        block = ctx.enter_context(nc.Block())

        @block.sync
        def _(sp):
            sp.dma_start(x[:], a["x"]).then_inc(x_loaded, 16)
            sp.dma_start(gates[:], a["gates"].to_broadcast([P] + list(a["gates"].shape[1:]))).then_inc(gates_loaded, 16)
            sp.dma_start(order_pos[:], a["order_pos"]).then_inc(gates_loaded, 16)
            sp.dma_start(ident[:], a["ident"]).then_inc(ident_loaded, 16)
            for n in range(4):
                if n == 3:
                    sp.wait_ge(phase_done, 4 * 13)
                for dst, name in loads[n]:
                    src = a[name]
                    if load_broadcast(name):
                        src = src.to_broadcast([P] + list(src.shape[1:]))
                    sp.dma_start(dst[:], src).then_inc(loaded[n], 16)
                if n == 2:
                    sync_ffn(sp, 0, 0, CHUNKS[0] // 2)
                    sync_ffn(sp, 1, 0, CHUNKS[1] // 2)
            for n in range(2, 4):
                sync_ffn(sp, n, 0, CHUNKS[n] // 2)
            sp.wait_ge(phase_done, 4 * BARRIERS)
            sp.dma_start(out, x[:]).then_inc(out_stored, 16)
            sp.wait_ge(out_stored, 16)

        @block.tensor
        def _(pe):
            pe.wait_ge(ident_loaded, 16)
            for n in range(3):
                tensor_norm(pe, n)
                barrier(pe)
                pe.wait_ge(loaded[n], LOADS[n])
                if n == 2:
                    pe.wait_ge(loaded[1], LOADS[1])
                tensor_project(pe, n)
                barrier(pe)
                if n == 0:
                    barrier(pe)
                if n == 1:
                    tensor_linear(pe)
                else:
                    tensor_heads(pe, n)
                barrier(pe)
                if n != 1:
                    barrier(pe)
                tensor_out(pe, n)
                barrier(pe)
                if n:
                    tensor_route(pe, n)
                    barrier(pe)
                if n == 2:
                    tensor_bias2(pe)
                    barrier(pe)
                tensor_ffn_start(pe, n)
                tensor_ffn(pe, n)
                barrier(pe)
            tensor_norm(pe, 3)
            barrier(pe)
            pe.wait_ge(loaded[3], LOADS[3])
            tensor_norm3(pe)
            barrier(pe)
            tensor_route(pe, 3)
            barrier(pe)
            tensor_ffn_start(pe, 3)
            tensor_layer3(pe)
            barrier(pe)

        @block.scalar
        def _(act):
            scalar_gates(act)
            for n in range(3):
                scalar_norm(act, n)
                barrier(act)
                scalar_project(act, n)
                barrier(act)
                if n == 0:
                    barrier(act)
                if n == 1:
                    scalar_linear(act)
                else:
                    scalar_heads(act, n)
                barrier(act)
                if n == 0:
                    scalar_rows(act)
                if n != 1:
                    barrier(act)
                scalar_out(act, n)
                barrier(act)
                if n:
                    scalar_route(act, n)
                    barrier(act)
                if n == 2:
                    barrier(act)
                scalar_ffn(act, n)
                barrier(act)
            scalar_norm(act, 3)
            barrier(act)
            act.wait_ge(loaded[3], LOADS[3])
            scalar_norm3(act)
            barrier(act)
            scalar_route(act, 3)
            barrier(act)
            scalar_layer3(act)
            barrier(act)

        @block.vector
        def _(dve):
            dve.wait_ge(ident_loaded, 16)
            vector_gates(dve)
            for n in range(3):
                vector_norm(dve, n)
                barrier(dve)
                dve.wait_ge(loaded[n], LOADS[n])
                vector_project(dve, n)
                barrier(dve)
                if n == 0:
                    vector_diffs(dve)
                    barrier(dve)
                if n == 1:
                    vector_linear(dve)
                else:
                    vector_heads(dve, n)
                barrier(dve)
                if n == 0:
                    vector_rows(dve)
                if n == 2:
                    vector_divide(dve)
                if n != 1:
                    barrier(dve)
                vector_out(dve, n)
                barrier(dve)
                if n:
                    vector_route(dve, n)
                    barrier(dve)
                if n == 2:
                    vector_bias2(dve)
                    barrier(dve)
                vector_ffn_start(dve, n)
                vector_ffn(dve, n)
                barrier(dve)
            vector_norm(dve, 3)
            barrier(dve)
            dve.wait_ge(loaded[3], LOADS[3])
            vector_norm3(dve)
            barrier(dve)
            vector_route(dve, 3)
            barrier(dve)
            vector_ffn_start(dve, 3)
            vector_layer3(dve)
            barrier(dve)

        @block.gpsimd
        def _(pool):
            pool.wait_ge(gates_ready, 1)
            for n in range(3):
                pool_norm(pool, n)
                barrier(pool)
                barrier(pool)
                if n == 0:
                    barrier(pool)
                if n == 1:
                    pool_linear(pool)
                else:
                    pool_heads(pool, n)
                barrier(pool)
                if n != 1:
                    barrier(pool)
                barrier(pool)
                if n:
                    barrier(pool)
                if n == 2:
                    barrier(pool)
                barrier(pool)
            pool_norm(pool, 3)
            barrier(pool)
            pool_norm3(pool)
            barrier(pool)
            barrier(pool)
            pool_layer3(pool)
            barrier(pool)




def _constants(np):
    p = np.arange(P)
    c = {"ident": np.eye(P, dtype=np.float32)}
    c["head_mask"] = (p[:, None] // HD == np.arange(GH)[None, :]).astype(np.float32)
    c["causal"] = np.where(p[None, :] > p[:, None], np.float32(MASKED), np.float32(0))
    c["own_block"] = (p[:, None] // HD == p[None, :] // HD).astype(np.float32)
    pos = (np.arange(TPS)[None, :] * P + p[:, None]).astype(np.float32)
    c["order_pos"] = (pos / np.float32(S) * np.float32(0.05)).astype(np.float32)
    half = HD // 2
    th1 = np.float32(10000.0) ** (np.float32(-2.0) * np.arange(half, dtype=np.float32) / np.float32(HD))
    th2 = np.float32(1.0) / np.float32(10000.0) ** (np.arange(0, HD, 2, dtype=np.float32) / np.float32(HD))
    rope = np.zeros((P, 2, TPS, 2, half), np.float32)
    for i, th in enumerate((th1, th2)):
        ang = (pos[:, :, None] * th.astype(np.float32)).astype(np.float32)
        rope[:, i, :, 0, :] = np.cos(ang)
        rope[:, i, :, 1, :] = np.sin(ang)
    c["rope"] = rope
    lam = -(2.0 ** (-8.0 * (np.arange(H) + 1.0) / H))
    d = p[None, None, :] - p[:, None, None]
    c["decay"] = np.where(d >= 0, np.exp(lam[None, :, None] * np.maximum(d, 0)), 0.0).astype(np.float32)
    c["decay_q"] = np.exp(lam[None, :] * (p[:, None] + 1.0)).astype(np.float32)
    c["decay_k"] = np.exp(lam[None, :] * (P - 1.0 - p[:, None])).astype(np.float32)
    lc = np.exp(lam * P).reshape(NG, GH)
    c["lam_chunk"] = np.ascontiguousarray(np.broadcast_to(lc[:, p // HD].T[:, :, None], (P, NG, P))).astype(np.float32)
    e = np.arange(16)
    c["lower"] = np.broadcast_to((e[None, :] < e[:, None]).astype(np.float32)[None], (1, 16, 16)).copy()
    for n, w in ((1, 176), (2, 256), (3, 176)):
        unit = np.arange(CHUNKS[n] * P)
        owner = np.minimum(unit // w, EXPERTS[n])
        sel = np.zeros((CHUNKS[n], CR, P), np.float32)
        for part in range(3):
            sel[unit // P, part * NE + owner, unit % P] = 1
        c[f"sel{n}"] = sel
    return c


def _rows(np, w):
    return np.ascontiguousarray(w.reshape(-1, P, w.shape[1]).transpose(1, 0, 2))


def kernel(**inputs):
    import ml_dtypes
    import numpy as np
    import concourse.bacc as bacc
    from concourse.bass_utils import run_bass_kernel_spmd as run

    i = {k: np.asarray(v) for k, v in inputs.items()}
    a = _constants(np)
    for n in (1, 2, 3):
        a[f"sel{n}"] = a[f"sel{n}"].astype(ml_dtypes.bfloat16)

    def row(*names):
        return np.concatenate([i[k].reshape(-1) for k in names])[None, :]

    a["x"] = np.ascontiguousarray(i["L0_attn_hidden_states"].reshape(NT, P, D).transpose(1, 0, 2))
    a["wqkv0"] = _rows(np, np.concatenate([i[f"L0_attn_W{c}"].T for c in "qkv"], 1))
    a["bqkv"] = row("L0_attn_bq", "L0_attn_bk", "L0_attn_bv")
    a["wo0"], a["bo"] = _rows(np, i["L0_attn_Wo"].T), row("L0_attn_bo")
    a["gates"] = row(*[f"L0_attn_{c}_gate" for c in ("truth", "balance", "order", "justice", "harmony")])
    a["wqkv1"] = _rows(np, np.concatenate([i[f"L1_attn_W{c}"] for c in "qkv"], 1))
    a["wo1"], a["router1"] = _rows(np, i["L1_attn_Wo"]), _rows(np, i["L1_ffn_gate_w"])
    a["wg1"], a["wg2"] = _rows(np, i["L1_attn_Wg1"]), i["L1_attn_Wg2"]
    a["norm_w"] = row("L1_attn_norm_weight")
    wk = np.repeat(i["L2_attn_wk"].reshape(D, 4, HD), 4, axis=1).reshape(D, D)
    a["wqkv2"] = _rows(np, np.concatenate([i["L2_attn_wq"], wk, i["L2_attn_wv"]], 1))
    a["wo2"], a["router2"] = _rows(np, i["L2_attn_wo"]), _rows(np, i["L2_ffn_router_weight"].T)
    a["rbias"], a["dbias"] = row("L2_ffn_router_bias"), i["L2_ffn_down_proj_bias"]
    a["wq3"] = _rows(np, i["L3_attn_Wq"].T)
    a["wk3"], a["wv3"] = i["L3_attn_Wk"].T, i["L3_attn_Wv"].T
    a["wo3"] = _rows(np, i["L3_attn_Wo"].T)
    a["mem"] = _rows(np, i["L3_attn_memory"])
    a["aff"] = np.concatenate([i["L3_attn_g_state"].reshape(2, P).T, i["L3_attn_b_state"].reshape(2, P).T,
                               i["L3_attn_g_mem"][:, None], i["L3_attn_b_mem"][:, None]], 1)
    a["lbeta"] = row("L3_attn_log_beta")
    a["router3"] = _rows(np, np.concatenate([i["L3_ffn_gate_w"], i["L3_ffn_shared_gate_vec"]], 0).T)

    def wide(w):
        return w.transpose(1, 0, 2).reshape(D, -1)

    ffn = [(i["L0_ffn_w_gate"].T, i["L0_ffn_w_up"].T, i["L0_ffn_w_down"].T, None)]
    ffn.append((np.concatenate([wide(i["L1_ffn_w_gate"]), i["L1_ffn_sw_gate"]], 1),
                np.concatenate([wide(i["L1_ffn_w_up"]), i["L1_ffn_sw_up"]], 1),
                np.concatenate([i["L1_ffn_w_down"].reshape(-1, D), i["L1_ffn_sw_down"]], 0), None))
    gu, bias = i["L2_ffn_gate_up_proj"], i["L2_ffn_gate_up_proj_bias"]
    ffn.append((wide(gu[:, :, 0::2]), wide(gu[:, :, 1::2]), i["L2_ffn_down_proj"].reshape(-1, D),
                (bias[:, 0::2].reshape(-1), bias[:, 1::2].reshape(-1))))
    eg, sg = i["L3_ffn_expert_gate_up"].transpose(0, 2, 1), i["L3_ffn_shared_gate_up"]
    ffn.append((np.concatenate([wide(eg[:, :, :176]), sg[:704].T], 1),
                np.concatenate([wide(eg[:, :, 176:]), sg[704:].T], 1),
                np.concatenate([i["L3_ffn_expert_down"].transpose(0, 2, 1).reshape(-1, D), i["L3_ffn_shared_down"].T], 0),
                None))
    a["gu"] = np.zeros((sum(CHUNKS), P, GUW), np.float32)
    a["down"] = np.zeros((sum(CHUNKS), P, D), np.float32)
    first = 0
    for n, (g, u, d, b) in enumerate(ffn):
        hidden, width = g.shape[1], CHUNKS[n] * P
        for at, w in ((0, g), (2 * P, u)):
            full = np.zeros((D, width), np.float32)
            full[:, :hidden] = w
            parts = full.reshape(KD, P, CHUNKS[n], P).transpose(2, 1, 0, 3).reshape(CHUNKS[n], P, D)
            a["gu"][first:first + CHUNKS[n], :, at:at + D] = parts
        if b is not None:
            a["gu_bias"] = np.stack([c.reshape(CHUNKS[n], P).T for c in b], 2)
        full = np.zeros((width, D), np.float32)
        full[:hidden] = d
        a["down"][first:first + CHUNKS[n]] = full.reshape(CHUNKS[n], P, D)
        first += CHUNKS[n]

    nc = bacc.Bacc("TRN2", target_bir_lowering=False, num_devices=1)
    arrays = {k: np.ascontiguousarray(v) for k, v in a.items()}
    aps = {k: nc.dram_tensor(f"in_{k}", v.shape, mybir.dt.from_np(v.dtype), kind="ExternalInput").ap()
           for k, v in arrays.items()}
    out = nc.dram_tensor("out", (P, NT, D), F32, kind="ExternalOutput").ap()
    build(nc, aps, out)
    r = run(nc, [{f"in_{k}": v for k, v in arrays.items()}], core_ids=[0])
    return r.results[0]["out"].transpose(1, 0, 2).reshape(B, S, D)
```
